# Optimizing a Trainium2 kernel written in Bass

```python
import numpy as np
import jax
import jax.numpy as jnp

def _softmax(x, axis=-1):
    return jax.nn.softmax(x, axis=axis)
def _gelu(x):
    return jax.nn.gelu(x, approximate=True)
def _silu(x):
    return jax.nn.silu(x)
def _sigmoid(x):
    return jax.nn.sigmoid(x)
def _layernorm(x, axis=-1, eps=1e-5):
    m = jnp.mean(x, axis=axis, keepdims=True)
    v = jnp.var(x, axis=axis, keepdims=True)
    return (x - m) / jnp.sqrt(v + eps)
def _scatter_add(tgt, idx, src, axis=0):
    return tgt.at[idx].add(src)
def _segment_sum(src, seg, n):
    return jax.ops.segment_sum(src, seg, n)

kernel_name = 'mk_metaformer_d2_conv_nchw128_67af74'

def setup_inputs(seed: int = 0):
    np.random.seed(seed)
    _w = jnp.asarray
    def _rec_inputs():
        import jax
        import jax.numpy as jnp
        _gk = jax.random.key(seed)
        x = 7.22e-05 + 1 * jax.random.normal(jax.random.fold_in(_gk, 1), (4, 128, 128, 128), jnp.float32)
        return x
    x = _rec_inputs()
    def _L0_conv_setup():
        import jax, jax.numpy as jnp
        import numpy as np
        from jax import lax
        K = 3
        PAD = 1

        def _offset_conv(x, w_off):
            return lax.conv_general_dilated(x, w_off, window_strides=(1, 1), padding=((PAD, PAD), (PAD, PAD)), dimension_numbers=('NCHW', 'OIHW', 'NCHW'))

        def _bilinear_gather(x, py, px):
            B, C, H, W = x.shape
            y0 = jnp.floor(py)
            x0 = jnp.floor(px)
            y1 = y0 + 1.0
            x1 = x0 + 1.0
            wy1 = py - y0
            wy0 = 1.0 - wy1
            wx1 = px - x0
            wx0 = 1.0 - wx1

            def corner(iy, ix, w):
                valid = (iy >= 0) & (iy <= H - 1) & (ix >= 0) & (ix <= W - 1)
                iyc = jnp.clip(iy, 0, H - 1).astype(jnp.int32)
                ixc = jnp.clip(ix, 0, W - 1).astype(jnp.int32)
                g = jax.vmap(lambda img, yy, xx: img[:, yy, xx])(x, iyc, ixc)
                return g * (w * valid.astype(x.dtype))[:, None]
            return corner(y0, x0, wy0 * wx0) + corner(y0, x1, wy0 * wx1) + corner(y1, x0, wy1 * wx0) + corner(y1, x1, wy1 * wx1)

        def _deform_forward(x, w_off, w_conv):
            B, C, H, W = x.shape
            offset = _offset_conv(x, w_off)
            Ho, Wo = (offset.shape[2], offset.shape[3])
            off = offset.reshape(B, K * K, 2, Ho, Wo)
            dy, dx = (off[:, :, 0], off[:, :, 1])
            ky, kx = jnp.meshgrid(jnp.arange(K), jnp.arange(K), indexing='ij')
            base_y = (jnp.arange(Ho) - PAD)[None, :, None] + ky.reshape(-1)[:, None, None]
            base_x = (jnp.arange(Wo) - PAD)[None, None, :] + kx.reshape(-1)[:, None, None]
            py = base_y.astype(x.dtype)[None] + dy
            px = base_x.astype(x.dtype)[None] + dx
            sampled = _bilinear_gather(x, py, px)
            O = w_conv.shape[0]
            return jnp.einsum('bckhw,ock->bohw', sampled, w_conv.reshape(O, C, K * K))
        key = jax.random.key(seed)
        k1, k2, k3 = jax.random.split(key, 3)
        B, C, H, W, O = (4, 128, 128, 128, 128)
        x = jax.random.normal(k1, (B, C, H, W), dtype=jnp.float32)
        w_off = jax.random.normal(k2, (2 * K * K, C, K, K), dtype=jnp.float32) * 0.01
        w_conv = jax.random.normal(k3, (O, C, K, K), dtype=jnp.float32) * 0.05
        return {'x': x, 'w_off': w_off, 'w_conv': w_conv}
    _L0_conv_all = _L0_conv_setup()
    _L0_conv_in = {k: v for k, v in _L0_conv_all.items() if k in ('w_off', 'w_conv', )}
    del _L0_conv_all

    def _L0_ffn_setup():
        import jax, jax.numpy as jnp
        import numpy as np
        B, N, D, C, E, K = (8, 8192, 128, 128, 8, 2)
        key = jax.random.key(seed)
        k0, k1, k2 = jax.random.split(key, 3)
        x = jax.random.normal(k0, (B, N, D), dtype=jnp.float32)
        router_w = jax.random.normal(k1, (D, E), dtype=jnp.float32) * 0.05
        router_b = jnp.zeros((E,), dtype=jnp.float32)
        expert_w = jax.random.normal(k2, (E, D, C), dtype=jnp.float32) * (1.0 / np.sqrt(D))
        expert_b = jnp.zeros((E, C), dtype=jnp.float32)
        return {'x': x, 'router_w': router_w, 'router_b': router_b, 'expert_w': expert_w, 'expert_b': expert_b}
    _L0_ffn_all = _L0_ffn_setup()
    _L0_ffn_in = {k: v for k, v in _L0_ffn_all.items() if k in ('router_w', 'router_b', 'expert_w', 'expert_b', )}
    del _L0_ffn_all

    def _L1_conv_setup():
        import jax, jax.numpy as jnp
        import numpy as np
        B, CIN, COUT, H, W = (8, 128, 128, 128, 128)
        key = jax.random.key(seed)
        kx, ka, kb = jax.random.split(key, 3)
        x = jax.random.normal(kx, (B, CIN, H, W), dtype=jnp.float32)
        alphas = jax.random.normal(ka, (COUT, CIN), dtype=jnp.float32)
        betas = jax.random.normal(kb, (COUT, CIN), dtype=jnp.float32)
        return {'x': x, 'alphas': alphas, 'betas': betas}
    _L1_conv_all = _L1_conv_setup()
    _L1_conv_in = {k: v for k, v in _L1_conv_all.items() if k in ('alphas', 'betas', )}
    del _L1_conv_all

    def _L1_ffn_setup():
        import jax, jax.numpy as jnp
        import numpy as np
        B, S, D, E, H, O, K = (512, 2048, 128, 64, 512, 128, 8)
        key = jax.random.key(seed)
        k0, k1, k2, k3 = jax.random.split(key, 4)
        x = jax.random.normal(k0, (B, S, D), dtype=jnp.float32)
        gate_w = jax.random.normal(k1, (E, D), dtype=jnp.float32) * (1.0 / np.sqrt(D))
        gate_b = jnp.zeros((E,), dtype=jnp.float32)
        weight1 = jax.random.uniform(k2, (E, D + 1, H), dtype=jnp.float32, minval=-1.0, maxval=1.0) * (1.0 / np.sqrt(D + 1))
        weight2 = jax.random.uniform(k3, (E, H + 1, O), dtype=jnp.float32, minval=-1.0, maxval=1.0) * (1.0 / np.sqrt(H + 1))
        return {'x': x, 'gate_w': gate_w, 'gate_b': gate_b, 'weight1': weight1, 'weight2': weight2}
    _L1_ffn_all = _L1_ffn_setup()
    _L1_ffn_in = {k: v for k, v in _L1_ffn_all.items() if k in ('gate_w', 'gate_b', 'weight1', 'weight2', )}
    del _L1_ffn_all

    return {
        "x": x,
        "L0_conv_w_off": _L0_conv_in["w_off"],
        "L0_conv_w_conv": _L0_conv_in["w_conv"],
        "L0_ffn_router_w": _L0_ffn_in["router_w"],
        "L0_ffn_router_b": _L0_ffn_in["router_b"],
        "L0_ffn_expert_w": _L0_ffn_in["expert_w"],
        "L0_ffn_expert_b": _L0_ffn_in["expert_b"],
        "L1_conv_alphas": _L1_conv_in["alphas"],
        "L1_conv_betas": _L1_conv_in["betas"],
        "L1_ffn_gate_w": _L1_ffn_in["gate_w"],
        "L1_ffn_gate_b": _L1_ffn_in["gate_b"],
        "L1_ffn_weight1": _L1_ffn_in["weight1"],
        "L1_ffn_weight2": _L1_ffn_in["weight2"],
    }

def reference(x, L0_conv_w_off, L0_conv_w_conv, L0_ffn_router_w, L0_ffn_router_b, L0_ffn_expert_w, L0_ffn_expert_b, L1_conv_alphas, L1_conv_betas, L1_ffn_gate_w, L1_ffn_gate_b, L1_ffn_weight1, L1_ffn_weight2):
    import jax
    import jax.numpy as jnp
    def _L0_conv_ref(x, w_off, w_conv):
        import jax, jax.numpy as jnp
        import numpy as np
        from jax import lax
        K = 3
        PAD = 1

        def _offset_conv(x, w_off):
            return lax.conv_general_dilated(x, w_off, window_strides=(1, 1), padding=((PAD, PAD), (PAD, PAD)), dimension_numbers=('NCHW', 'OIHW', 'NCHW'))

        def _bilinear_gather(x, py, px):
            B, C, H, W = x.shape
            y0 = jnp.floor(py)
            x0 = jnp.floor(px)
            y1 = y0 + 1.0
            x1 = x0 + 1.0
            wy1 = py - y0
            wy0 = 1.0 - wy1
            wx1 = px - x0
            wx0 = 1.0 - wx1

            def corner(iy, ix, w):
                valid = (iy >= 0) & (iy <= H - 1) & (ix >= 0) & (ix <= W - 1)
                iyc = jnp.clip(iy, 0, H - 1).astype(jnp.int32)
                ixc = jnp.clip(ix, 0, W - 1).astype(jnp.int32)
                g = jax.vmap(lambda img, yy, xx: img[:, yy, xx])(x, iyc, ixc)
                return g * (w * valid.astype(x.dtype))[:, None]
            return corner(y0, x0, wy0 * wx0) + corner(y0, x1, wy0 * wx1) + corner(y1, x0, wy1 * wx0) + corner(y1, x1, wy1 * wx1)

        def _deform_forward(x, w_off, w_conv):
            B, C, H, W = x.shape
            offset = _offset_conv(x, w_off)
            Ho, Wo = (offset.shape[2], offset.shape[3])
            off = offset.reshape(B, K * K, 2, Ho, Wo)
            dy, dx = (off[:, :, 0], off[:, :, 1])
            ky, kx = jnp.meshgrid(jnp.arange(K), jnp.arange(K), indexing='ij')
            base_y = (jnp.arange(Ho) - PAD)[None, :, None] + ky.reshape(-1)[:, None, None]
            base_x = (jnp.arange(Wo) - PAD)[None, None, :] + kx.reshape(-1)[:, None, None]
            py = base_y.astype(x.dtype)[None] + dy
            px = base_x.astype(x.dtype)[None] + dx
            sampled = _bilinear_gather(x, py, px)
            O = w_conv.shape[0]
            return jnp.einsum('bckhw,ock->bohw', sampled, w_conv.reshape(O, C, K * K))
        return _deform_forward(x, w_off, w_conv)

    def _L0_ffn_ref(x, router_w, router_b, expert_w, expert_b):
        import jax, jax.numpy as jnp
        import numpy as np
        B, N, D, C, E, K = (8, 8192, 128, 128, 8, 2)
        router_probs = jax.nn.softmax(x @ router_w + router_b, axis=-1)
        top_p, top_i = jax.lax.top_k(router_probs, K)
        top_p = top_p / jnp.sum(top_p, axis=-1, keepdims=True)
        expert_out = jnp.einsum('bnd,edc->bnec', x, expert_w) + expert_b
        gathered = jnp.take_along_axis(expert_out, top_i[..., None], axis=2)
        return jnp.einsum('bnk,bnkc->bnc', top_p, gathered)

    def _L1_conv_ref(x, alphas, betas):
        import jax, jax.numpy as jnp
        import numpy as np
        B, CIN, COUT, H, W = (8, 128, 128, 128, 128)
        x_fft = jnp.fft.fft2(x, axes=(-2, -1))
        re, im = (x_fft.real, x_fft.imag)
        new_real = jnp.einsum('oi,bihw->bohw', alphas, re) + jnp.einsum('oi,bihw->bohw', betas, im)
        new_imag = jnp.einsum('oi,bihw->bohw', betas, re) - jnp.einsum('oi,bihw->bohw', alphas, im)
        y = jnp.fft.ifft2(new_real + 1j * new_imag, axes=(-2, -1))
        return jnp.real(y).astype(jnp.float32)

    def _L1_ffn_ref(x, gate_w, gate_b, weight1, weight2):
        import jax, jax.numpy as jnp
        import numpy as np
        B, S, D, E, H, O, K = (512, 2048, 128, 64, 512, 128, 8)
        Bn, Sn, Dn = x.shape
        logits = jnp.einsum('bsd,ed->bse', x, gate_w) + gate_b
        probs = jax.nn.softmax(logits, axis=1)
        vals, idx = jax.lax.top_k(probs.transpose(0, 2, 1), K)
        topv = vals.transpose(0, 2, 1)
        topi = idx.transpose(0, 2, 1)
        flat_idx = topi.reshape(Bn, K * E)
        gathered = jnp.take_along_axis(x, flat_idx[:, :, None], axis=1)
        gathered = gathered.reshape(Bn, K, E, Dn)
        pooled = jnp.einsum('bked,bke->bed', gathered, topv)
        ones = jnp.ones((E, Bn, 1), dtype=x.dtype)
        h = jnp.concatenate([pooled.transpose(1, 0, 2), ones], axis=-1)
        h = jax.nn.gelu(jnp.einsum('ebd,edh->ebh', h, weight1), approximate=False)
        h = jnp.concatenate([h, ones], axis=-1)
        out = jnp.einsum('ebh,eho->ebo', h, weight2)
        out = out.transpose(1, 0, 2)
        weighted = jnp.einsum('beo,bke->bkeo', out, topv).reshape(Bn, K * E, O)
        outputs = jnp.zeros((Bn, Sn, O), dtype=x.dtype)
        outputs = outputs.at[jnp.arange(Bn)[:, None], flat_idx].add(weighted)
        return outputs

    def _gn(v, G=32, eps=1e-5):
        B_, C_, H_, W_ = v.shape
        g = v.reshape(B_, G, C_ // G, H_, W_)
        m = jnp.mean(g, axis=(2, 3, 4), keepdims=True)
        s = jnp.var(g, axis=(2, 3, 4), keepdims=True)
        return ((g - m) / jnp.sqrt(s + eps)).reshape(v.shape)

    def _ln_c(v, eps=1e-6):
        m = jnp.mean(v, axis=1, keepdims=True)
        s = jnp.var(v, axis=1, keepdims=True)
        return (v - m) / jnp.sqrt(s + eps)

    def _ln_t(v, eps=1e-5):
        m = jnp.mean(v, axis=-1, keepdims=True)
        s = jnp.var(v, axis=-1, keepdims=True)
        return (v - m) / jnp.sqrt(s + eps)

    def _to_tokens(v):
        B_, C_, H_, W_ = v.shape
        return v.reshape(B_, C_, H_ * W_).transpose(0, 2, 1)
    def _from_tokens(t, like):
        B_, C_, H_, W_ = like.shape
        return t.transpose(0, 2, 1).reshape(B_, C_, H_, W_)

    x = x + _L0_conv_ref(_ln_c(x), L0_conv_w_off, L0_conv_w_conv)
    t = _to_tokens(x)
    t = t + _L0_ffn_ref(_ln_t(t), L0_ffn_router_w, L0_ffn_router_b, L0_ffn_expert_w, L0_ffn_expert_b)
    x = _from_tokens(t, x)
    x = x + _L1_conv_ref(_ln_c(x), L1_conv_alphas, L1_conv_betas)
    t = _to_tokens(x)
    t = t + _L1_ffn_ref(_ln_t(t), L1_ffn_gate_w, L1_ffn_gate_b, L1_ffn_weight1, L1_ffn_weight2)
    x = _from_tokens(t, x)
    return x


_drawn_inputs = setup_inputs


def setup_inputs(seed=0):
    import zlib

    import numpy as np

    out = dict(_drawn_inputs(seed))
    spreads = {'L0_ffn_router_b': (0.0, 0.1), 'L0_ffn_expert_b': (0.0, 0.1), 'L1_ffn_gate_b': (0.0, 0.1)}
    factors = {'L1_conv_betas': 8.0, 'L1_ffn_gate_w': 8.0, 'L1_ffn_weight1': 8.0, 'L1_ffn_weight2': 8.0}
    for name, (base, spread) in spreads.items():
        noise = np.random.default_rng([zlib.crc32(name.encode()), seed]).standard_normal(out[name].shape)
        drawn = base * np.exp(spread * noise) if base else spread * noise
        out[name] = jnp.asarray(drawn.astype(out[name].dtype))
    for name, factor in factors.items():
        out[name] = (out[name] * factor).astype(out[name].dtype)
    return out
```

```python
from contextlib import ExitStack

import numpy as np
import concourse.bass as bass
from concourse import mybir

F32 = mybir.dt.float32
BF16 = mybir.dt.bfloat16
I32 = mybir.dt.int32
U32 = mybir.dt.uint32
ALU = mybir.AluOpType
ACT = mybir.ActivationFunctionType
AX = mybir.AxisListType

B, C, H, W = 4, 128, 128, 128
NG = B * H // 4
GI = H // 4
PR, PC = 134, 136
PIX = PR * PC
NPART = 120
E0, E1, HID = 8, 64, 512


class Engine:

    def __init__(self, name, sem):
        self.name, self.sem, self.n, self.todo, self.seen = name, sem, 0, [], {}

    def wait(self, *tokens):
        for t in tokens:
            if t is None:
                continue
            s, v = t
            if self.seen.get(s.num, 0) < v:
                self.seen[s.num] = v
                self.todo.append(lambda e, s=s, v=v: e.wait_ge(s, v))

    def op(self, f, *waits, sig=True):
        self.wait(*waits)
        if not sig:
            self.todo.append(f)
            return None
        self.n += 1
        self.todo.append(lambda e, s=self.sem: f(e).then_inc(s, 1))
        return (self.sem, self.n)

    def run(self, e):
        for f in self.todo:
            f(e)
        self.todo = []


class Queue:

    def __init__(self, engine, sems):
        self.engine, self.sems, self.k = engine, sems, 0

    def dma(self, f, *waits):
        i, r = self.k % len(self.sems), self.k // len(self.sems)
        s = self.sems[i]
        self.engine.wait(*waits)
        if r:
            self.engine.wait((s, 16 * r))
        self.engine.todo.append(lambda e: f(e).then_inc(s, 16))
        self.k += 1
        return (s, 16 * (r + 1))

    def all(self):
        n = len(self.sems)
        return [(self.sems[i], 16 * ((self.k - i + n - 1) // n)) for i in range(min(n, self.k))]


class Phase:
    def __init__(self, nc, ctx, tag, queues):
        sem = lambda n: ctx.enter_context(nc.semaphore(f"{tag}_{n}"))
        self.pe, self.act, self.dve, self.pool, self.sp = (
            Engine(n, sem(n)) for n in ("pe", "act", "dve", "pool", "sp"))
        self.q = {}
        for name, (eng, n) in queues.items():
            self.q[name] = Queue({"sp": self.sp, "act": self.act, "pool": self.pool}[eng],
                                 [sem(f"{name}{i}") for i in range(n)])

    def emit(self, nc):
        for q in self.q.values():
            self.sp.wait(*q.all())
        with nc.Block() as block:
            @block.tensor
            def _(e):
                self.pe.run(e)

            @block.scalar
            def _(e):
                self.act.run(e)

            @block.vector
            def _(e):
                self.dve.run(e)

            @block.gpsimd
            def _(e):
                self.pool.run(e)

            @block.sync
            def _(e):
                self.sp.run(e)


def layernorm_tokens(p, src, stats, mv, rstd, out, eps, src_tok, free_tok, mhalf, after, wait_mv=None):
    t = []
    for i in range(4):
        t.append(p.dve.op(lambda e, i=i: e.bn_stats(stats[:, i, :], src[:, i, :]), src_tok, wait_mv))
    a = None
    for i in range(4):
        a = p.dve.op(lambda e, i=i: e.bn_aggr(mv[:, i, :], stats[:, i, :]), t[i])
    b = p.pool.op(lambda e: e.tensor_scalar(rstd[:, 0:4], mv[:, :, 1], float(eps), None, ALU.add), a)
    c = p.pool.op(lambda e: e.tensor_tensor(rstd[:, 4:8], rstd[:, 0:4], mhalf[:, 0:4], ALU.pow), b)
    d = None
    for i in range(4):
        d = p.dve.op(lambda e, i=i: e.tensor_scalar(out[:, i, :], src[:, i, :], mv[:, i, 0:1],
                                                    rstd[:, 4 + i:5 + i], ALU.subtract, ALU.mult),
                     c, *after)
    return d


def setup_phase(nc, ctx, p, ins, k, xtp):
    q = p.q["c"]
    z = p.dve.op(lambda e: e.memset(k["zero"][:, :], 0.0))
    p.dve.op(lambda e: e.memset(k["mhalf"][:, :], -0.5))
    m = p.dve.op(lambda e: e.memset(k["ones"][:, :], 1.0))
    q.dma(lambda e: e.dma_start(k["ident"][:, :], ins["ident"][:, :]))
    q.dma(lambda e: e.dma_start(k["wof"][:, :, :], ins["wof"][:, :, :]))
    q.dma(lambda e: e.dma_start(k["wcv"][:, :, :], ins["wcv"][:, :, :]))
    s = q.dma(lambda e: e.dma_start(k["self"][:, :, :], ins["sel"][:, :, :]))
    c = q.dma(lambda e: e.dma_start(k["cst"][96:98, :], ins["cst"][:, :]))
    a = p.dve.op(lambda e: e.tensor_copy(k["sel"][:, :, :], k["self"][:, :, :]), s)
    for i in range(NPR):
        p.dve.op(lambda e, i=i: e.tensor_copy(k["P"][96:98, i * 512:(i + 1) * 512], k["cst"][96:98, :]), c)
    for b in range(B):
        v = xtp[b * PIX:(b + 1) * PIX, :]
        for r0 in (0, 131):
            f = v[r0 * PC:(r0 + 3) * PC, :].rearrange("(p r) c -> p (r c)", p=102)
            q.dma(lambda e, f=f: e.dma_start(f, k["zero"][0:102, 0:512]), z)
        g = v[3 * PC:131 * PC, :].rearrange("(r w) c -> r (w c)", w=PC)
        q.dma(lambda e, g=g: e.dma_start(g[:, 0:384], k["zero"][:, 0:384]), z)
        q.dma(lambda e, g=g: e.dma_start(g[:, 131 * 128:136 * 128], k["zero"][:, 0:640]), z)


NPR = 4
NX = 8
NXN = 24
NSR = 12
NPT = 4
REACH = 2.0


def pieces(r0, n, ring):
    out = []
    while n:
        s = r0 % ring
        m = min(n, ring - s)
        out.append((r0, s, m))
        r0, n = r0 + m, n - m
    return out


def phase_a(nc, ctx, p, ins, k, xtp, offd, x1d):
    S = lambda shape, dt=F32, name=None: ctx.enter_context(nc.sbuf_tensor(name, shape, dt))
    xin = S([128, NX, 512], name="a_xin")
    tok = S([128, 2, 4, 128], name="a_tok")
    tn = S([128, 3, 4, 128], name="a_tn")
    st = S([128, 2, 4, 6], name="a_st")
    mv = S([128, 2, 4, 2], name="a_mv")
    rs = S([128, 2, 8], name="a_rs")
    xn = S([128, NXN, 130], name="a_xn")
    off = S([96, 2, 512], name="a_off")
    r1 = S([96, 2, 512], name="a_r1")
    r2 = S([96, 2, 512], name="a_r2")
    t1 = S([96, 2, 512], BF16, name="a_t1")
    win = S([NPART, NPT, 8, 128], name="a_win")
    ab = S([NPART, 3, 2, 384], name="a_ab")
    sw = S([NPART, 2, 9, 128], name="a_sw")
    sr = S([128, NSR, 9, 128], name="a_sr")
    xo = S([128, 2, 512], name="a_xo")
    PB = [ctx.enter_context(nc.psum_tensor(f"a_p{i}", [128, 512], F32)) for i in range(2)]
    PW = ctx.enter_context(nc.psum_tensor("a_pw", [128, 2, 512], F32))
    PB += [None, None] + [ctx.enter_context(nc.psum_tensor(f"a_p{i}", [128, 512], F32)) for i in range(4, 8)]
    Pt = k["P"]
    pe, act, dve, pool = p.pe, p.act, p.dve, p.pool
    ident = k["ident"]

    za = dve.op(lambda e: e.memset(xn[:, :, 0:1], 0.0))
    zb = dve.op(lambda e: e.memset(xn[:, :, 129:130], 0.0))
    k["xn_zero"] = zb
    tl, tt, tst, tcv = {}, {}, {}, {}
    bank = {"k": 0, "free": [None, None]}
    tns = {}
    toks = {}
    xnw = {}
    xnr = {}
    offw, pw, pr = {}, {}, {}
    offst = {}
    cz = {}

    def take():
        i = bank["k"] % 2
        bank["k"] += 1
        return i, PB[i], bank["free"][i]

    def ln(G):
        b, q = divmod(G, GI)
        i, T, fr = take()
        v = T[:, :].rearrange("p (r c) -> p r c", r=4)
        for r in range(4):
            t = pe.op(lambda e, r=r: e.transpose(v[:, r, :], xin[:, G % NX, r * 128:(r + 1) * 128],
                                                 ident[:, :]), tl[G], fr, sig=(r == 3))
        u = act.op(lambda e: e.copy(tok[:, G % 2, :, :], v), t, toks.get(G - 2))
        bank["free"][i] = u
        toks[G] = layernorm_tokens(p, tok[:, G % 2], st[:, G % 2], mv[:, G % 2], rs[:, G % 2],
                                   tn[:, G % 3], 1e-6, u, None, k["mhalf"],
                                   (tns.get(G - 3), tt.get(G - 3)), toks.get(G - 2))
        dst = xtp[b * PIX + (4 * q + 3) * PC:b * PIX + (4 * q + 7) * PC, :].rearrange(
            "(r w) c -> w r c", w=PC)[3:131]
        tns[G] = p.q["st"].dma(lambda e: e.dma_start(dst, tn[:, G % 3, :, :]), toks[G])
        tst[G] = tns[G]

    def back(G):
        b, q = divmod(G, GI)
        i, T, fr = take()
        for r in range(4):
            t = pe.op(lambda e, r=r: e.transpose(T[:, r * 128:(r + 1) * 128], tn[:, G % 3, r, :],
                                                 ident[:, :]), toks[G], fr, sig=(r == 3))
        tt[G] = t
        s = (4 * G) % NXN
        u = act.op(lambda e: e.copy(xn[:, s:s + 4, 1:129], T[:, :].rearrange("p (r c) -> p r c", r=4)),
                   t, tcv.get(G - NXN // 4 + 1), zb)
        bank["free"][i] = u
        xnw[G] = u

    def offsets(G):
        b, q = divmod(G, GI)
        i, T, fr = take()
        need = [xnw[g] for g in (G - 1, G, G + 1) if g in xnw]
        first = True
        todo = []
        for ky in (1, 0, 2):
            lo, hi = 4 * q + ky - 1, 4 * q + ky + 3
            lo, hi = max(lo, 0), min(hi, H)
            for r0, s, m in pieces(H * b + lo, hi - lo, NXN):
                o0 = (r0 - H * b) - (4 * q + ky - 1)
                for kx in range(3):
                    todo.append((ky, kx, s, m, o0))
        for n, (ky, kx, s, m, o0) in enumerate(todo):
            t = pe.op(lambda e, ky=ky, kx=kx, s=s, m=m, o0=o0, n=n: e.matmul(
                T[0:96, o0 * 128:(o0 + m) * 128].rearrange("p (r c) -> p r c", r=m),
                k["wof"][:, 3 * ky + kx, :], xn[:, s:s + m, kx:kx + 128],
                start=(n == 0), stop=(n == len(todo) - 1)), fr, *need, sig=(n == len(todo) - 1))
        tcv[G] = t
        w = G % 2
        pp = Pt[0:96, (G % NPR) * 512:(G % NPR + 1) * 512]
        o = act.op(lambda e: e.copy(off[:, w, :], T[0:96, :]), t, offst.get(G - 2), cz.get(G - 2))
        bank["free"][i] = o
        rows = b * H * W + 4 * q * W
        offst[G] = p.q["st"].dma(lambda e: e.dma_start(offd[:, rows:rows + 512], off[0:18, w, :]), o)
        dve.op(lambda e: e.tensor_reduce(k["fm"][:, G:G + 1], off[:, w, :], AX.X, ALU.max), o)
        dve.op(lambda e: e.tensor_reduce(k["fm"][:, NG + G:NG + G + 1], off[:, w, :], AX.X, ALU.min))
        h = dve.op(lambda e: e.tensor_copy(pp, off[:, w, :]), o, pr.get(G - NPR))
        a = pool.op(lambda e: e.tensor_tensor(r1[:, w, :], off[:, w, :], pp, ALU.subtract), h, cz.get(G - 2), pw.get(G - 2))
        m1 = pool.op(lambda e: e.tensor_copy(t1[:, w, :], r1[:, w, :]), a)
        m2 = dve.op(lambda e: e.tensor_copy(Pt[32:64, (G % NPR) * 512:(G % NPR + 1) * 512],
                                            r1[32:64, w, :]), a)
        c = pool.op(lambda e: e.tensor_tensor(r2[:, w, :], r1[:, w, :], t1[:, w, :], ALU.subtract), m1)
        cz[G] = c
        pw[G] = dve.op(lambda e: e.tensor_copy(Pt[64:96, (G % NPR) * 512:(G % NPR + 1) * 512],
                                               r2[64:96, w, :]), c)

    winw, winr = {}, {}
    nwin = [0]
    ay_free, ax_free = [None], [None]
    nch = [0]
    chunk_s = {}
    srw, srr = {}, {}
    swr = {}
    smp_free = [None, None, None]
    TB = {0: (0, 3), 1: (3, 6), 2: (6, 8)}

    def kys(c):
        return [ky for ky in range(3) if 0 <= c + 1 - ky < H]

    def load_window(b, c):
        n = nwin[0]
        nwin[0] += 1
        dep = [tst[g] for g in range(b * GI + max(0, (c - 2) // 4), b * GI + min(GI - 1, (c + 2) // 4) + 1)]
        last = []
        for j in range(5):
            r = c + j - 2 + 3
            a = b * PIX + r * PC
            src = bass.AP(xtp.tensor, a * 128, [[128, 24], [16 * 128, 8], [1, 128]])
            last.append(p.q["w"].dma(lambda e, j=j, src=src: e.dma_start(
                win[24 * j:24 * j + 24, n % NPT, :, :], src), *dep, winr.get(n - NPT)))
        winw[(b, c)] = (n, last)

    ax_bufs = {}

    def weights(b, c):
        n, _ = winw[(b, c)]
        out = []
        for ky in kys(c):
            y = c + 1 - ky
            G = b * GI + y // 4
            col = (G % NPR) * 512 + (y % 4) * 128
            m = nch[0]
            nch[0] += 1
            for half in range(2):
                for kx in range(3):
                    tx = pe.op(lambda e, kx=kx, ky=ky, half=half, col=col: e.matmul(
                        PW[0:NPART, half, kx * 128:(kx + 1) * 128], k["sel"][0:98, 9 * half + 3 * ky + kx, :],
                        Pt[0:98, col:col + 128], start=True, stop=True), pw[G], ay_free[0],
                        sig=(half == 1 and kx == 2))
            pr[G] = tx
            i = m % 3
            a = act.op(lambda e, i=i: e.activation(ab[:, i, :, :], PW[0:NPART, :, 0:384], ACT.Abs), tx,
                       chunk_s.get(m - 3))
            ay_free[0] = a
            v = dve.op(lambda e, i=i: e.tensor_scalar(ab[:, i, :, :], ab[:, i, :, :], 1.0, 1.0,
                                                      ALU.min, ALU.subtract), a)
            s = dve.op(lambda e, i=i, ky=ky: e.tensor_tensor(
                sw[:, n % 2, 3 * ky:3 * ky + 3, :].rearrange("p a b -> p (a b)"), ab[:, i, 0, :],
                ab[:, i, 1, :], ALU.mult), v, swr.get(n - 2))
            chunk_s[m] = s
            out.append(s)
        return out

    def sample(b, c, stok):
        n, wt = winw[(b, c)]
        ks = kys(c)
        t0, t1_ = 3 * ks[0], 3 * ks[-1] + 3
        ring = b * 132 + c
        slot = ring % NSR
        evs = []
        for bk, (g0, g1) in TB.items():
            ng = g1 - g0
            v = PB[4 + bk][:, 0:9 * ng * 16].rearrange("p (t x) -> p t x", t=9)
            for g in range(g0, g1):
                t = pe.op(lambda e, g=g, v=v, g0=g0: e.matmul(
                    v[:, t0:t1_, (g - g0) * 16:(g - g0 + 1) * 16], win[:, n % NPT, g, :],
                    sw[:, n % 2, t0:t1_, 16 * g:16 * g + 16], start=True, stop=True),
                    *wt, *stok, smp_free[bk], sig=(g == g1 - 1))
            eng = act if (bk == 0 or (bk == 1 and c % 3 == 0)) else dve
            o = sr[:, slot, t0:t1_, g0 * 16:g1 * 16]
            if eng is act:
                x = act.op(lambda e, o=o, v=v: e.activation(o, v[:, t0:t1_, :], ACT.Copy),
                           t, srr.get(slot))
            else:
                x = dve.op(lambda e, o=o, v=v: e.tensor_copy(o, v[:, t0:t1_, :]),
                           t, srr.get(slot))
            smp_free[bk] = x
            evs.append(x)
        winr[n] = t
        swr[n] = t
        srw[(b, c)] = evs

    xow, oc_free = {}, [None]
    xl = {}

    def outconv(G):
        b, q = divmod(G, GI)
        need = [t for c in range(4 * q - 1, 4 * q + 5) for t in srw[(b, c)]]
        todo = []
        for ky in (1, 0, 2):
            for r0, s, m in pieces(b * 132 + 4 * q + ky - 1, 4, NSR):
                o0 = r0 - (b * 132 + 4 * q + ky - 1)
                for kx in range(3):
                    todo.append((3 * ky + kx, s, m, o0))
        for n, (tap, s, m, o0) in enumerate(todo):
            t = pe.op(lambda e, tap=tap, s=s, m=m, o0=o0, n=n: e.matmul(
                PB[7][:, o0 * 128:(o0 + m) * 128].rearrange("p (r c) -> p r c", r=m),
                k["wcv"][:, tap, :], sr[:, s:s + m, tap, :],
                start=(n == 0), stop=(n == len(todo) - 1), skip_group_check=True),
                oc_free[0], *need, sig=(n == len(todo) - 1))
        for c in range(4 * q - 1, 4 * q + 5):
            srr[(b * 132 + c) % NSR] = t
        u = dve.op(lambda e: e.tensor_tensor(xo[:, G % 2, :], PB[7][:, :], xin[:, G % NX, :], ALU.add),
                   t, xow.get(G - 2))
        oc_free[0] = u
        xl[G] = u
        xow[G] = p.q["st"].dma(lambda e: e.dma_start(
            x1d[b * 128:(b + 1) * 128, 4 * q * W:4 * q * W + 512], xo[:, G % 2, :]), u)

    def load(G):
        b, q = divmod(G, GI)
        tl[G] = p.q["ld"].dma(lambda e: e.dma_start(
            xin[:, G % NX, :], ins["x"][b * 128:(b + 1) * 128, 4 * q * W:4 * q * W + 512]), xl.get(G - NX))

    centres = [(b, c) for b in range(B) for c in range(-1, H + 1)]
    rank = {bc: i for i, bc in enumerate(centres)}
    prev = None
    done = 0
    stok = {}

    def advance(upto):
        nonlocal done
        while done < upto:
            bc = centres[done]
            load_window(*bc)
            stok[bc] = weights(*bc)
            if done:
                sample(*centres[done - 1], stok.pop(centres[done - 1]))
                pb, pc = centres[done - 1]
                if pc >= 4 and pc % 4 == 0:
                    outconv(pb * GI + pc // 4 - 1)
            done += 1

    for G in range(NX - 1):
        load(G)
    for G in range(NG + 3):
        if G < NG:
            ln(G)
        if G >= 1 and G - 1 < NG:
            back(G - 1)
            if G + NX - 2 < NG and G >= 1:
                pass
        if 0 <= G - 2 < NG:
            offsets(G - 2)
        if G >= 3:
            g = G - 3
            b, q = divmod(g, GI)
            last = (b, H) if q == GI - 1 else (b, 4 * q + 1)
            upto = rank[last] + 1
            advance(upto)
        n = G + NX - 1
        if n < NG and (n - NX) in xl:
            load(n)
        elif n < NG:
            if n < NX:
                load(n)
            else:
                k.setdefault("late", []).append(n)
        while k.get("late") and (k["late"][0] - NX) in xl:
            load(k["late"].pop(0))
    bc = centres[-1]
    sample(*bc, stok.pop(bc))
    outconv(NG - 1)


def far_flag(nc, ctx, p, k):
    S = lambda name, shape, dt=F32: ctx.enter_context(nc.sbuf_tensor(name, shape, dt))
    r = S("g_r", [96, 3])
    T = ctx.enter_context(nc.psum_tensor("g_t", [1, 512], F32))
    d = p.dve
    a = d.op(lambda e: e.tensor_reduce(r[:, 0:1], k["fm"][:, 0:NG], AX.X, ALU.max))
    b = d.op(lambda e: e.tensor_reduce(r[:, 1:2], k["fm"][:, NG:2 * NG], AX.X, ALU.min))
    b = d.op(lambda e: e.tensor_scalar(r[:, 1:2], r[:, 1:2], -1.0, None, ALU.mult), b)
    c = d.op(lambda e: e.tensor_tensor(r[:, 2:3], r[:, 0:1], r[:, 1:2], ALU.max), a, b)
    t = p.pe.op(lambda e: e.transpose(T[0:1, 0:96], r[:, 2:3], k["ident"][0:96, 0:96]), c)
    g = d.op(lambda e: e.tensor_reduce(k["gm"][:, 0:1], T[0:1, 0:96], AX.X, ALU.max), t)
    g = d.op(lambda e: e.tensor_scalar(k["gm"][:, 0:1], k["gm"][:, 0:1], REACH, None, ALU.is_gt), g)
    t = d.op(lambda e: e.tensor_copy(k["flag"][:, :], k["gm"][:, 0:1]), g)
    for eng in (p.pe, p.act, p.dve, p.pool, p.sp):
        eng.wait(t)


def far_rows(nc, ins, k, xtp, offd, x1d):
    with ExitStack() as ctx:
        S = lambda name, shape, dt=F32: ctx.enter_context(nc.sbuf_tensor(name, shape, dt))
        orow = S("f_or", [18, 128]); of = S("f_of", [128, 9, 2]); ri = S("f_ri", [128, 9, 2], I32)
        rf = S("f_rf", [128, 9, 2]); gt = S("f_gt", [128, 9, 2]); fl = S("f_fl", [128, 9, 2])
        fr = S("f_fr", [128, 2, 9, 2]); ps = S("f_ps", [128, 9, 2]); xf = S("f_xf", [128, 4, 9])
        ii = S("f_ii", [128, 4, 9], I32); wt = S("f_wt", [128, 4, 9]); ct = S("f_ct", [128, 9, 2])
        ctx0 = S("f_c0", [128, 9, 2]); bb = S("f_bb", [128, 1]); xr = S("f_xr", [128, 128])
        g = S("f_g", [128, 9, 4, 128]); sT = S("f_sT", [128, 9, 128]); xo = S("f_xo", [128, 128])
        P0 = ctx.enter_context(nc.psum_tensor("f_p0", [128, 512], F32))
        PT = [ctx.enter_context(nc.psum_tensor(f"f_pt{i}", [128, 512], F32)) for i in range(3)]
        PO = ctx.enter_context(nc.psum_tensor("f_po", [128, 512], F32))
        s0 = ctx.enter_context(nc.semaphore("f_init"))
        with nc.Block() as block:
            @block.sync
            def _(e):
                e.dma_start(ctx0[:, :, :], ins["far"][:, :, :]).then_inc(s0, 16)
                e.wait_ge(s0, 16)

            @block.vector
            def _(e):
                e.memset(bb[:, :], float(3 * PC + 3))
                e.wait_ge(s0, 16)

            @block.tensor
            def _(e):
                e.wait_ge(s0, 16)

            @block.scalar
            def _(e):
                e.wait_ge(s0, 16)

            @block.gpsimd
            def _(e):
                e.wait_ge(s0, 16)
        names = ("pe", "act", "dve", "pool", "sp", "in0", "in1", "st0", "g0", "g1", "g2", "g3")
        sems = [ctx.enter_context(nc.semaphore("f_" + n)) for n in names]

        def row(b, y):
            sm = dict(zip(names, sems))
            p = Phase.__new__(Phase)
            p.pe, p.act, p.dve, p.pool, p.sp = (Engine(n, sm[n]) for n in names[:5])
            p.q = {"i": Queue(p.sp, [sm["in0"], sm["in1"]]), "g": Queue(p.pool, [sm[f"g{i}"] for i in range(4)]),
                   "o": Queue(p.sp, [sm["st0"]])}
            pe, act, dve, pool = p.pe, p.act, p.dve, p.pool
            t0 = p.q["i"].dma(lambda e: e.dma_start(
                orow[:, :], offd[:, bass.ds(b * (H * W) + y * W, W)]))
            t1 = p.q["i"].dma(lambda e: e.dma_start(
                xr[:, :], ins["x"][bass.ds(b * 128, 128), bass.ds(y * W, W)]))
            t = pe.op(lambda e: e.transpose(P0[:, 0:18], orow[:, :], k["ident"][0:18, 0:18]), t0)
            v = dve.op(lambda e: e.tensor_scalar(of[:, :, :].rearrange("p a b -> p (a b)"), P0[:, 0:18],
                                                 -400.0, 400.0, ALU.max, ALU.min), t)
            v = dve.op(lambda e: e.tensor_copy(ri[:, :, :], of[:, :, :]), v)
            v = dve.op(lambda e: e.tensor_copy(rf[:, :, :], ri[:, :, :]), v)
            v = dve.op(lambda e: e.tensor_tensor(gt[:, :, :], rf[:, :, :], of[:, :, :], ALU.is_gt), v)
            v = dve.op(lambda e: e.tensor_tensor(fl[:, :, :], rf[:, :, :], gt[:, :, :], ALU.subtract), v)
            f1 = dve.op(lambda e: e.tensor_tensor(fr[:, 1], of[:, :, :], fl[:, :, :], ALU.subtract), v)
            f0 = dve.op(lambda e: e.tensor_scalar(fr[:, 0], fr[:, 1], -1.0, 1.0, ALU.mult, ALU.add), f1)
            v = dve.op(lambda e: e.tensor_tensor(ps[:, :, :], fl[:, :, :], ct[:, :, :], ALU.add), v)
            c0 = dve.op(lambda e: e.tensor_scalar(ps[:, :, 0:1], ps[:, :, 0:1], -2.0, 129.0, ALU.max,
                                                  ALU.min), v)
            c1 = dve.op(lambda e: e.tensor_scalar(ps[:, :, 1:2], ps[:, :, 1:2], -2.0, 130.0, ALU.max,
                                                  ALU.min), v)
            v = dve.op(lambda e: e.scalar_tensor_tensor(out=xf[:, 0, :], in0=ps[:, :, 0], scalar=float(PC),
                                                        in1=ps[:, :, 1], op0=ALU.mult, op1=ALU.add), c0, c1)
            v = dve.op(lambda e: e.tensor_scalar(xf[:, 0, :], xf[:, 0, :], bb[:, 0:1], None, ALU.add), v)
            for j, o in ((1, 1), (2, PC), (3, PC + 1)):
                z = dve.op(lambda e, j=j, o=o: e.tensor_scalar(xf[:, j, :], xf[:, 0, :], float(o), None,
                                                               ALU.add), v)
            z = dve.op(lambda e: e.tensor_copy(ii[:, :, :], xf[:, :, :]), z)
            for j in range(4):
                wv = dve.op(lambda e, j=j: e.tensor_tensor(wt[:, j, :], fr[:, j // 2, :, 0],
                                                           fr[:, j % 2, :, 1], ALU.mult), f0)
            nx = dve.op(lambda e: e.tensor_scalar(ct[:, :, 0:1], ct[:, :, 0:1], 1.0, None, ALU.add), v)
            for t_ in range(9):
                for j in range(4):
                    p.q["g"].dma(lambda e, t_=t_, j=j: e.indirect_dma_start(
                        out=g[:, t_, j, :], out_offset=None, in_=xtp[:, :],
                        in_offset=bass.IndirectOffsetOnAxis(ap=ii[:, j, t_:t_ + 1], axis=0)), z)
            dve.wait(*p.q["g"].all())
            pool.wait(*p.q["g"].all())
            for t_ in range(9):
                a = dve.op(lambda e, t_=t_: e.tensor_scalar(g[:, t_, 0, :], g[:, t_, 0, :], wt[:, 0, t_:t_ + 1],
                                                            None, ALU.mult), wv)
                for j in range(1, 4):
                    a = dve.op(lambda e, t_=t_, j=j: e.scalar_tensor_tensor(
                        out=g[:, t_, 0, :], in0=g[:, t_, j, :], scalar=wt[:, j, t_:t_ + 1],
                        in1=g[:, t_, 0, :], op0=ALU.mult, op1=ALU.add), a)
            for t_ in range(9):
                t = pe.op(lambda e, t_=t_: e.transpose(PT[t_ // 3][:, (t_ % 3) * 128:(t_ % 3 + 1) * 128],
                                                       g[:, t_, 0, :], k["ident"][:, :]), a)
            for i in range(3):
                u = act.op(lambda e, i=i: e.copy(sT[:, 3 * i:3 * i + 3, :].rearrange("p a b -> p (a b)"),
                                                 PT[i][:, 0:384]), t)
            for t_ in range(9):
                t = pe.op(lambda e, t_=t_: e.matmul(PO[:, 0:128], k["wcv"][:, t_, :], sT[:, t_, :],
                                                    start=(t_ == 0), stop=(t_ == 8)), u)
            o = dve.op(lambda e: e.tensor_tensor(xo[:, :], PO[:, 0:128], xr[:, :], ALU.add), t, t1)
            s = p.q["o"].dma(lambda e: e.dma_start(
                x1d[bass.ds(b * 128, 128), bass.ds(y * W, W)], xo[:, :]), o)
            p.emit(nc)
            with nc.Block() as block:
                @block.gpsimd
                def _(e):
                    e.dma_reset(range(min(s.num for s in sems[-4:]), max(s.num for s in sems[-4:]) + 1))
                    for s in sems:
                        e.sem_clear(s)

        with nc.Fori(0, B) as b:
            with nc.Block() as block:
                @block.vector
                def _(e):
                    e.tensor_copy(ct[:, :, :], ctx0[:, :, :])
            with nc.Fori(0, H) as y:
                row(b, y)
            with nc.Block() as block:
                @block.vector
                def _(e):
                    e.tensor_scalar(bb[:, :], bb[:, :], float(PIX), None, ALU.add)


def phase_bc(nc, ctx, p, ins, k, x1d, x2d, x3d, lgd):
    S = lambda name, shape, dt=F32: ctx.enter_context(nc.sbuf_tensor(name, shape, dt))
    ew = S("b_ew", [128, 8, 128]); rw = S("b_rw", [128, 8]); eb = S("b_eb", [8, 128])
    rb = S("b_rb", [128, 8]); al = S("b_al", [128, 128]); gw = S("b_gw", [128, 64]); gb = S("b_gb", [64, 1])
    x1 = S("b_x1", [128, 3, 512])
    tk = S("b_tk", [128, 3, 4, 128]); tn = S("b_tn", [128, 2, 4, 128]); tnT = S("b_tnT", [128, 2, 512])
    st = S("b_st", [128, 2, 4, 6]); mv = S("b_mv", [128, 2, 4, 2]); rs = S("b_rs", [128, 2, 8])
    lg = S("b_lg", [128, 2, 4, 8]); mx = S("b_mx", [128, 2, 4, 8]); m2 = S("b_m2", [128, 2, 4, 8])
    l2 = S("b_l2", [128, 2, 4, 8]); lm = S("b_lm", [128, 2, 4, 8]); ex = S("b_ex", [128, 2, 4, 8])
    mk = S("b_mk", [128, 2, 4, 8]); pm = S("b_pm", [128, 2, 4, 8]); sm = S("b_sm", [128, 2, 8])
    pw = S("b_pw", [128, 2, 4, 8]); pT = S("b_pT", [8, 2, 512])
    xa = S("b_xa", [128, 3, 4, 128]); xb = S("b_xb", [128, 2, 4, 128])
    sy = S("b_sy", [128, 4, 2, 128])
    st2 = S("b_st2", [128, 2, 4, 6]); mv2 = S("b_mv2", [128, 2, 4, 2]); rs2 = S("b_rs2", [128, 2, 8])
    tn2 = S("b_tn2", [128, 2, 4, 128])
    xf = S("b_xf", [128, 2, 128, 128])
    x2r = S("c_x2", [128, 3, 4, 128]); x3t = S("c_x3", [128, 3, 4, 128])
    st3 = S("c_st", [128, 2, 4, 6]); mv3 = S("c_mv", [128, 2, 4, 2]); rs3 = S("c_rs", [128, 2, 8])
    tn3 = S("c_tn", [128, 2, 4, 128]); tnT3 = S("c_tnT", [128, 2, 512]); lo = S("c_lo", [64, 2, 512])
    PS = lambda name, shape: ctx.enter_context(nc.psum_tensor(name, shape, F32))
    TB = [PS("b_t0", [128, 512]), PS("b_t1", [128, 512])]
    YB = [PS("b_y0", [128, 2, 4, 128]), PS("b_y1", [128, 2, 4, 128])]
    RB, ZB = PS("b_r", [128, 512]), PS("b_z", [128, 4, 128])
    pe, act, dve, pool = p.pe, p.act, p.dve, p.pool
    ident = k["ident"]

    q = p.q["c"]
    for t, n in ((rw, "rw"), (eb, "eb"), (rb, "rb"), (al, "al"), (gw, "gw"), (gb, "gb")):
        cw = q.dma(lambda e, t=t, n=n: e.dma_start(t[:, :], ins[n][:, :]))
    consts = q.all() + [q.dma(lambda e: e.dma_start(ew[:, :, :], ins["ew"][:, :, :]))]
    pe.wait(*consts)
    dve.wait(*consts)
    act.wait(*consts)
    big = dve.op(lambda e: e.memset(m2[:, :, :, :], 3.0e38))

    pool_k = [0]
    free = [None, None]
    yfree = [None, None]
    rfree, zfree = [None], [None]
    T = {}
    g_ = lambda *key: T.get(key)

    def take():
        i = pool_k[0] % 2
        pool_k[0] += 1
        return i, TB[i]

    def transposes(src, *waits):
        i, D = take()
        for r in range(4):
            t = pe.op(lambda e, r=r: e.transpose(D[:, r * 128:(r + 1) * 128], src(r), ident[:, :]),
                      free[i], *waits, sig=(r == 3))
        return i, D, t

    def load(G):
        b, h = divmod(G, GI)
        T["x1", G] = p.q["ld"].dma(lambda e: e.dma_start(
            x1[:, G % 3, :], x1d[b * 128:(b + 1) * 128, h * 512:h * 512 + 512]), g_("t1", G - 3))

    def b1(G):
        i, D, t = transposes(lambda r: x1[:, G % 3, r * 128:(r + 1) * 128], T["x1", G])
        T["t1", G] = t
        u = act.op(lambda e: e.copy(tk[:, G % 3], D[:, :].rearrange("p (r c) -> p r c", r=4)), t,
                   g_("x0", G - 3))
        free[i] = u
        T["tk", G] = u
        T["tn", G] = layernorm_tokens(p, tk[:, G % 3], st[:, G % 2], mv[:, G % 2], rs[:, G % 2],
                                      tn[:, G % 2], 1e-5, u, None, k["mhalf"], (g_("t2", G - 2),),
                                      g_("tn", G - 2))

    def b2(G):
        w = G % 2
        i, D, t = transposes(lambda r: tn[:, w, r, :], T["tn", G])
        T["t2", G] = t
        u = act.op(lambda e: e.copy(tnT[:, w, :], D[:, :]), t, g_("y", G - 2))
        free[i] = u
        T["tT", G] = u
        for r in range(4):
            t = pe.op(lambda e, r=r: e.matmul(RB[:, r * 8:r * 8 + 8], tnT[:, w, r * 128:(r + 1) * 128],
                                              rw[:, :], start=True, stop=True), u, rfree[0], sig=(r == 3))
        L = dve.op(lambda e: e.tensor_tensor(lg[:, w], RB[:, 0:32].rearrange("p (r e) -> p r e", r=4),
                                             rb[:, None, :].to_broadcast([128, 4, 8]), ALU.add), t,
                   g_("pm", G - 2))
        T["lg", G] = L
        for r in range(4):
            m = dve.op(lambda e, r=r: e.max(mx[:, w, r, :], lg[:, w, r, :]), L, g_("lm", G - 2))
        c = dve.op(lambda e: e.tensor_copy(m2[:, w, :, 0:2], mx[:, w, :, 0:2]), m, big)
        lmt = dve.op(lambda e: e.tensor_tensor(lm[:, w], lg[:, w],
                                               mx[:, w, :, 0:1].to_broadcast([128, 4, 8]), ALU.subtract),
                     g_("ex", G - 2))
        T["lm", G] = lmt
        for r in range(4):
            z = dve.op(lambda e, r=r: e.match_replace(l2[:, w, r, :], m2[:, w, r, :], lg[:, w, r, :],
                                                      -3.0e38), c, g_("mk", G - 2))
        xt = act.op(lambda e: e.activation(ex[:, w], lm[:, w], ACT.Exp), lmt, g_("pm", G - 2))
        T["ex", G] = xt
        T["mk", G] = dve.op(lambda e: e.tensor_tensor(mk[:, w], l2[:, w], lg[:, w], ALU.is_lt), z)
        T["pm", G] = dve.op(lambda e: e.tensor_tensor(pm[:, w], ex[:, w], mk[:, w], ALU.mult), xt,
                            T["mk", G])
        s = dve.op(lambda e: e.tensor_reduce(sm[:, w, 0:4], pm[:, w], AX.X, ALU.add), T["pm", G])
        s = dve.op(lambda e: e.reciprocal(sm[:, w, 4:8], sm[:, w, 0:4]), s)
        T["p", G] = dve.op(lambda e: e.tensor_tensor(pw[:, w], pm[:, w],
                                                     sm[:, w, 4:8, None].to_broadcast([128, 4, 8]), ALU.mult),
                           s, g_("acc", G - 2), g_("pt", G - 2))

    def b3(G):
        w = G % 2
        for r in range(4):
            t = pe.op(lambda e, r=r: e.transpose(RB[0:8, r * 128:(r + 1) * 128], pw[:, w, r, :], ident[:, :]),
                      T["p", G], g_("lg", G + 1), rfree[0], sig=(r == 3))
        T["pt", G] = t
        u = act.op(lambda e: e.copy(pT[:, w, :], RB[0:8, :]), t, g_("pb", G - 2))
        rfree[0] = u
        for r in range(4):
            t = pe.op(lambda e, r=r: e.matmul(ZB[:, r, :], pT[0:8, w, r * 128:(r + 1) * 128], eb[:, :],
                                              start=True, stop=True), u, zfree[0], sig=(r == 3))
        T["pb", G] = t
        a3 = xa[:, G % 3]
        v = dve.op(lambda e: e.tensor_tensor(a3, ZB[:, :, :], tk[:, G % 3], ALU.add), t,
                   g_("x2s", G - 3), g_("tn2", G - 3))
        zfree[0] = v
        T["x0", G] = v
        for r in range(4):
            n = 4 * G + r
            Y = YB[n % 2]
            for j in range(2):
                t = pe.op(lambda e, r=r, j=j, Y=Y: e.matmul(
                    Y[:, j].rearrange("p a b -> p (a b)"), tnT[:, w, r * 128:(r + 1) * 128],
                    ew[:, 4 * j:4 * j + 4, :].rearrange("p a b -> p (a b)"), start=True, stop=True),
                    yfree[n % 2], T["tT", G], sig=(j == 1))
            ta, tb = v, g_("acc", G - 2)
            for i in range(4):
                ta = dve.op(lambda e, r=r, i=i, Y=Y: e.scalar_tensor_tensor(
                    out=a3[:, r, :], in0=Y[:, 0, i, :], scalar=pw[:, w, r, i:i + 1], in1=a3[:, r, :],
                    op0=ALU.mult, op1=ALU.add), t, ta)
                if i == 0:
                    tb = dve.op(lambda e, r=r, Y=Y: e.tensor_scalar(
                        xb[:, w, r, :], Y[:, 1, 0, :], pw[:, w, r, 4:5], None, ALU.mult), tb)
                else:
                    tb = dve.op(lambda e, r=r, i=i, Y=Y: e.scalar_tensor_tensor(
                        out=xb[:, w, r, :], in0=Y[:, 1, i, :], scalar=pw[:, w, r, 4 + i:5 + i],
                        in1=xb[:, w, r, :], op0=ALU.mult, op1=ALU.add), tb)
            yfree[n % 2] = tb
        T["y", G] = t
        T["acc", G] = dve.op(lambda e: e.tensor_tensor(a3, a3, xb[:, w], ALU.add), tb, ta)
        b, h = divmod(G, GI)
        dst = x2d[b * H * W + h * 512:b * H * W + h * 512 + 512, :].rearrange("(r w) c -> w r c", w=128)
        T["x2s", G] = p.q["st"].dma(lambda e: e.dma_start(dst, a3), T["acc", G])

    def b4(G):
        w = G % 2
        T["tn2", G] = layernorm_tokens(p, xa[:, G % 3], st2[:, w], mv2[:, w], rs2[:, w], tn2[:, w], 1e-6,
                                       T["acc", G], None, k["mhalf"], (g_("t4", G - 2),), g_("tn2", G - 2))

    def b5(G):
        b, h = divmod(G, GI)
        w = G % 2
        i, D, t = transposes(lambda r: tn2[:, w, r, :], T["tn2", G])
        T["t4", G] = t
        F = xf[:, b % 2]
        v = D[:, :].rearrange("p (r c) -> p r c", r=4)
        runs = [(0, 1, 0, 1), (1, 4, 127, -1)] if h == 0 else [(0, 4, 128 - 4 * h, -1)]
        for r0, r1, o, s in runs:
            rows = slice(o, o - (r1 - r0) if o - (r1 - r0) >= 0 else None, -1) if s < 0 else slice(o, o + 1)
            act.op(lambda e, r0=r0, r1=r1, rows=rows: e.copy(F[:, rows, 0:1], v[:, r0:r1, 0:1]), t,
                   g_("c", b - 2))
            u = act.op(lambda e, r0=r0, r1=r1, rows=rows: e.copy(F[:, rows, 127:0:-1], v[:, r0:r1, 1:128]))
        free[i] = u
        T["xf", G] = u

    def loadc(G):
        b, h = divmod(G, GI)
        src = x2d[b * H * W + h * 512:b * H * W + h * 512 + 512, :].rearrange("(r w) c -> w r c", w=128)
        T["x2", G] = p.q["lc"].dma(lambda e: e.dma_start(x2r[:, G % 3], src), T["x2s", G], g_("x3", G - 3))

    def c1(G):
        b, h = divmod(G, GI)
        w = G % 2
        need = T["xf", b * GI + GI - 1]
        for r in range(4):
            t = pe.op(lambda e, r=r: e.matmul(ZB[:, r, :], xf[:, b % 2, 4 * h + r, :], al[:, :],
                                              start=True, stop=True), need, zfree[0], sig=(r == 3))
        T["c", b] = t
        u = dve.op(lambda e: e.tensor_tensor(x3t[:, G % 3], ZB[:, :, :], x2r[:, G % 3], ALU.add), t,
                   T["x2", G], g_("x3s", G - 3), g_("tn3", G - 3))
        zfree[0] = u
        T["x3", G] = u
        dst = x3d[b * H * W + h * 512:b * H * W + h * 512 + 512, :].rearrange("(r w) c -> w r c", w=128)
        T["x3s", G] = p.q["st"].dma(lambda e: e.dma_start(dst, x3t[:, G % 3]), u)
        T["tn3", G] = layernorm_tokens(p, x3t[:, G % 3], st3[:, w], mv3[:, w], rs3[:, w], tn3[:, w], 1e-5,
                                       u, None, k["mhalf"], (g_("t5", G - 2),), g_("tn3", G - 2))

    def c2(G):
        w = G % 2
        i, D, t = transposes(lambda r: tn3[:, w, r, :], T["tn3", G])
        T["t5", G] = t
        u = act.op(lambda e: e.copy(tnT3[:, w, :], D[:, :]), t, g_("lgm", G - 2))
        free[i] = u
        T["tT3", G] = u

    def c3(G):
        b, h = divmod(G, GI)
        w = G % 2
        i, D = take()
        t = pe.op(lambda e: e.matmul(D[0:64, :], gw[:, :], tnT3[:, w, :], start=True, stop=True),
                  free[i], T["tT3", G])
        T["lgm", G] = t
        u = act.op(lambda e: e.activation(lo[:, w, :], D[0:64, :], ACT.Identity, bias=gb[:, 0:1]), t,
                   g_("los", G - 2))
        free[i] = u
        T["los", G] = p.q["st"].dma(lambda e: e.dma_start(
            lgd[b * 64:b * 64 + 64, h * 512:h * 512 + 512], lo[:, w, :]), u)

    LAG = GI + 3
    for G in range(3):
        load(G)
    for s in range(NG + LAG + 4):
        if s < NG:
            b1(s)
            if s + 3 < NG:
                load(s + 3)
        if 0 <= s - 1 < NG:
            b2(s - 1)
        if 0 <= s - LAG < NG:
            if s == LAG:
                loadc(0)
                loadc(1)
            c1(s - LAG)
            if s - LAG + 2 < NG:
                loadc(s - LAG + 2)
        if 0 <= s - 2 < NG:
            b3(s - 2)
            b4(s - 2)
        if 0 <= s - 3 < NG:
            b5(s - 3)
        if 0 <= s - LAG - 1 < NG:
            c2(s - LAG - 1)
        if 0 <= s - LAG - 2 < NG:
            c3(s - LAG - 2)


def phase_d(nc, ctx, p, ins, k, x3d, lgd):
    S = lambda name, shape, dt=F32: ctx.enter_context(nc.sbuf_tensor(name, shape, dt))
    NP_, NCH, EC = B // 2, 8, 8
    Lb = S("d_L", [128, H * W])
    w1 = S("d_w1", [128, 3, EC, 512]); w2 = S("d_w2", [128, 2, EC, 4, 128])
    b1r = S("d_b1r", [64, 512]); b2r = S("d_b2r", [128, 128]); base = S("d_base", [128, 2])
    b1t = S("d_b1t", [128, 4, 64])
    v8 = S("d_v8", [128, NP_, 8]); ix = S("d_ix", [128, NP_, 8], U32); nm = S("d_nm", [128, NP_, 1])
    sm = S("d_sm", [128, NP_, 2]); ev = S("d_ev", [128, NP_, 8]); tv = S("d_tv", [128, NP_, 8])
    ixf = S("d_ixf", [128, NP_, 8]); gi = S("d_gi", [128, NP_, 8], I32)
    xg = S("d_xg", [128, NP_, 8, 128]); ln = S("d_ln", [128, 2, 4, 128])
    st = S("d_st", [128, 2, 4, 6]); mv = S("d_mv", [128, 2, 4, 2]); rs = S("d_rs", [128, 2, 8])
    pl = S("d_pl", [128, NP_, 128]); plT = S("d_plT", [128, B, 64])
    hb = S("d_hb", [128, 64, 4, B]); hs = S("d_hs", [128, 64, 4, B])
    oT = S("d_oT", [128, B, 64]); ov = S("d_ov", [128, NP_, 128])
    bi = S("d_bi", [128, NP_, 8, 128]); ib = S("d_ib", [128, 8, 128])
    A = S("d_A", [128, NP_, 8, 128]); eq = S("d_eq", [128, 8, 128])
    PS = lambda name, shape: ctx.enter_context(nc.psum_tensor(name, shape, F32))
    P0, P1 = PS("d_p0", [128, 512]), PS("d_p1", [128, 512])
    HB = PS("d_h", [128, 64, 4, B]) if B == 4 else PS("d_h", [128, 64, 4, B])
    OB = PS("d_o", [128, 512])
    IB = PS("d_i", [128, 2, 512])
    pe, act, dve, pool = p.pe, p.act, p.dve, p.pool
    ident = k["ident"]

    q = p.q["c"]
    tb1 = q.dma(lambda e: e.dma_start(b1r[:, :], ins["w1"][:, 128, :]))
    q.dma(lambda e: e.dma_start(b2r[0:64, :], ins["w2"][:, 512, :]))
    q.dma(lambda e: e.dma_start(b2r[64:128, :], ins["w2"][:, 512, :]))
    q.dma(lambda e: e.dma_start(base[:, :], ins["base"][:, :]))
    consts = q.all()
    tL = {}
    tL[0] = p.q["L"].dma(lambda e: e.dma_start(Lb[:, :], lgd[0:128, :]))
    w1t, w2t, w1r, w2r = {}, {}, {}, {}

    def ldw1(c):
        w1t[c] = p.q["w1"].dma(lambda e: e.dma_start(
            w1[:, c % 3], ins["w1"][c * EC:(c + 1) * EC, 0:128, :].rearrange("e d h -> d e h")), w1r.get(c - 3))

    def ldw2(c):
        w2t[c] = p.q["w2"].dma(lambda e: e.dma_start(
            w2[:, c % 2].rearrange("p e c o -> p e (c o)"),
            ins["w2"][c * EC:(c + 1) * EC, 0:512, :].rearrange("e (p c) o -> p e (c o)", c=4)),
            w2r.get(c - 2))

    for c in range(3):
        ldw1(c)
    for c in range(2):
        ldw2(c)
    for c in range(4):
        t = pe.op(lambda e, c=c: e.transpose(P0[:, c * 64:(c + 1) * 64], b1r[:, c:512:4], ident[0:64, 0:64]),
                  tb1, sig=(c == 3))
    tb = act.op(lambda e: e.copy(b1t[:, :, :], P0[:, 0:256].rearrange("p (c e) -> p c e", c=4)), t)
    p0free = tb
    dve.wait(*consts)
    one = None
    tg, tA = {}, {}
    for a in range(NP_):
        if a:
            tL[a] = p.q["L"].dma(lambda e, a=a: e.dma_start(Lb[:, :], lgd[a * 128:(a + 1) * 128, :]), xe, xm)
        m = dve.op(lambda e, a=a: e.max(v8[:, a, :], Lb[:, :]), tL[a])
        n = dve.op(lambda e, a=a: e.tensor_scalar(nm[:, a, :], v8[:, a, 0:1], -1.0, None, ALU.mult), m)
        xm = dve.op(lambda e, a=a: e.max_index(ix[:, a, :], v8[:, a, :], Lb[:, :]), m)
        xv = act.op(lambda e, a=a: e.activation(ev[:, a, :], v8[:, a, :], ACT.Exp, bias=nm[:, a, :]), n)
        xe = act.op(lambda e, a=a: e.activation(Lb[:, :], Lb[:, :], ACT.Exp, bias=nm[:, a, :],
                                                accum_out=sm[:, a, 0:1]), xm)
        f = dve.op(lambda e, a=a: e.tensor_copy(ixf[:, a, :], ix[:, a, :]), xm)
        f = dve.op(lambda e, a=a: e.tensor_scalar(ixf[:, a, :], ixf[:, a, :], base[:, a:a + 1], None,
                                                  ALU.add), f)
        g = dve.op(lambda e, a=a: e.tensor_copy(gi[:, a, :], ixf[:, a, :]), f)
        r = dve.op(lambda e, a=a: e.reciprocal(sm[:, a, 1:2], sm[:, a, 0:1]), xe)
        tvt = dve.op(lambda e, a=a: e.tensor_scalar(tv[:, a, :], ev[:, a, :], sm[:, a, 1:2], None,
                                                    ALU.mult), r, xv)
        tx = []
        for kk in range(8):
            tx.append(p.q["g"].dma(lambda e, a=a, kk=kk: e.indirect_dma_start(
                out=xg[:, a, kk, :], out_offset=None, in_=x3d[:, :],
                in_offset=bass.IndirectOffsetOnAxis(ap=gi[:, a, kk:kk + 1], axis=0)), g))
        tg[a] = tx
        last, prev = None, None
        for half in range(2):
            last = layernorm_tokens(p, xg[:, a, 4 * half:4 * half + 4, :], st[:, half], mv[:, half],
                                    rs[:, half], ln[:, half], 1e-5, tx[4 * half + 3], None, k["mhalf"],
                                    (prev,), prev)
            if half == 0:
                dve.wait(*tx)
            for j in range(4):
                kk = 4 * half + j
                if kk == 0:
                    prev = dve.op(lambda e, a=a: e.tensor_scalar(pl[:, a, :], ln[:, 0, 0, :], tv[:, a, 0:1],
                                                                 None, ALU.mult), last, tvt)
                else:
                    prev = dve.op(lambda e, a=a, kk=kk: e.scalar_tensor_tensor(
                        out=pl[:, a, :], in0=ln[:, kk // 4, kk % 4, :], scalar=tv[:, a, kk:kk + 1],
                        in1=pl[:, a, :], op0=ALU.mult, op1=ALU.add), last, prev)
        t = pe.op(lambda e, a=a: e.transpose(P0[:, 0:128], pl[:, a, :], ident[:, :]), prev, p0free)
        plt = act.op(lambda e, a=a: e.copy(plT[:, 2 * a:2 * a + 2, :].rearrange("p b e -> p (b e)"),
                                           P0[:, 0:128]), t)
        p0free = plt
        for kk in range(8):
            bt = pool.op(lambda e, a=a, kk=kk: e.tensor_scalar(bi[:, a, kk, :], k["ones"][:, :],
                                                               ixf[:, a, kk:kk + 1], None, ALU.mult), f)
            t = pe.op(lambda e, a=a, kk=kk: e.matmul(IB[:, kk // 4, (kk % 4) * 128:(kk % 4 + 1) * 128],
                                                     bi[:, a, kk, :], ident[:, :], start=True, stop=True),
                      bt, tA.get("ib"), sig=(kk == 7))
        tA["ib"] = act.op(lambda e: e.copy(ib[:, :, :].rearrange("p (a k) c -> p a (k c)", a=2), IB[:, :, :]),
                          t, tA.get("last"))
        prevA, pe_ = None, None
        for kk in range(8):
            dst = A[:, a] if kk == 0 else eq
            pe_ = dve.op(lambda e, a=a, kk=kk, dst=dst: e.tensor_scalar(
                dst[:, :, :], ib[:, :, :], ixf[:, a, kk:kk + 1], tv[:, a, kk:kk + 1], ALU.is_equal, ALU.mult),
                tA["ib"], tvt, prevA)
            if kk:
                prevA = dve.op(lambda e, a=a: e.tensor_tensor(A[:, a], A[:, a], eq[:, :, :], ALU.add), pe_)
            else:
                prevA = pe_
        tA["last"] = prevA
        tA[a] = prevA
    for c in range(NCH):
        for ee in range(EC):
            x = c * EC + ee
            for ch in range(4):
                t = pe.op(lambda e, x=x, ee=ee, ch=ch, c=c: e.matmul(
                    HB[:, x, ch, :], w1[:, c % 3, ee, ch:512:4], plT[:, :, x], start=True, stop=True),
                    w1t[c], plt, sig=(ee == EC - 1 and ch == 3))
        w1r[c] = t
        if c + 3 < NCH:
            ldw1(c + 3)
        if c % 4 == 3:
            e0, e1 = (c - 3) * EC, (c + 1) * EC
            for b in range(B):
                h = dve.op(lambda e, e0=e0, e1=e1, b=b: e.tensor_tensor(
                    hb[:, e0:e1, :, b], HB[:, e0:e1, :, b],
                    b1t[:, :, e0:e1].rearrange("p c e -> p e c"), ALU.add), t, tb)
            hg = act.op(lambda e, e0=e0, e1=e1: e.activation(hs[:, e0:e1].rearrange("p e c b -> p (e c b)"),
                                                             hb[:, e0:e1].rearrange("p e c b -> p (e c b)"),
                                                             ACT.Gelu), h)
            for cc in range(c - 3, c + 1):
                for ee in range(EC):
                    x = cc * EC + ee
                    for ch in range(4):
                        t2 = pe.op(lambda e, x=x, ee=ee, ch=ch, cc=cc: e.matmul(
                            OB[:, x:64 * B:64], w2[:, cc % 2, ee, ch, :], hs[:, x, ch, :],
                            start=(ch == 0), stop=(ch == 3)), w2t[cc], hg, sig=(ee == EC - 1 and ch == 3))
                w2r[cc] = t2
                if cc + 2 < NCH:
                    ldw2(cc + 2)
    ot = act.op(lambda e: e.copy(oT[:, :, :].rearrange("p b e -> p (b e)"), OB[:, 0:64 * B]), t2)
    for a in range(NP_):
        t = pe.op(lambda e, a=a: e.transpose(P0[:, 0:128], oT[:, 2 * a:2 * a + 2, :].rearrange(
            "p b e -> p (b e)"), ident[:, :]), ot, p0free)
        o = dve.op(lambda e, a=a: e.tensor_tensor(ov[:, a, :], P0[:, 0:128], b2r[:, :], ALU.add), t)
        p0free = o
        for kk in range(8):
            D = IB[:, kk // 4, (kk % 4) * 128:(kk % 4 + 1) * 128]
            t = pe.op(lambda e, a=a, kk=kk, D=D: e.matmul(D, A[:, a, kk, :], ov[:, a, :], start=True,
                                                          stop=True), o, tA[a], tA.get("fin"), tA["ib"],
                      sig=(kk == 7))
        u = dve.op(lambda e, a=a: e.tensor_tensor(
            xg[:, a].rearrange("p (h k) c -> p h (k c)", h=2), IB[:, :, :],
            xg[:, a].rearrange("p (h k) c -> p h (k c)", h=2), ALU.add), t, *tg[a])
        tA["fin"] = u
        sc = None
        for kk in range(8):
            sc = p.q["sc"].dma(lambda e, a=a, kk=kk: e.indirect_dma_start(
                out=x3d[:, :], out_offset=bass.IndirectOffsetOnAxis(ap=gi[:, a, kk:kk + 1], axis=0),
                in_=xg[:, a, kk, :], in_offset=None), u, sc)


def phase_e(nc, ctx, p, k, x3d, out):
    S = lambda name, shape, dt=F32: ctx.enter_context(nc.sbuf_tensor(name, shape, dt))
    NB_ = 6
    xt = S("e_x", [128, NB_, 4, 128]); xo = S("e_o", [128, NB_, 512])
    PB = [ctx.enter_context(nc.psum_tensor(f"e_p{i}", [128, 512], F32)) for i in range(4)]
    ld, tr, ev, so = {}, {}, {}, {}

    def load(G):
        src = x3d[G * 512:G * 512 + 512, :].rearrange("(r w) c -> w r c", w=128)
        ld[G] = p.q["ld"].dma(lambda e: e.dma_start(xt[:, G % NB_], src), tr.get(G - NB_))

    for G in range(NB_ - 1):
        load(G)
    for G in range(NG):
        b, h = divmod(G, GI)
        D = PB[G % 4]
        for r in range(4):
            t = p.pe.op(lambda e, r=r, D=D, G=G: e.transpose(D[:, r * 128:(r + 1) * 128], xt[:, G % NB_, r, :],
                                                             k["ident"][:, :]), ld[G], ev.get(G - 4),
                        sig=(r == 3))
        tr[G] = t
        eng = p.act if G % 2 else p.dve
        f = (lambda e, D=D, G=G: e.copy(xo[:, G % NB_, :], D[:, :])) if G % 2 else (
            lambda e, D=D, G=G: e.tensor_copy(xo[:, G % NB_, :], D[:, :]))
        ev[G] = eng.op(f, t, so.get(G - NB_))
        so[G] = p.q["st"].dma(lambda e, b=b, h=h, G=G: e.dma_start(
            out[b * 128:(b + 1) * 128, h * 512:h * 512 + 512], xo[:, G % NB_, :]), ev[G])
        if G + NB_ - 1 < NG:
            load(G + NB_ - 1)


def program(nc, ins, out, dbg):
    with ExitStack() as ctx:
        S = lambda name, shape, dt=F32: ctx.enter_context(nc.sbuf_tensor(name, shape, dt))
        D = lambda name, shape: dbg(name, shape)
        k = {
            "zero": S("zero", [128, 640]), "mhalf": S("mhalf", [128, 8]), "ones": S("ones", [128, 128]),
            "ident": S("ident", [128, 128]), "fm": S("fm", [96, 2 * NG]),
            "gm": S("gm", [1, 1]), "flag": S("flag", [1, 1], I32),
        }
        xtp = D("xtp", [B * PIX, 128])
        offd = D("offd", [18, B * H * W])
        x1d = D("x1d", [B * 128, H * W])
        x2d = D("x2d", [B * H * W, 128])
        x3d = D("x3d", [B * H * W, 128])
        lgd = D("lgd", [B * 64, H * W])
        with ExitStack() as ca:
            SA = lambda name, shape, dt=F32: ca.enter_context(nc.sbuf_tensor(name, shape, dt))
            k |= {"wof": SA("wof", [128, 9, 96]), "wcv": SA("wcv", [128, 9, 128]),
                  "sel": SA("sel", [128, 18, 120], BF16), "P": SA("P", [128, NPR * 512], BF16)}
            with ExitStack() as c0:
                k["self"] = c0.enter_context(nc.sbuf_tensor("self", [128, 18, 120], F32))
                k["cst"] = c0.enter_context(nc.sbuf_tensor("cst", [128, 512], F32))
                p0 = Phase(nc, c0, "s", {"c": ("sp", 24)})
                setup_phase(nc, c0, p0, ins, k, xtp)
                p0.emit(nc)
            with ExitStack() as c1:
                p1 = Phase(nc, c1, "a", {"ld": ("sp", 4), "w": ("sp", 20), "st": ("sp", 8)})
                phase_a(nc, c1, p1, ins, k, xtp, offd, x1d)
                p1.emit(nc)
            with ExitStack() as c1:
                pf = Phase(nc, c1, "g", {})
                far_flag(nc, c1, pf, k)
                pf.emit(nc)
            far = nc.values_load(k["flag"][0:1, 0:1], min_val=0, max_val=1)
            with nc.If(far > 0):
                far_rows(nc, ins, k, xtp, offd, x1d)
        with ExitStack() as c2:
            p2 = Phase(nc, c2, "b", {"c": ("sp", 8), "ld": ("sp", 3), "lc": ("sp", 3), "st": ("sp", 6)})
            phase_bc(nc, c2, p2, ins, k, x1d, x2d, x3d, lgd)
            p2.emit(nc)
        with ExitStack() as c3:
            p3 = Phase(nc, c3, "d", {"c": ("sp", 4), "L": ("sp", 1), "w1": ("sp", 3), "w2": ("sp", 2),
                                     "g": ("pool", 8), "sc": ("pool", 8)})
            phase_d(nc, c3, p3, ins, k, x3d, lgd)
            p3.emit(nc)
        with ExitStack() as c4:
            p4 = Phase(nc, c4, "e", {"ld": ("sp", 6), "st": ("act", 6)})
            phase_e(nc, c4, p4, k, x3d, out)
            p4.emit(nc)


def constants():
    ident = np.eye(128, dtype=np.float32)
    sel = np.zeros((128, 18, 120), np.float32)
    m = np.arange(120)
    j, i = m // 24, m % 24
    for t in range(9):
        for part in (0, 32, 64):
            sel[part + 2 * t, t, :] = 1.0
            sel[part + 2 * t + 1, 9 + t, :] = 1.0
        sel[96, t, :] = 2 - j
        sel[96, 9 + t, :] = t % 3 + 2 - i
        sel[97, 9 + t, :] = 1.0
    cst = np.ones((2, 512), np.float32)
    cst[1] = np.arange(512) % 16
    base = (np.arange(128)[:, None] // 64 + 2 * np.arange(2)[None, :]).astype(np.float32) * (H * W)
    far = np.zeros((128, 9, 2), np.float32)
    far[:, :, 0] = np.arange(9)[None, :] // 3 - 1
    far[:, :, 1] = np.arange(9)[None, :] % 3 - 1 + np.arange(128)[:, None]
    return {"ident": ident, "sel": sel, "cst": cst, "base": base, "far": far}


OUTN = ["out"]
DBG = ["xtp", "offd", "x1d", "x2d", "x3d", "lgd"]


def kernel(**inputs):
    import concourse.bacc as _bacc
    from concourse.bass_utils import run_bass_kernel_spmd as _run

    a = {n: np.ascontiguousarray(v) for n, v in inputs.items()}
    arr = {"x": a["x"].reshape(B * 128, H * W)}
    wo = np.zeros((128, 9, 96), np.float32)
    t = a["L0_conv_w_off"].reshape(18, 128, 9).transpose(1, 2, 0)
    for s in (0, 32, 64):
        wo[:, :, s:s + 18] = t
    arr["wof"] = wo
    arr["wcv"] = np.ascontiguousarray(a["L0_conv_w_conv"].reshape(128, 128, 9).transpose(1, 2, 0))
    arr["rw"] = a["L0_ffn_router_w"]
    arr["rb"] = np.ascontiguousarray(np.broadcast_to(a["L0_ffn_router_b"][None, :], (128, 8)))
    arr["ew"] = np.ascontiguousarray(a["L0_ffn_expert_w"].transpose(1, 0, 2))
    arr["eb"] = a["L0_ffn_expert_b"]
    arr["al"] = np.ascontiguousarray(a["L1_conv_alphas"].T)
    arr["gw"] = np.ascontiguousarray(a["L1_ffn_gate_w"].T)
    arr["gb"] = a["L1_ffn_gate_b"].reshape(64, 1)
    arr["w1"] = a["L1_ffn_weight1"]
    arr["w2"] = a["L1_ffn_weight2"]
    arr |= constants()
    nc = _bacc.Bacc("TRN2", target_bir_lowering=False, num_devices=1)
    ins, arrays = {}, {}
    for n, v in arr.items():
        arrays["in_" + n] = v
        ins[n] = nc.dram_tensor("in_" + n, v.shape, mybir.dt.from_np(v.dtype), kind="ExternalInput").ap()
    out = nc.dram_tensor("out", (B * 128, H * W), F32, kind="ExternalOutput").ap()

    def dbg(name, shape):
        return nc.dram_tensor(name, shape, F32, kind="Internal").ap()

    program(nc, ins, out, dbg)
    r = _run(nc, [arrays], core_ids=[0])
    return r.results[0]["out"].reshape(B, 128, H, W)
```

```python
from contextlib import ExitStack

import numpy as np
import concourse.bass as bass
from concourse import mybir

F32 = mybir.dt.float32
BF16 = mybir.dt.bfloat16
I32 = mybir.dt.int32
U32 = mybir.dt.uint32
ALU = mybir.AluOpType
ACT = mybir.ActivationFunctionType
AX = mybir.AxisListType

B, C, H, W = 4, 128, 128, 128
NG = B * H // 4
GI = H // 4
PR, PC = 134, 136
PIX = PR * PC
NPART = 120
E0, E1, HID = 8, 64, 512


class Engine:

    def __init__(self, name, sem):
        self.name, self.sem, self.n, self.todo, self.seen = name, sem, 0, [], {}

    def wait(self, *tokens):
        for t in tokens:
            if t is None:
                continue
            s, v = t
            if self.seen.get(s.num, 0) < v:
                self.seen[s.num] = v
                self.todo.append(lambda e, s=s, v=v: e.wait_ge(s, v))

    def op(self, f, *waits, sig=True):
        self.wait(*waits)
        if not sig:
            self.todo.append(f)
            return None
        self.n += 1
        self.todo.append(lambda e, s=self.sem: f(e).then_inc(s, 1))
        return (self.sem, self.n)

    def run(self, e):
        for f in self.todo:
            f(e)
        self.todo = []


class Queue:

    def __init__(self, engine, sems):
        self.engine, self.sems, self.k = engine, sems, 0

    def dma(self, f, *waits):
        i, r = self.k % len(self.sems), self.k // len(self.sems)
        s = self.sems[i]
        self.engine.wait(*waits)
        if r:
            self.engine.wait((s, 16 * r))
        self.engine.todo.append(lambda e: f(e).then_inc(s, 16))
        self.k += 1
        return (s, 16 * (r + 1))

    def all(self):
        n = len(self.sems)
        return [(self.sems[i], 16 * ((self.k - i + n - 1) // n)) for i in range(min(n, self.k))]


class Phase:
    def __init__(self, nc, ctx, tag, queues):
        sem = lambda n: ctx.enter_context(nc.semaphore(f"{tag}_{n}"))
        self.pe, self.act, self.dve, self.pool, self.sp = (
            Engine(n, sem(n)) for n in ("pe", "act", "dve", "pool", "sp"))
        self.q = {}
        for name, (eng, n) in queues.items():
            self.q[name] = Queue({"sp": self.sp, "act": self.act, "pool": self.pool}[eng],
                                 [sem(f"{name}{i}") for i in range(n)])

    def emit(self, nc):
        for q in self.q.values():
            self.sp.wait(*q.all())
        with nc.Block() as block:
            @block.tensor
            def _(e):
                self.pe.run(e)

            @block.scalar
            def _(e):
                self.act.run(e)

            @block.vector
            def _(e):
                self.dve.run(e)

            @block.gpsimd
            def _(e):
                self.pool.run(e)

            @block.sync
            def _(e):
                self.sp.run(e)


def token_stats(p, src, stats, mv, rstd, eps, src_tok, mhalf, after=(), n_act=0):
    t = []
    for i in range(4):
        t.append(p.dve.op(lambda e, i=i: e.bn_stats(stats[:, i, :], src[:, i, :]), src_tok, *(after or ())))
    a = None
    for i in range(4):
        a = p.dve.op(lambda e, i=i: e.bn_aggr(mv[:, i, :], stats[:, i, :]), t[i])
    b = p.pool.op(lambda e: e.tensor_scalar(rstd[:, 0:4], mv[:, :, 1], float(eps), None, ALU.add), a)
    c = p.pool.op(lambda e: e.tensor_tensor(rstd[:, 4:8], rstd[:, 0:4], mhalf[:, 0:4], ALU.pow), b)
    g = None
    if n_act:
        g = p.pool.op(lambda e: e.tensor_tensor(rstd[:, 0:4], rstd[:, 4:8], mv[:, :, 0], ALU.mult), c)
        g = p.pool.op(lambda e: e.tensor_scalar(rstd[:, 0:4], rstd[:, 0:4], -1.0, 0.0, ALU.mult, ALU.add), g)
    return c, g


def token_norm(p, src, mv, rstd, out, ready, after=(), n_act=0):
    c, g = ready
    d, f = None, None
    for i in range(4 - n_act, 4):
        f = p.act.op(lambda e, i=i: e.activation(out[:, i, :], src[:, i, :], ACT.Identity,
                                                 bias=rstd[:, i:i + 1], scale=rstd[:, 4 + i:5 + i]),
                     g, *after)
    for i in range(4 - n_act):
        d = p.dve.op(lambda e, i=i: e.tensor_scalar(out[:, i, :], src[:, i, :], mv[:, i, 0:1],
                                                    rstd[:, 4 + i:5 + i], ALU.subtract, ALU.mult),
                     c, *after)
    return [x for x in (d, f) if x]


def layernorm_tokens(p, src, stats, mv, rstd, out, eps, src_tok, mhalf, after, wait_mv=None, n_act=0):
    ready = token_stats(p, src, stats, mv, rstd, eps, src_tok, mhalf, wait_mv, n_act)
    return token_norm(p, src, mv, rstd, out, ready, after, n_act)


def setup_phase(nc, ctx, p, ins, k, xtp):
    q = p.q["c"]
    z = p.dve.op(lambda e: e.memset(k["zero"][:, :], 0.0))
    p.dve.op(lambda e: e.memset(k["mhalf"][:, :], -0.5))
    m = p.dve.op(lambda e: e.memset(k["ones"][:, :], 1.0))
    q.dma(lambda e: e.dma_start(k["ident"][:, :], ins["ident"][:, :]))
    q.dma(lambda e: e.dma_start(k["wof"][:, :, :], ins["wof"][:, :, :]))
    q.dma(lambda e: e.dma_start(k["selz"][:, :], ins["selz"][:, :]))
    q.dma(lambda e: e.dma_start(k["wcv"][:, :, :], ins["wcv"][:, :, :]))
    s = q.dma(lambda e: e.dma_start(k["self"][:, :, :], ins["sel"][:, :, :]))
    c = q.dma(lambda e: e.dma_start(k["cst"][96:98, :], ins["cst"][:, :]))
    a = p.dve.op(lambda e: e.tensor_copy(k["sel"][:, :, :], k["self"][:, :, :]), s)
    for i in range(NPR):
        p.dve.op(lambda e, i=i: e.tensor_copy(k["P"][96:98, i * 512:(i + 1) * 512], k["cst"][96:98, :]), c)
    for b in range(B):
        v = xtp[b * PIX:(b + 1) * PIX, :]
        for r0 in (0, 131):
            f = v[r0 * PC:(r0 + 3) * PC, :].rearrange("(p r) c -> p (r c)", p=102)
            q.dma(lambda e, f=f: e.dma_start(f, k["zero"][0:102, 0:512]), z)
        g = v[3 * PC:131 * PC, :].rearrange("(r w) c -> r (w c)", w=PC)
        q.dma(lambda e, g=g: e.dma_start(g[:, 0:384], k["zero"][:, 0:384]), z)
        q.dma(lambda e, g=g: e.dma_start(g[:, 131 * 128:136 * 128], k["zero"][:, 0:640]), z)


NPR = 4
NX = 9
NXN = 3
NZ = 16
NSR = 12
NPT = 5
NA_B = 3
POOL_E = (3, 7)
ORDER = ("lp", "o", "b", "n")
SHARES = (1.2, 0, 1.1, 0, 1.1, 0)
SHARE_MAX = 2.0
NA_A = 2
EV_ACT = [(1, 1, 1), (1, 0, 1), (1, 1, 1), (1, 0, 1)]
REACH = 2.0


def pieces(r0, n, ring):
    out = []
    while n:
        s = r0 % ring
        m = min(n, ring - s)
        out.append((r0, s, m))
        r0, n = r0 + m, n - m
    return out


def phase_a(nc, ctx, p, ins, k, xtp, offd, x1d):
    S = lambda shape, dt=F32, name=None: ctx.enter_context(nc.sbuf_tensor(name, shape, dt))
    xin = S([128, NX, 512], name="a_xin")
    tok = S([128, 2, 4, 128], name="a_tok")
    tn = S([128, 3, 4, 128], name="a_tn")
    st = S([128, 2, 4, 6], name="a_st")
    mv = S([128, 2, 4, 2], name="a_mv")
    rs = S([128, 2, 8], name="a_rs")
    xn = S([128, NXN, 4, 130], name="a_xn")
    zs = S([96, NZ, 128], name="a_zs")
    off = S([96, 2, 512], name="a_off")
    r1 = S([96, 2, 512], name="a_r1")
    r2 = S([96, 2, 512], name="a_r2")
    t1 = S([96, 2, 512], BF16, name="a_t1")
    win = S([NPART, NPT, 8, 128], name="a_win")
    ab = S([NPART, 3, 2, 384], name="a_ab")
    sw = S([NPART, 2, 9, 128], name="a_sw")
    sr = S([128, NSR, 9, 128], name="a_sr")
    xo = S([128, 2, 512], name="a_xo")
    PB = [ctx.enter_context(nc.psum_tensor(f"a_p{i}", [128, 512], F32)) for i in range(2)]
    PW = ctx.enter_context(nc.psum_tensor("a_pw", [128, 2, 512], F32))
    PB += [None, None] + [ctx.enter_context(nc.psum_tensor(f"a_p{i}", [128, 512], F32)) for i in range(4, 8)]
    Pt = k["P"]
    pe, act, dve, pool = p.pe, p.act, p.dve, p.pool
    ident = k["ident"]

    dve.op(lambda e: e.memset(xn[:, :, :, 0:1], 0.0))
    zb = dve.op(lambda e: e.memset(xn[:, :, :, 129:130], 0.0))
    tl, tt, tst, tcv = {}, {}, {}, {}
    bank = {"k": 0, "free": [None, None]}
    tns = {}
    toks, ready = {}, {}
    xnw = {}
    xnr = {}
    offw, pw, pr = {}, {}, {}
    offst, offr = {}, {}
    cz, zw, szr = {}, {}, {}
    splits = []
    stores = []

    def take():
        i = bank["k"] % 2
        bank["k"] += 1
        return i, PB[i], bank["free"][i]

    def ln(G):
        b, q = divmod(G, GI)
        i, T, fr = take()
        v = T[:, :].rearrange("p (r c) -> p r c", r=4)
        for r in range(4):
            t = pe.op(lambda e, r=r: e.transpose(v[:, r, :], xin[:, G % NX, r * 128:(r + 1) * 128],
                                                 ident[:, :]), tl[G], fr, sig=(r == 3))
        u = act.op(lambda e: e.copy(tok[:, G % 2, :, :], v), t, *toks.get(G - 2, ()))
        bank["free"][i] = u
        ready[G] = token_stats(p, tok[:, G % 2], st[:, G % 2], mv[:, G % 2], rs[:, G % 2], 1e-6, u,
                               k["mhalf"], toks.get(G - 2), NA_A)

    def norm(G):
        b, q = divmod(G, GI)
        toks[G] = token_norm(p, tok[:, G % 2], mv[:, G % 2], rs[:, G % 2], tn[:, G % 3], ready[G],
                             (tns.get(G - 3), tt.get(G - 3)), NA_A)
        dst = xtp[b * PIX + (4 * q + 3) * PC:b * PIX + (4 * q + 7) * PC, :].rearrange(
            "(r w) c -> w r c", w=PC)[3:131]

        def store():
            tns[G] = tst[G] = p.q["st"].dma(lambda e: e.dma_start(dst, tn[:, G % 3, :, :]), *toks[G])
        stores.append([2, store])

    def back(G):
        b, q = divmod(G, GI)
        i, T, fr = take()
        for r in range(4):
            t = pe.op(lambda e, r=r: e.transpose(T[:, r * 128:(r + 1) * 128], tn[:, G % 3, r, :],
                                                 ident[:, :]), *toks[G], fr, sig=(r == 3))
        tt[G] = t
        u = act.op(lambda e: e.copy(xn[:, G % NXN, :, 1:129], T[:, :].rearrange("p (r c) -> p r c", r=4)),
                   t, tcv.get(G - NXN), zb)
        bank["free"][i] = u
        xnw[G] = u

    def parts(G):
        b, q = divmod(G, GI)
        i, T, fr = take()
        for kx in range(3):
            t = pe.op(lambda e, kx=kx: e.matmul(
                T[0:96, :].rearrange("p (r c) -> p r c", r=4), k["wof"][:, kx, :],
                xn[:, G % NXN, :, kx:kx + 128], start=(kx == 0), stop=(kx == 2)), fr, xnw[G], sig=(kx == 2))
            if kx < 2:
                yield 0.86
        tcv[G] = t
        v = T[0:96, :].rearrange("p (r c) -> p r c", r=4)
        R = b * 132
        for ky in range(3):
            y0, y1 = max(4 * q + 1 - ky, 0), min(4 * q + 5 - ky, H)
            P3 = slice(32 * ky, 32 * ky + 32)
            for r0, s, m in pieces(R + y0, y1 - y0, NZ):
                o = r0 - R + ky - 1 - 4 * q
                u = act.op(lambda e, P3=P3, s=s, m=m, o=o: e.copy(zs[P3, s:s + m, :], v[P3, o:o + m, :]),
                           t, szr.get(G - 2))
        zw[G] = [u]
        bank["free"][i] = u
        if q == 0:
            zw[G].append(dve.op(lambda e: e.memset(zs[0:32, R % NZ, :], 0.0), szr.get(G - 2)))
        if q == GI - 1:
            zw[G].append(dve.op(lambda e: e.memset(zs[64:96, (R + H - 1) % NZ, :], 0.0), szr.get(G - 2)))
        yield 0.86

    def offsets(G):
        b, q = divmod(G, GI)
        i, T, fr = take()
        s = (b * 132 + 4 * q) % NZ
        need = zw[G] + (zw[G + 1] if q < GI - 1 else []) + (zw[G - 1] if q else [])
        t = pe.op(lambda e: e.matmul(T[0:96, :], k["selz"][:, :], zs[:, s:s + 4, :].rearrange(
            "p r c -> p (r c)"), start=True, stop=True), fr, *need)
        szr[G] = t
        w = G % 2
        pp = Pt[0:96, (G % NPR) * 512:(G % NPR + 1) * 512]
        o = act.op(lambda e: e.copy(off[:, w, :], T[0:96, :]), t, offst.get(G - 2), cz.get(G - 2), offr.get(G - 2))
        bank["free"][i] = o
        rows = b * H * W + 4 * q * W

        def store():
            offst[G] = p.q["st"].dma(lambda e: e.dma_start(offd[:, rows:rows + 512], off[0:18, w, :]), o)
        stores.append([2, store])
        h = dve.op(lambda e: e.tensor_copy(pp, off[:, w, :]), o, pr.get(G - NPR))
        a = pool.op(lambda e: e.tensor_tensor(r1[:, w, :], off[:, w, :], pp, ALU.subtract), h, cz.get(G - 2), pw.get(G - 2))
        m1 = pool.op(lambda e: e.tensor_copy(t1[:, w, :], r1[:, w, :]), a)
        c = pool.op(lambda e: e.tensor_tensor(r2[:, w, :], r1[:, w, :], t1[:, w, :], ALU.subtract), m1)
        cz[G] = c

        def rest():
            dve.op(lambda e: e.tensor_copy(Pt[32:64, (G % NPR) * 512:(G % NPR + 1) * 512], r1[32:64, w, :]), a)
            pw[G] = dve.op(lambda e: e.tensor_copy(Pt[64:96, (G % NPR) * 512:(G % NPR + 1) * 512],
                                                   r2[64:96, w, :]), c)
        splits.append([1, rest])

        def reach(dst, alu):
            offr[G] = dve.op(lambda e: e.tensor_reduce(dst, off[:, w, :], AX.X, alu), o)
        splits.append([2, lambda: reach(k["fm"][:, G:G + 1], ALU.max)])
        splits.append([2, lambda: reach(k["fm"][:, NG + G:NG + G + 1], ALU.min)])
        yield 0.86

    winw, winr = {}, {}
    nwin = [0]
    ay_free, ax_free = [None], [None]
    nch = [0]
    chunk_s = {}
    srw, srr = {}, {}
    swr = {}
    smp_free = [None, None, None]
    TB = {0: (0, 3), 1: (3, 6), 2: (6, 8)}

    def kys(c):
        return [ky for ky in range(3) if 0 <= c + 1 - ky < H]

    def load_window(b, c):
        n = nwin[0]
        nwin[0] += 1
        dep = [tst[g] for g in range(b * GI + max(0, (c - 2) // 4), b * GI + min(GI - 1, (c + 2) // 4) + 1)]
        last = []
        for j in range(5):
            r = c + j - 2 + 3
            a = b * PIX + r * PC
            src = bass.AP(xtp.tensor, a * 128, [[128, 24], [16 * 128, 8], [1, 128]])
            last.append(p.q["w"].dma(lambda e, j=j, src=src: e.dma_start(
                win[24 * j:24 * j + 24, n % NPT, :, :], src), *dep, winr.get(n - NPT)))
        winw[(b, c)] = (n, last)

    ax_bufs = {}

    def expand(b, c, ky):
        y = c + 1 - ky
        G = b * GI + y // 4
        col = (G % NPR) * 512 + (y % 4) * 128
        m = nch[0]
        nch[0] += 1
        for half in range(2):
            for kx in range(3):
                tx = pe.op(lambda e, kx=kx, half=half: e.matmul(
                    PW[0:NPART, half, kx * 128:(kx + 1) * 128], k["sel"][0:98, 9 * half + 3 * ky + kx, :],
                    Pt[0:98, col:col + 128], start=True, stop=True), pw[G], ay_free[0],
                    sig=(half == 1 and kx == 2))
        pr[G] = tx
        i = m % 3
        a = act.op(lambda e: e.activation(ab[:, i, :, :], PW[0:NPART, :, 0:384], ACT.Abs), tx,
                   chunk_s.get(m - 3))
        ay_free[0] = a
        return m, ky, a

    def clip(m, a):
        i = m % 3
        return dve.op(lambda e: e.tensor_scalar(ab[:, i, :, :], ab[:, i, :, :], 1.0, 1.0, ALU.min,
                                                ALU.subtract), a)

    def weigh(n, m, ky, v):
        i = m % 3
        chunk_s[m] = dve.op(lambda e: e.tensor_tensor(
            sw[:, n % 2, 3 * ky:3 * ky + 3, :].rearrange("p a b -> p (a b)"), ab[:, i, 0, :],
            ab[:, i, 1, :], ALU.mult), v, swr.get(n - 2))
        return chunk_s[m]

    def sample(b, c, stok, bk):
        n, wt = winw[(b, c)]
        ks = kys(c)
        t0, t1_ = 3 * ks[0], 3 * ks[-1] + 3
        slot = (b * 132 + c) % NSR
        g0, g1 = TB[bk]
        v = PB[4 + bk][:, 0:9 * (g1 - g0) * 16].rearrange("p (t x) -> p t x", t=9)
        for g in range(g0, g1):
            t = pe.op(lambda e, g=g: e.matmul(
                v[:, t0:t1_, (g - g0) * 16:(g - g0 + 1) * 16], win[:, n % NPT, g, :],
                sw[:, n % 2, t0:t1_, 16 * g:16 * g + 16], start=True, stop=True),
                *wt, *stok, smp_free[bk], sig=(g == g1 - 1))
        o = sr[:, slot, t0:t1_, g0 * 16:g1 * 16]
        if EV_ACT[c % 4][bk]:
            x = act.op(lambda e: e.activation(o, v[:, t0:t1_, :], ACT.Copy), t, srr.get(slot))
        else:
            x = dve.op(lambda e: e.tensor_copy(o, v[:, t0:t1_, :]), t, srr.get(slot))
        smp_free[bk] = x
        srw.setdefault((b, c), []).append(x)
        if bk == 2:
            winr[n] = t
            swr[n] = t

    xow, oc_free = {}, [None]
    xl = {}

    def outconv(G):
        b, q = divmod(G, GI)
        todo = []
        for ky in (1, 0, 2):
            for r0, s, m in pieces(b * 132 + 4 * q + ky - 1, 4, NSR):
                o0 = r0 - (b * 132 + 4 * q + ky - 1)
                for kx in range(3):
                    todo.append((3 * ky + kx, s, m, o0))
        need = [t for c in range(4 * q - 1, 4 * q + 5) for t in srw[(b, c)]]
        for n, (tap, s, m, o0) in enumerate(todo):
            if n:
                yield 0.22 * todo[n - 1][2]
            t = pe.op(lambda e, tap=tap, s=s, m=m, o0=o0, n=n: e.matmul(
                PB[7][:, o0 * 128:(o0 + m) * 128].rearrange("p (r c) -> p r c", r=m),
                k["wcv"][:, tap, :], sr[:, s:s + m, tap, :],
                start=(n == 0), stop=(n == len(todo) - 1), skip_group_check=True),
                oc_free[0], *need, sig=(n == len(todo) - 1))
        for c in range(4 * q - 1, 4 * q + 5):
            srr[(b * 132 + c) % NSR] = t
        u = dve.op(lambda e: e.tensor_tensor(xo[:, G % 2, :], PB[7][:, :], xin[:, G % NX, :], ALU.add),
                   t, xow.get(G - 2))
        oc_free[0] = u
        xl[G] = u

        def store():
            xow[G] = p.q["st"].dma(lambda e: e.dma_start(
                x1d[b * 128:(b + 1) * 128, 4 * q * W:4 * q * W + 512], xo[:, G % 2, :]), u)
        stores.append([2, store])
        while late and (late[0] - NX) in xl:
            load(late.pop(0))
        yield 0.22 * todo[-1][2]

    def load(G):
        b, q = divmod(G, GI)
        tl[G] = p.q["ld"].dma(lambda e: e.dma_start(
            xin[:, G % NX, :], ins["x"][b * 128:(b + 1) * 128, 4 * q * W:4 * q * W + 512]), xl.get(G - NX))

    centres = [(b, c) for b in range(B) for c in range(-1, H + 1)]
    rank = {bc: i for i, bc in enumerate(centres)}
    late = []
    jobs = []
    stok = {}
    state = {"done": 0, "loaded": 0, "credit": 0.0}

    def flush():
        for x in stores:
            x[0] -= 1
        while stores and stores[0][0] < 0:
            stores.pop(0)[1]()
        for x in splits:
            x[0] -= 1
        while splits and splits[0][0] < 0:
            splits.pop(0)[1]()

    def piece():
        weight = next(jobs[0], None)
        if weight is None:
            jobs.pop(0)
        return weight or 0.0

    def weave(credit):
        state["credit"] = min(state["credit"] + credit, SHARE_MAX)
        while jobs and state["credit"] > 0:
            state["credit"] -= piece()

    def until(ready):
        while not ready():
            if jobs:
                piece()
            else:
                splits.pop(0)[1]()

    def centre_step(idx):
        bc = centres[idx] if idx < len(centres) else None
        before = centres[idx - 1] if idx else None
        ks = kys(bc[1]) if bc else []
        n = winw[bc][0] if bc else None
        clipped, stk = [], []
        for ky in ks:
            g = bc[0] * GI + (bc[1] + 1 - ky) // 4
            until(lambda: g in pw)
        if before:
            old = before[0] * 132 + before[1] - NSR
            ob, oc = divmod(old + 1, 132)
            og = ob * GI + min((oc - 1 + 1) // 4, GI - 1)
            if ob >= 0 and oc - 1 <= H:
                until(lambda: og in xl)
        flush()
        for j in range(3):
            if j < len(ks):
                m, ky, a = expand(*bc, ks[j])
                clipped.append((m, ky, clip(m, a)))
            weave(SHARES[2 * j])
            if before:
                sample(*before, stok[before], j)
            if j and j - 1 < len(ks):
                m, ky, v = clipped[j - 1]
                stk.append(weigh(n, m, ky, v))
            weave(SHARES[2 * j + 1])
        if len(ks) == 3:
            m, ky, v = clipped[2]
            stk.append(weigh(n, m, ky, v))
        if bc:
            stok[bc] = stk
        if before and before[1] >= 4 and before[1] % 4 == 0:
            jobs.append(outconv(before[0] * GI + before[1] // 4 - 1))

    def advance(upto, between):
        while state["done"] < upto:
            i = state["done"]
            if between:
                between.pop(0)()
            while state["loaded"] < min(i + 4, len(centres)):
                load_window(*centres[state["loaded"]])
                state["loaded"] += 1
            centre_step(i)
            state["done"] += 1

    def finish(job):
        for _ in job:
            pass

    for G in range(NX - 1):
        load(G)
    for G in range(NG + 4):
        steps = {"p": lambda G=G: jobs.append(parts(G - 2)), "o": lambda G=G: jobs.append(offsets(G - 3)),
                 "l": lambda G=G: ln(G), "b": lambda G=G: back(G - 1), "n": lambda G=G: norm(G)}
        live = {"p": 0 <= G - 2 < NG, "o": 0 <= G - 3 < NG, "l": G < NG, "b": 0 <= G - 1 < NG, "n": G < NG}
        between = [lambda w=w: [steps[x]() for x in w if live[x]] for w in ORDER]
        between = [(lambda w=w, steps=steps, live=live: [steps[x]() for x in w if live[x]]) for w in ORDER]
        if G >= 4:
            b, q = divmod(G - 4, GI)
            advance(rank[(b, H) if q == GI - 1 else (b, 4 * q + 1)] + 1, between)
        for f in between:
            f()
        if G < 4:
            while jobs:
                finish(jobs.pop(0))
            for _ in range(3):
                flush()
        n = G + NX - 1
        if NX - 1 <= n < NG:
            late.append(n)
        while late and (late[0] - NX < 0 or (late[0] - NX) in xl):
            load(late.pop(0))
    centre_step(len(centres))
    while jobs:
        finish(jobs.pop(0))
    for _ in range(4):
        flush()


def far_flag(nc, ctx, p, k):
    S = lambda name, shape, dt=F32: ctx.enter_context(nc.sbuf_tensor(name, shape, dt))
    r = S("g_r", [96, 3])
    T = ctx.enter_context(nc.psum_tensor("g_t", [1, 512], F32))
    d = p.dve
    a = d.op(lambda e: e.tensor_reduce(r[:, 0:1], k["fm"][:, 0:NG], AX.X, ALU.max))
    b = d.op(lambda e: e.tensor_reduce(r[:, 1:2], k["fm"][:, NG:2 * NG], AX.X, ALU.min))
    b = d.op(lambda e: e.tensor_scalar(r[:, 1:2], r[:, 1:2], -1.0, None, ALU.mult), b)
    c = d.op(lambda e: e.tensor_tensor(r[:, 2:3], r[:, 0:1], r[:, 1:2], ALU.max), a, b)
    t = p.pe.op(lambda e: e.transpose(T[0:1, 0:96], r[:, 2:3], k["ident"][0:96, 0:96]), c)
    g = d.op(lambda e: e.tensor_reduce(k["gm"][:, 0:1], T[0:1, 0:96], AX.X, ALU.max), t)
    g = d.op(lambda e: e.tensor_scalar(k["gm"][:, 0:1], k["gm"][:, 0:1], REACH, None, ALU.is_gt), g)
    t = d.op(lambda e: e.tensor_copy(k["flag"][:, :], k["gm"][:, 0:1]), g)
    for eng in (p.pe, p.act, p.dve, p.pool, p.sp):
        eng.wait(t)


def far_rows(nc, ins, k, xtp, offd, x1d):
    with ExitStack() as ctx:
        S = lambda name, shape, dt=F32: ctx.enter_context(nc.sbuf_tensor(name, shape, dt))
        orow = S("f_or", [18, 128]); of = S("f_of", [128, 9, 2]); ri = S("f_ri", [128, 9, 2], I32)
        rf = S("f_rf", [128, 9, 2]); gt = S("f_gt", [128, 9, 2]); fl = S("f_fl", [128, 9, 2])
        fr = S("f_fr", [128, 2, 9, 2]); ps = S("f_ps", [128, 9, 2]); xf = S("f_xf", [128, 4, 9])
        ii = S("f_ii", [128, 4, 9], I32); wt = S("f_wt", [128, 4, 9]); ct = S("f_ct", [128, 9, 2])
        ctx0 = S("f_c0", [128, 9, 2]); bb = S("f_bb", [128, 1]); xr = S("f_xr", [128, 128])
        g = S("f_g", [128, 9, 4, 128]); sT = S("f_sT", [128, 9, 128]); xo = S("f_xo", [128, 128])
        P0 = ctx.enter_context(nc.psum_tensor("f_p0", [128, 512], F32))
        PT = [ctx.enter_context(nc.psum_tensor(f"f_pt{i}", [128, 512], F32)) for i in range(3)]
        PO = ctx.enter_context(nc.psum_tensor("f_po", [128, 512], F32))
        s0 = ctx.enter_context(nc.semaphore("f_init"))
        with nc.Block() as block:
            @block.sync
            def _(e):
                e.dma_start(ctx0[:, :, :], ins["far"][:, :, :]).then_inc(s0, 16)
                e.wait_ge(s0, 16)

            @block.vector
            def _(e):
                e.memset(bb[:, :], float(3 * PC + 3))
                e.wait_ge(s0, 16)

            @block.tensor
            def _(e):
                e.wait_ge(s0, 16)

            @block.scalar
            def _(e):
                e.wait_ge(s0, 16)

            @block.gpsimd
            def _(e):
                e.wait_ge(s0, 16)
        names = ("pe", "act", "dve", "pool", "sp", "in0", "in1", "st0", "g0", "g1", "g2", "g3")
        sems = [ctx.enter_context(nc.semaphore("f_" + n)) for n in names]

        def row(b, y):
            sm = dict(zip(names, sems))
            p = Phase.__new__(Phase)
            p.pe, p.act, p.dve, p.pool, p.sp = (Engine(n, sm[n]) for n in names[:5])
            p.q = {"i": Queue(p.sp, [sm["in0"], sm["in1"]]), "g": Queue(p.pool, [sm[f"g{i}"] for i in range(4)]),
                   "o": Queue(p.sp, [sm["st0"]])}
            pe, act, dve, pool = p.pe, p.act, p.dve, p.pool
            t0 = p.q["i"].dma(lambda e: e.dma_start(
                orow[:, :], offd[:, bass.ds(b * (H * W) + y * W, W)]))
            t1 = p.q["i"].dma(lambda e: e.dma_start(
                xr[:, :], ins["x"][bass.ds(b * 128, 128), bass.ds(y * W, W)]))
            t = pe.op(lambda e: e.transpose(P0[:, 0:18], orow[:, :], k["ident"][0:18, 0:18]), t0)
            v = dve.op(lambda e: e.tensor_scalar(of[:, :, :].rearrange("p a b -> p (a b)"), P0[:, 0:18],
                                                 -400.0, 400.0, ALU.max, ALU.min), t)
            v = dve.op(lambda e: e.tensor_copy(ri[:, :, :], of[:, :, :]), v)
            v = dve.op(lambda e: e.tensor_copy(rf[:, :, :], ri[:, :, :]), v)
            v = dve.op(lambda e: e.tensor_tensor(gt[:, :, :], rf[:, :, :], of[:, :, :], ALU.is_gt), v)
            v = dve.op(lambda e: e.tensor_tensor(fl[:, :, :], rf[:, :, :], gt[:, :, :], ALU.subtract), v)
            f1 = dve.op(lambda e: e.tensor_tensor(fr[:, 1], of[:, :, :], fl[:, :, :], ALU.subtract), v)
            f0 = dve.op(lambda e: e.tensor_scalar(fr[:, 0], fr[:, 1], -1.0, 1.0, ALU.mult, ALU.add), f1)
            v = dve.op(lambda e: e.tensor_tensor(ps[:, :, :], fl[:, :, :], ct[:, :, :], ALU.add), v)
            c0 = dve.op(lambda e: e.tensor_scalar(ps[:, :, 0:1], ps[:, :, 0:1], -2.0, 129.0, ALU.max,
                                                  ALU.min), v)
            c1 = dve.op(lambda e: e.tensor_scalar(ps[:, :, 1:2], ps[:, :, 1:2], -2.0, 130.0, ALU.max,
                                                  ALU.min), v)
            v = dve.op(lambda e: e.scalar_tensor_tensor(out=xf[:, 0, :], in0=ps[:, :, 0], scalar=float(PC),
                                                        in1=ps[:, :, 1], op0=ALU.mult, op1=ALU.add), c0, c1)
            v = dve.op(lambda e: e.tensor_scalar(xf[:, 0, :], xf[:, 0, :], bb[:, 0:1], None, ALU.add), v)
            for j, o in ((1, 1), (2, PC), (3, PC + 1)):
                z = dve.op(lambda e, j=j, o=o: e.tensor_scalar(xf[:, j, :], xf[:, 0, :], float(o), None,
                                                               ALU.add), v)
            z = dve.op(lambda e: e.tensor_copy(ii[:, :, :], xf[:, :, :]), z)
            for j in range(4):
                wv = dve.op(lambda e, j=j: e.tensor_tensor(wt[:, j, :], fr[:, j // 2, :, 0],
                                                           fr[:, j % 2, :, 1], ALU.mult), f0)
            nx = dve.op(lambda e: e.tensor_scalar(ct[:, :, 0:1], ct[:, :, 0:1], 1.0, None, ALU.add), v)
            for t_ in range(9):
                for j in range(4):
                    p.q["g"].dma(lambda e, t_=t_, j=j: e.indirect_dma_start(
                        out=g[:, t_, j, :], out_offset=None, in_=xtp[:, :],
                        in_offset=bass.IndirectOffsetOnAxis(ap=ii[:, j, t_:t_ + 1], axis=0)), z)
            dve.wait(*p.q["g"].all())
            pool.wait(*p.q["g"].all())
            for t_ in range(9):
                a = dve.op(lambda e, t_=t_: e.tensor_scalar(g[:, t_, 0, :], g[:, t_, 0, :], wt[:, 0, t_:t_ + 1],
                                                            None, ALU.mult), wv)
                for j in range(1, 4):
                    a = dve.op(lambda e, t_=t_, j=j: e.scalar_tensor_tensor(
                        out=g[:, t_, 0, :], in0=g[:, t_, j, :], scalar=wt[:, j, t_:t_ + 1],
                        in1=g[:, t_, 0, :], op0=ALU.mult, op1=ALU.add), a)
            for t_ in range(9):
                t = pe.op(lambda e, t_=t_: e.transpose(PT[t_ // 3][:, (t_ % 3) * 128:(t_ % 3 + 1) * 128],
                                                       g[:, t_, 0, :], k["ident"][:, :]), a)
            for i in range(3):
                u = act.op(lambda e, i=i: e.copy(sT[:, 3 * i:3 * i + 3, :].rearrange("p a b -> p (a b)"),
                                                 PT[i][:, 0:384]), t)
            for t_ in range(9):
                t = pe.op(lambda e, t_=t_: e.matmul(PO[:, 0:128], k["wcv"][:, t_, :], sT[:, t_, :],
                                                    start=(t_ == 0), stop=(t_ == 8)), u)
            o = dve.op(lambda e: e.tensor_tensor(xo[:, :], PO[:, 0:128], xr[:, :], ALU.add), t, t1)
            s = p.q["o"].dma(lambda e: e.dma_start(
                x1d[bass.ds(b * 128, 128), bass.ds(y * W, W)], xo[:, :]), o)
            p.emit(nc)
            with nc.Block() as block:
                @block.gpsimd
                def _(e):
                    e.dma_reset(range(min(s.num for s in sems[-4:]), max(s.num for s in sems[-4:]) + 1))
                    for s in sems:
                        e.sem_clear(s)

        with nc.Fori(0, B) as b:
            with nc.Block() as block:
                @block.vector
                def _(e):
                    e.tensor_copy(ct[:, :, :], ctx0[:, :, :])
            with nc.Fori(0, H) as y:
                row(b, y)
            with nc.Block() as block:
                @block.vector
                def _(e):
                    e.tensor_scalar(bb[:, :], bb[:, :], float(PIX), None, ALU.add)


def phase_bc(nc, ctx, p, ins, k, x1d, x2d, x3d, lgd):
    S = lambda name, shape, dt=F32: ctx.enter_context(nc.sbuf_tensor(name, shape, dt))
    ew = S("b_ew", [128, 8, 128]); rw = S("b_rw", [128, 8]); ebf = S("b_ebf", [24, 3, 128])
    ebb = S("b_ebb", [24, 3, 128], BF16)
    rb = S("b_rb", [128, 8]); al = S("b_al", [128, 128]); gw = S("b_gw", [128, 64]); gb = S("b_gb", [64, 1])
    sef = S("b_sef", [24, 8, 128]); se = S("b_se", [24, 8, 128], BF16); idb = S("b_idb", [128, 128], BF16)
    x1 = S("b_x1", [128, 3, 512])
    tk = S("b_tk", [128, 4, 4, 128]); tn = S("b_tn", [128, 2, 4, 128]); tnT = S("b_tnT", [128, 2, 512])
    st = S("b_st", [128, 2, 4, 6]); mv = S("b_mv", [128, 2, 4, 2]); rs = S("b_rs", [128, 2, 8])
    lg = S("b_lg", [128, 2, 4, 8]); mx = S("b_mx", [128, 2, 4, 8]); m2 = S("b_m2", [128, 2, 4, 8])
    l2 = S("b_l2", [128, 2, 4, 8]); lm = S("b_lm", [128, 2, 4, 8]); ex = S("b_ex", [128, 2, 4, 8])
    mk = S("b_mk", [128, 2, 4, 8]); pm = S("b_pm", [128, 2, 4, 8]); sm = S("b_sm", [128, 2, 8])
    pw = S("b_pw", [128, 2, 4, 8]); q1 = S("b_q1", [128, 2, 4, 8]); q2 = S("b_q2", [128, 2, 4, 8])
    pp = S("b_pp", [128, 2, 4, 24], BF16); pT = S("b_pT", [24, 3, 512], BF16)
    z = S("b_z", [128, 2, 8, 512]); zp = S("b_zp", [128, 2, 512])
    xa = S("b_xa", [128, 3, 4, 128])
    st2 = S("b_st2", [128, 2, 4, 6]); mv2 = S("b_mv2", [128, 2, 4, 2]); rs2 = S("b_rs2", [128, 2, 8])
    tn2 = S("b_tn2", [128, 2, 4, 128])
    xf = S("b_xf", [128, 128, 128])
    x2r = S("c_x2", [128, 3, 4, 128]); x3t = S("c_x3", [128, 3, 4, 128])
    st3 = S("c_st", [128, 2, 4, 6]); mv3 = S("c_mv", [128, 2, 4, 2]); rs3 = S("c_rs", [128, 2, 8])
    tn3 = S("c_tn", [128, 2, 4, 128]); tnT3 = S("c_tnT", [128, 2, 512]); lo = S("c_lo", [64, 2, 512])
    PS = lambda name, shape: ctx.enter_context(nc.psum_tensor(name, shape, F32))
    TB = [PS("b_t0", [128, 512]), PS("b_t1", [128, 512])]
    PB = [PS("b_p0", [128, 512]), PS("b_p1", [128, 512])]
    RB, PT = PS("b_r", [128, 512]), PS("b_pt", [24, 512])
    ZE, ZC = PS("b_ze", [128, 4, 128]), PS("b_zc", [128, 4, 128])
    pe, act, dve, pool = p.pe, p.act, p.dve, p.pool
    ident = k["ident"]

    q = p.q["c"]
    for t, n in ((rw, "rw"), (rb, "rb"), (al, "al"), (gw, "gw"), (gb, "gb"), (sef, "sele")):
        q.dma(lambda e, t=t, n=n: e.dma_start(t[:, :] if len(t.shape) == 2 else t[:, :, :],
                                              ins[n][:, :] if len(t.shape) == 2 else ins[n][:, :, :]))
    for i in range(3):
        q.dma(lambda e, i=i: e.dma_start(ebf[8 * i:8 * i + 8, 0, :], ins["eb"][:, :]))
    q.dma(lambda e: e.dma_start(ew[:, :, :], ins["ew"][:, :, :]))
    consts = q.all()
    pe.wait(*consts)
    dve.wait(*consts)
    act.wait(*consts)
    big = dve.op(lambda e: e.memset(m2[:, :, :, :], 3.0e38))
    dve.op(lambda e: e.tensor_copy(se[:, :, :], sef[:, :, :]))
    cc = dve.op(lambda e: e.tensor_copy(idb[:, :], ident[:, :]))
    for j in range(3):
        cc = dve.op(lambda e, j=j: e.tensor_copy(ebb[:, j, :], ebf[:, j, :]), cc)
        if j < 2:
            cc = dve.op(lambda e, j=j: e.tensor_tensor(ebf[:, j + 1, :], ebf[:, j, :], ebb[:, j, :],
                                                       ALU.subtract), cc)
    pe.wait(cc)

    pool_k = [0]
    free = [None, None]
    pfree = [None, None]
    rfree, ptfree, zefree, zcfree = [None], [None], [None], [None]
    zpr = [None, None]
    npb, nzp = [0], [0]
    T = {}
    g_ = lambda *key: T.get(key)

    def transposes(src, *waits):
        i = pool_k[0] % 2
        pool_k[0] += 1
        D = TB[i]
        for r in range(4):
            t = pe.op(lambda e, r=r: e.transpose(D[:, r * 128:(r + 1) * 128], src(r), ident[:, :]),
                      free[i], *waits, sig=(r == 3))
        return i, D, t

    def rows_of(G):
        b, h = divmod(G, GI)
        n = b * H * W + h * 512
        return lambda d: d[n:n + 512, :].rearrange("(r w) c -> w r c", w=128)

    def load(G):
        b, h = divmod(G, GI)
        T["x1", G] = p.q["ld"].dma(lambda e: e.dma_start(
            x1[:, G % 3, :], x1d[b * 128:(b + 1) * 128, h * 512:h * 512 + 512]), g_("t1", G - 3))

    def tokens(G):
        i, D, t = transposes(lambda r: x1[:, G % 3, r * 128:(r + 1) * 128], T["x1", G])
        T["t1", G] = t
        T["tk", G] = free[i] = act.op(
            lambda e: e.copy(tk[:, G % 4], D[:, :].rearrange("p (r c) -> p r c", r=4)), t,
            g_("x2", G - 4), *(g_("tn", G - 4) or ()))

    def stats1(G):
        T["s1", G] = token_stats(p, tk[:, G % 4], st[:, G % 2], mv[:, G % 2], rs[:, G % 2], 1e-5, T["tk", G],
                                 k["mhalf"], g_("tn", G - 2), NA_B)

    def norm1(G):
        T["tn", G] = token_norm(p, tk[:, G % 4], mv[:, G % 2], rs[:, G % 2], tn[:, G % 2], T["s1", G],
                                (g_("t2", G - 2),), NA_B)

    def channels(G):
        i, D, t = transposes(lambda r: tn[:, G % 2, r, :], *T["tn", G])
        T["t2", G] = t
        T["tT", G] = free[i] = act.op(lambda e: e.copy(tnT[:, G % 2, :], D[:, :]), t, *(g_("z", G - 2) or ()))

    def router(G):
        w = G % 2
        for r in range(4):
            t = pe.op(lambda e, r=r: e.matmul(RB[:, r * 8:r * 8 + 8], tnT[:, w, r * 128:(r + 1) * 128],
                                              rw[:, :], start=True, stop=True), T["tT", G], rfree[0],
                      sig=(r == 3))
        L = dve.op(lambda e: e.tensor_tensor(lg[:, w], RB[:, 0:32].rearrange("p (r e) -> p r e", r=4),
                                             rb[:, None, :].to_broadcast([128, 4, 8]), ALU.add), t,
                   g_("p", G - 2))
        rfree[0] = L
        T["rt", G] = t
        for r in range(4):
            m = dve.op(lambda e, r=r: e.max(mx[:, w, r, :], lg[:, w, r, :]), L)
        lmt = dve.op(lambda e: e.tensor_tensor(lm[:, w], lg[:, w],
                                               mx[:, w, :, 0:1].to_broadcast([128, 4, 8]), ALU.subtract),
                     m, g_("ex", G - 2))
        c = dve.op(lambda e: e.tensor_copy(m2[:, w, :, 0:2], mx[:, w, :, 0:2]), m, big)
        for r in range(4):
            zt = dve.op(lambda e, r=r: e.match_replace(l2[:, w, r, :], m2[:, w, r, :], lg[:, w, r, :],
                                                       -3.0e38), c)
        T["ex", G] = act.op(lambda e: e.activation(ex[:, w], lm[:, w], ACT.Exp), lmt, g_("p", G - 2))
        T["mk", G] = dve.op(lambda e: e.tensor_tensor(mk[:, w], l2[:, w], lg[:, w], ALU.is_lt), zt)

    def weights(G):
        w = G % 2
        t = dve.op(lambda e: e.tensor_tensor(pm[:, w], ex[:, w], mk[:, w], ALU.mult), T["ex", G], T["mk", G])
        s = dve.op(lambda e: e.tensor_reduce(sm[:, w, 0:4], pm[:, w], AX.X, ALU.add), t)
        s = dve.op(lambda e: e.reciprocal(sm[:, w, 4:8], sm[:, w, 0:4]), s)
        s = dve.op(lambda e: e.tensor_tensor(pw[:, w], pm[:, w],
                                             sm[:, w, 4:8, None].to_broadcast([128, 4, 8]), ALU.mult), s)
        s = dve.op(lambda e: e.tensor_copy(pp[:, w, :, 0:8], pw[:, w]), s, g_("ptm", G - 2))
        s = dve.op(lambda e: e.tensor_tensor(q1[:, w], pw[:, w], pp[:, w, :, 0:8], ALU.subtract), s)
        s = dve.op(lambda e: e.tensor_copy(pp[:, w, :, 8:16], q1[:, w]), s)
        s = dve.op(lambda e: e.tensor_tensor(q2[:, w], q1[:, w], pp[:, w, :, 8:16], ALU.subtract), s)
        T["p", G] = dve.op(lambda e: e.tensor_copy(pp[:, w, :, 16:24], q2[:, w]), s)

    def weights_t(G):
        for r in range(4):
            t = pe.op(lambda e, r=r: e.matmul(PT[:, r * 128:(r + 1) * 128], pp[:, G % 2, r, :], idb[:, :],
                                              start=True, stop=True), T["p", G], ptfree[0], sig=(r == 3))
        T["ptm", G] = t
        T["pT", G] = ptfree[0] = act.op(lambda e: e.copy(pT[:, G % 3, :], PT[:, :]), t, g_("ye", G - 3))

    def scale(G, e0):
        w = G % 2
        i = npb[0] % 2
        npb[0] += 1
        t = pe.op(lambda e: e.matmul(PB[i][:, :], se[:, e0, :], pT[:, G % 3, :], start=True, stop=True),
                  T["pT", G], pfree[i])
        if e0 in POOL_E:
            j = nzp[0] % 2
            nzp[0] += 1
            pfree[i] = act.op(lambda e: e.copy(zp[:, j, :], PB[i][:, :]), t, zpr[j])
            zpr[j] = u = pool.op(lambda e: e.tensor_tensor(z[:, w, e0, :], tnT[:, w, :], zp[:, j, :],
                                                           ALU.mult), pfree[i], T["tT", G], g_("ye", G - 2))
        else:
            pfree[i] = u = dve.op(lambda e: e.tensor_tensor(z[:, w, e0, :], tnT[:, w, :], PB[i][:, :],
                                                            ALU.mult), t, T["tT", G], g_("ye", G - 2))
        T.setdefault(("z", G), []).append(u)

    def experts(G, r):
        w = G % 2
        for j in range(3):
            pe.op(lambda e, j=j: e.matmul(ZE[:, r, :], pT[:, G % 3, r * 128:(r + 1) * 128], ebb[:, j, :],
                                          start=(j == 0), stop=False), zefree[0], *T["z", G], sig=False)
        for x in range(8):
            t = pe.op(lambda e, x=x: e.matmul(ZE[:, r, :], z[:, w, x, r * 128:(r + 1) * 128], ew[:, x, :],
                                              start=False, stop=(x == 7)), sig=(x == 7))
        if r == 3:
            T["ye", G] = t

    def stats2(G):
        a3 = xa[:, G % 3]
        T["x2", G] = zefree[0] = dve.op(lambda e: e.tensor_tensor(a3, ZE[:, :, :], tk[:, G % 4], ALU.add),
                                        T["ye", G], g_("x2s", G - 3), *(g_("tn2", G - 3) or ()))
        T["s2", G] = token_stats(p, a3, st2[:, G % 2], mv2[:, G % 2], rs2[:, G % 2], 1e-6, T["x2", G],
                                 k["mhalf"], g_("tn2", G - 2), NA_B)
        T["x2s", G] = p.q["st"].dma(lambda e: e.dma_start(rows_of(G)(x2d), a3), T["x2", G])

    def norm2(G):
        w = G % 2
        T["tn2", G] = token_norm(p, xa[:, G % 3], mv2[:, w], rs2[:, w], tn2[:, w], T["s2", G],
                                 (g_("t4", G - 2),), NA_B)

    def place(G):
        b, h = divmod(G, GI)
        i, D, t = transposes(lambda r: tn2[:, G % 2, r, :], *T["tn2", G])
        T["t4", G] = t
        v = D[:, :].rearrange("p (r c) -> p r c", r=4)
        if b % 2:
            runs = [(0, 4, slice(4 * h, 4 * h + 4))]
        elif h == 0:
            runs = [(0, 1, slice(0, 1)), (1, 4, slice(127, 124, -1))]
        else:
            runs = [(0, 4, slice(128 - 4 * h, 124 - 4 * h, -1))]
        for r0, r1, rows in runs:
            act.op(lambda e, r0=r0, r1=r1, rows=rows: e.copy(xf[:, rows, 0:1], v[:, r0:r1, 0:1]), t,
                   g_("c", G - GI))
            u = act.op(lambda e, r0=r0, r1=r1, rows=rows: e.copy(xf[:, rows, 127:0:-1], v[:, r0:r1, 1:128]))
        free[i] = u
        T["xf", G] = u

    def loadc(G):
        T["x2r", G] = p.q["lc"].dma(lambda e: e.dma_start(x2r[:, G % 3], rows_of(G)(x2d)), T["x2s", G],
                                    g_("x3", G - 3))

    def fourier(G):
        b, h = divmod(G, GI)
        need = T["xf", b * GI + GI - 1]
        for r in range(4):
            y = 4 * h + r
            row = (128 - y) % 128 if b % 2 else y
            t = pe.op(lambda e, r=r, row=row: e.matmul(ZC[:, r, :], xf[:, row, :], al[:, :],
                                                       start=True, stop=True), need, zcfree[0], sig=(r == 3))
        T["c", G] = t

    def stats3(G):
        w = G % 2
        a3 = x3t[:, G % 3]
        T["x3", G] = zcfree[0] = dve.op(lambda e: e.tensor_tensor(a3, ZC[:, :, :], x2r[:, G % 3], ALU.add),
                                        T["c", G], T["x2r", G], g_("x3s", G - 3), *(g_("tn3", G - 3) or ()))
        T["s3", G] = token_stats(p, a3, st3[:, w], mv3[:, w], rs3[:, w], 1e-5, T["x3", G], k["mhalf"],
                                 g_("tn3", G - 2), NA_B)
        T["x3s", G] = p.q["st"].dma(lambda e: e.dma_start(rows_of(G)(x3d), a3), T["x3", G])

    def norm3(G):
        w = G % 2
        T["tn3", G] = token_norm(p, x3t[:, G % 3], mv3[:, w], rs3[:, w], tn3[:, w], T["s3", G],
                                 (g_("t5", G - 2),), NA_B)

    def channels3(G):
        i, D, t = transposes(lambda r: tn3[:, G % 2, r, :], *T["tn3", G])
        T["t5", G] = t
        T["tT3", G] = free[i] = act.op(lambda e: e.copy(tnT3[:, G % 2, :], D[:, :]), t, g_("lgm", G - 2))

    def gate(G):
        b, h = divmod(G, GI)
        w = G % 2
        i = pool_k[0] % 2
        pool_k[0] += 1
        D = TB[i]
        t = pe.op(lambda e: e.matmul(D[0:64, :], gw[:, :], tnT3[:, w, :], start=True, stop=True),
                  free[i], T["tT3", G])
        T["lgm", G] = t
        u = act.op(lambda e: e.activation(lo[:, w, :], D[0:64, :], ACT.Identity, bias=gb[:, 0:1]), t,
                   g_("los", G - 2))
        free[i] = u
        T["los", G] = p.q["st"].dma(lambda e: e.dma_start(
            lgd[b * 64:b * 64 + 64, h * 512:h * 512 + 512], lo[:, w, :]), u)

    LAG = GI + 4
    for G in range(3):
        load(G)
    for s in range(NG + LAG + 3):
        def at(lag, f, *a):
            if 0 <= s - lag < NG:
                f(s - lag, *a)
        at(LAG, fourier)
        at(0, tokens)
        at(3, experts, 0)
        at(2, scale, 0)
        at(2, scale, 1)
        at(1, norm1)
        at(LAG + 1, norm3)
        at(3, experts, 1)
        at(2, scale, 2)
        at(2, scale, 3)
        at(4, norm2)
        at(1, channels)
        at(LAG, stats3)
        at(3, experts, 2)
        at(1, router)
        at(2, scale, 4)
        at(2, scale, 5)
        at(LAG + 1, channels3)
        at(3, experts, 3)
        at(1, weights)
        at(4, place)
        at(2, scale, 6)
        at(2, scale, 7)
        at(0, stats1)
        at(3, stats2)
        at(LAG + 1, gate)
        at(1, weights_t)
        at(-3, load)
        if s + 2 >= LAG and s + 2 - LAG < NG:
            loadc(s + 2 - LAG)


def phase_d(nc, ctx, p, ins, k, x3d, lgd):
    S = lambda name, shape, dt=F32: ctx.enter_context(nc.sbuf_tensor(name, shape, dt))
    NP_, NCH, EC = B // 2, 8, 8
    Lb = S("d_L", [128, H * W])
    w1 = S("d_w1", [128, 3, EC, 512]); w2 = S("d_w2", [128, 2, EC, 4, 128])
    b1r = S("d_b1r", [64, 512]); b2r = S("d_b2r", [128, 128]); base = S("d_base", [128, 2])
    b1t = S("d_b1t", [128, 4, 64])
    v8 = S("d_v8", [128, NP_, 8]); ix = S("d_ix", [128, NP_, 8], U32); nm = S("d_nm", [128, NP_, 1])
    sm = S("d_sm", [128, NP_, 2]); ev = S("d_ev", [128, NP_, 8]); tv = S("d_tv", [128, NP_, 8])
    ixf = S("d_ixf", [128, NP_, 8]); gi = S("d_gi", [128, NP_, 8], I32)
    xg = S("d_xg", [128, NP_, 8, 128]); ln = S("d_ln", [128, 2, 4, 128])
    st = S("d_st", [128, 2, 4, 6]); mv = S("d_mv", [128, 2, 4, 2]); rs = S("d_rs", [128, 2, 8])
    pl = S("d_pl", [128, NP_, 128]); plT = S("d_plT", [128, B, 64])
    hb = S("d_hb", [128, 64, 4, B]); hs = S("d_hs", [128, 64, 4, B])
    oT = S("d_oT", [128, B, 64]); ov = S("d_ov", [128, NP_, 128])
    bi = S("d_bi", [128, NP_, 8, 128]); ib = S("d_ib", [128, 8, 128])
    A = S("d_A", [128, NP_, 8, 128]); eq = S("d_eq", [128, 8, 128])
    PS = lambda name, shape: ctx.enter_context(nc.psum_tensor(name, shape, F32))
    P0, P1 = PS("d_p0", [128, 512]), PS("d_p1", [128, 512])
    HB = PS("d_h", [128, 64, 4, B]) if B == 4 else PS("d_h", [128, 64, 4, B])
    OB = PS("d_o", [128, 512])
    IB = PS("d_i", [128, 2, 512])
    pe, act, dve, pool = p.pe, p.act, p.dve, p.pool
    ident = k["ident"]

    q = p.q["c"]
    tb1 = q.dma(lambda e: e.dma_start(b1r[:, :], ins["w1"][:, 128, :]))
    q.dma(lambda e: e.dma_start(b2r[0:64, :], ins["w2"][:, 512, :]))
    q.dma(lambda e: e.dma_start(b2r[64:128, :], ins["w2"][:, 512, :]))
    q.dma(lambda e: e.dma_start(base[:, :], ins["base"][:, :]))
    consts = q.all()
    tL = {}
    tL[0] = p.q["L"].dma(lambda e: e.dma_start(Lb[:, :], lgd[0:128, :]))
    w1t, w2t, w1r, w2r = {}, {}, {}, {}

    def ldw1(c):
        w1t[c] = p.q["w1"].dma(lambda e: e.dma_start(
            w1[:, c % 3], ins["w1"][c * EC:(c + 1) * EC, 0:128, :].rearrange("e d h -> d e h")), w1r.get(c - 3))

    def ldw2(c):
        w2t[c] = p.q["w2"].dma(lambda e: e.dma_start(
            w2[:, c % 2].rearrange("p e c o -> p e (c o)"),
            ins["w2"][c * EC:(c + 1) * EC, 0:512, :].rearrange("e (p c) o -> p e (c o)", c=4)),
            w2r.get(c - 2))

    for c in range(3):
        ldw1(c)
    for c in range(2):
        ldw2(c)
    for c in range(4):
        t = pe.op(lambda e, c=c: e.transpose(P0[:, c * 64:(c + 1) * 64], b1r[:, c:512:4], ident[0:64, 0:64]),
                  tb1, sig=(c == 3))
    tb = act.op(lambda e: e.copy(b1t[:, :, :], P0[:, 0:256].rearrange("p (c e) -> p c e", c=4)), t)
    p0free = tb
    dve.wait(*consts)
    one = None
    tg, tA = {}, {}
    for a in range(NP_):
        if a:
            tL[a] = p.q["L"].dma(lambda e, a=a: e.dma_start(Lb[:, :], lgd[a * 128:(a + 1) * 128, :]), xe, xm)
        m = dve.op(lambda e, a=a: e.max(v8[:, a, :], Lb[:, :]), tL[a])
        n = dve.op(lambda e, a=a: e.tensor_scalar(nm[:, a, :], v8[:, a, 0:1], -1.0, None, ALU.mult), m)
        xm = dve.op(lambda e, a=a: e.max_index(ix[:, a, :], v8[:, a, :], Lb[:, :]), m)
        xv = act.op(lambda e, a=a: e.activation(ev[:, a, :], v8[:, a, :], ACT.Exp, bias=nm[:, a, :]), n)
        xe = act.op(lambda e, a=a: e.activation(Lb[:, :], Lb[:, :], ACT.Exp, bias=nm[:, a, :],
                                                accum_out=sm[:, a, 0:1]), xm)
        f = dve.op(lambda e, a=a: e.tensor_copy(ixf[:, a, :], ix[:, a, :]), xm)
        f = dve.op(lambda e, a=a: e.tensor_scalar(ixf[:, a, :], ixf[:, a, :], base[:, a:a + 1], None,
                                                  ALU.add), f)
        g = dve.op(lambda e, a=a: e.tensor_copy(gi[:, a, :], ixf[:, a, :]), f)
        r = dve.op(lambda e, a=a: e.reciprocal(sm[:, a, 1:2], sm[:, a, 0:1]), xe)
        tvt = dve.op(lambda e, a=a: e.tensor_scalar(tv[:, a, :], ev[:, a, :], sm[:, a, 1:2], None,
                                                    ALU.mult), r, xv)
        tx = []
        for kk in range(8):
            tx.append(p.q["g"].dma(lambda e, a=a, kk=kk: e.indirect_dma_start(
                out=xg[:, a, kk, :], out_offset=None, in_=x3d[:, :],
                in_offset=bass.IndirectOffsetOnAxis(ap=gi[:, a, kk:kk + 1], axis=0)), g))
        tg[a] = tx
        last, prev = None, None
        for half in range(2):
            last = layernorm_tokens(p, xg[:, a, 4 * half:4 * half + 4, :], st[:, half], mv[:, half],
                                    rs[:, half], ln[:, half], 1e-5, tx[4 * half + 3], k["mhalf"],
                                    (prev,), (prev,))[0]
            if half == 0:
                dve.wait(*tx)
            for j in range(4):
                kk = 4 * half + j
                if kk == 0:
                    prev = dve.op(lambda e, a=a: e.tensor_scalar(pl[:, a, :], ln[:, 0, 0, :], tv[:, a, 0:1],
                                                                 None, ALU.mult), last, tvt)
                else:
                    prev = dve.op(lambda e, a=a, kk=kk: e.scalar_tensor_tensor(
                        out=pl[:, a, :], in0=ln[:, kk // 4, kk % 4, :], scalar=tv[:, a, kk:kk + 1],
                        in1=pl[:, a, :], op0=ALU.mult, op1=ALU.add), last, prev)
        t = pe.op(lambda e, a=a: e.transpose(P0[:, 0:128], pl[:, a, :], ident[:, :]), prev, p0free)
        plt = act.op(lambda e, a=a: e.copy(plT[:, 2 * a:2 * a + 2, :].rearrange("p b e -> p (b e)"),
                                           P0[:, 0:128]), t)
        p0free = plt
        for kk in range(8):
            bt = pool.op(lambda e, a=a, kk=kk: e.tensor_scalar(bi[:, a, kk, :], k["ones"][:, :],
                                                               ixf[:, a, kk:kk + 1], None, ALU.mult), f)
            t = pe.op(lambda e, a=a, kk=kk: e.matmul(IB[:, kk // 4, (kk % 4) * 128:(kk % 4 + 1) * 128],
                                                     bi[:, a, kk, :], ident[:, :], start=True, stop=True),
                      bt, tA.get("ib"), sig=(kk == 7))
        tA["ib"] = act.op(lambda e: e.copy(ib[:, :, :].rearrange("p (a k) c -> p a (k c)", a=2), IB[:, :, :]),
                          t, tA.get("last"))
        prevA, pe_ = None, None
        for kk in range(8):
            dst = A[:, a] if kk == 0 else eq
            pe_ = dve.op(lambda e, a=a, kk=kk, dst=dst: e.tensor_scalar(
                dst[:, :, :], ib[:, :, :], ixf[:, a, kk:kk + 1], tv[:, a, kk:kk + 1], ALU.is_equal, ALU.mult),
                tA["ib"], tvt, prevA)
            if kk:
                prevA = dve.op(lambda e, a=a: e.tensor_tensor(A[:, a], A[:, a], eq[:, :, :], ALU.add), pe_)
            else:
                prevA = pe_
        tA["last"] = prevA
        tA[a] = prevA
    for c in range(NCH):
        for ee in range(EC):
            x = c * EC + ee
            for ch in range(4):
                t = pe.op(lambda e, x=x, ee=ee, ch=ch, c=c: e.matmul(
                    HB[:, x, ch, :], w1[:, c % 3, ee, ch:512:4], plT[:, :, x], start=True, stop=True),
                    w1t[c], plt, sig=(ee == EC - 1 and ch == 3))
        w1r[c] = t
        if c + 3 < NCH:
            ldw1(c + 3)
        if c % 4 == 3:
            e0, e1 = (c - 3) * EC, (c + 1) * EC
            for b in range(B):
                h = dve.op(lambda e, e0=e0, e1=e1, b=b: e.tensor_tensor(
                    hb[:, e0:e1, :, b], HB[:, e0:e1, :, b],
                    b1t[:, :, e0:e1].rearrange("p c e -> p e c"), ALU.add), t, tb)
            hg = act.op(lambda e, e0=e0, e1=e1: e.activation(hs[:, e0:e1].rearrange("p e c b -> p (e c b)"),
                                                             hb[:, e0:e1].rearrange("p e c b -> p (e c b)"),
                                                             ACT.Gelu), h)
            for cc in range(c - 3, c + 1):
                for ee in range(EC):
                    x = cc * EC + ee
                    for ch in range(4):
                        t2 = pe.op(lambda e, x=x, ee=ee, ch=ch, cc=cc: e.matmul(
                            OB[:, x:64 * B:64], w2[:, cc % 2, ee, ch, :], hs[:, x, ch, :],
                            start=(ch == 0), stop=(ch == 3)), w2t[cc], hg, sig=(ee == EC - 1 and ch == 3))
                w2r[cc] = t2
                if cc + 2 < NCH:
                    ldw2(cc + 2)
    ot = act.op(lambda e: e.copy(oT[:, :, :].rearrange("p b e -> p (b e)"), OB[:, 0:64 * B]), t2)
    for a in range(NP_):
        t = pe.op(lambda e, a=a: e.transpose(P0[:, 0:128], oT[:, 2 * a:2 * a + 2, :].rearrange(
            "p b e -> p (b e)"), ident[:, :]), ot, p0free)
        o = dve.op(lambda e, a=a: e.tensor_tensor(ov[:, a, :], P0[:, 0:128], b2r[:, :], ALU.add), t)
        p0free = o
        for kk in range(8):
            D = IB[:, kk // 4, (kk % 4) * 128:(kk % 4 + 1) * 128]
            t = pe.op(lambda e, a=a, kk=kk, D=D: e.matmul(D, A[:, a, kk, :], ov[:, a, :], start=True,
                                                          stop=True), o, tA[a], tA.get("fin"), tA["ib"],
                      sig=(kk == 7))
        u = dve.op(lambda e, a=a: e.tensor_tensor(
            xg[:, a].rearrange("p (h k) c -> p h (k c)", h=2), IB[:, :, :],
            xg[:, a].rearrange("p (h k) c -> p h (k c)", h=2), ALU.add), t, *tg[a])
        tA["fin"] = u
        sc = None
        for kk in range(8):
            sc = p.q["sc"].dma(lambda e, a=a, kk=kk: e.indirect_dma_start(
                out=x3d[:, :], out_offset=bass.IndirectOffsetOnAxis(ap=gi[:, a, kk:kk + 1], axis=0),
                in_=xg[:, a, kk, :], in_offset=None), u, sc)


def phase_e(nc, ctx, p, k, x3d, out):
    S = lambda name, shape, dt=F32: ctx.enter_context(nc.sbuf_tensor(name, shape, dt))
    NB_ = 6
    xt = S("e_x", [128, NB_, 4, 128]); xo = S("e_o", [128, NB_, 512])
    PB = [ctx.enter_context(nc.psum_tensor(f"e_p{i}", [128, 512], F32)) for i in range(4)]
    ld, tr, ev, so = {}, {}, {}, {}

    def load(G):
        src = x3d[G * 512:G * 512 + 512, :].rearrange("(r w) c -> w r c", w=128)
        ld[G] = p.q["ld"].dma(lambda e: e.dma_start(xt[:, G % NB_], src), tr.get(G - NB_))

    for G in range(NB_ - 1):
        load(G)
    for G in range(NG):
        b, h = divmod(G, GI)
        D = PB[G % 4]
        for r in range(4):
            t = p.pe.op(lambda e, r=r, D=D, G=G: e.transpose(D[:, r * 128:(r + 1) * 128], xt[:, G % NB_, r, :],
                                                             k["ident"][:, :]), ld[G], ev.get(G - 4),
                        sig=(r == 3))
        tr[G] = t
        eng = p.act if G % 2 else p.dve
        f = (lambda e, D=D, G=G: e.copy(xo[:, G % NB_, :], D[:, :])) if G % 2 else (
            lambda e, D=D, G=G: e.tensor_copy(xo[:, G % NB_, :], D[:, :]))
        ev[G] = eng.op(f, t, so.get(G - NB_))
        so[G] = p.q["st"].dma(lambda e, b=b, h=h, G=G: e.dma_start(
            out[b * 128:(b + 1) * 128, h * 512:h * 512 + 512], xo[:, G % NB_, :]), ev[G])
        if G + NB_ - 1 < NG:
            load(G + NB_ - 1)


def program(nc, ins, out, dbg):
    with ExitStack() as ctx:
        S = lambda name, shape, dt=F32: ctx.enter_context(nc.sbuf_tensor(name, shape, dt))
        D = lambda name, shape: dbg(name, shape)
        k = {
            "zero": S("zero", [128, 640]), "mhalf": S("mhalf", [128, 8]), "ones": S("ones", [128, 128]),
            "ident": S("ident", [128, 128]), "fm": S("fm", [96, 2 * NG]),
            "gm": S("gm", [1, 1]), "flag": S("flag", [1, 1], I32),
        }
        xtp = D("xtp", [B * PIX, 128])
        offd = D("offd", [18, B * H * W])
        x1d = D("x1d", [B * 128, H * W])
        x2d = D("x2d", [B * H * W, 128])
        x3d = D("x3d", [B * H * W, 128])
        lgd = D("lgd", [B * 64, H * W])
        with ExitStack() as ca:
            SA = lambda name, shape, dt=F32: ca.enter_context(nc.sbuf_tensor(name, shape, dt))
            k |= {"wof": SA("wof", [128, 3, 96]), "selz": SA("selz", [96, 96]), "wcv": SA("wcv", [128, 9, 128]),
                  "sel": SA("sel", [128, 18, 120], BF16), "P": SA("P", [128, NPR * 512], BF16)}
            with ExitStack() as c0:
                k["self"] = c0.enter_context(nc.sbuf_tensor("self", [128, 18, 120], F32))
                k["cst"] = c0.enter_context(nc.sbuf_tensor("cst", [128, 512], F32))
                p0 = Phase(nc, c0, "s", {"c": ("sp", 24)})
                setup_phase(nc, c0, p0, ins, k, xtp)
                p0.emit(nc)
            with ExitStack() as c1:
                p1 = Phase(nc, c1, "a", {"ld": ("sp", 4), "w": ("sp", 20), "st": ("sp", 8)})
                phase_a(nc, c1, p1, ins, k, xtp, offd, x1d)
                p1.emit(nc)
            with ExitStack() as c1:
                pf = Phase(nc, c1, "g", {})
                far_flag(nc, c1, pf, k)
                pf.emit(nc)
            far = nc.values_load(k["flag"][0:1, 0:1], min_val=0, max_val=1)
            with nc.If(far > 0):
                far_rows(nc, ins, k, xtp, offd, x1d)
        with ExitStack() as c2:
            p2 = Phase(nc, c2, "b", {"c": ("sp", 10), "ld": ("sp", 3), "lc": ("sp", 3), "st": ("sp", 6)})
            phase_bc(nc, c2, p2, ins, k, x1d, x2d, x3d, lgd)
            p2.emit(nc)
        with ExitStack() as c3:
            p3 = Phase(nc, c3, "d", {"c": ("sp", 4), "L": ("sp", 1), "w1": ("sp", 3), "w2": ("sp", 2),
                                     "g": ("pool", 8), "sc": ("pool", 8)})
            phase_d(nc, c3, p3, ins, k, x3d, lgd)
            p3.emit(nc)
        with ExitStack() as c4:
            p4 = Phase(nc, c4, "e", {"ld": ("sp", 6), "st": ("act", 6)})
            phase_e(nc, c4, p4, k, x3d, out)
            p4.emit(nc)


def constants():
    ident = np.eye(128, dtype=np.float32)
    sel = np.zeros((128, 18, 120), np.float32)
    m = np.arange(120)
    j, i = m // 24, m % 24
    for t in range(9):
        for part in (0, 32, 64):
            sel[part + 2 * t, t, :] = 1.0
            sel[part + 2 * t + 1, 9 + t, :] = 1.0
        sel[96, t, :] = 2 - j
        sel[96, 9 + t, :] = t % 3 + 2 - i
        sel[97, 9 + t, :] = 1.0
    cst = np.ones((2, 512), np.float32)
    cst[1] = np.arange(512) % 16
    base = (np.arange(128)[:, None] // 64 + 2 * np.arange(2)[None, :]).astype(np.float32) * (H * W)
    far = np.zeros((128, 9, 2), np.float32)
    far[:, :, 0] = np.arange(9)[None, :] // 3 - 1
    far[:, :, 1] = np.arange(9)[None, :] % 3 - 1 + np.arange(128)[:, None]
    sele = np.zeros((24, 8, 128), np.float32)
    for i in range(24):
        sele[i, i % 8, :] = 1.0
    selz = np.tile(np.eye(32, dtype=np.float32), (3, 3))
    return {"selz": selz, "sele": sele, "ident": ident, "sel": sel, "cst": cst, "base": base, "far": far}


OUTN = ["out"]
DBG = ["xtp", "offd", "x1d", "x2d", "x3d", "lgd"]


def kernel(**inputs):
    import concourse.bacc as _bacc
    from concourse.bass_utils import run_bass_kernel_spmd as _run

    a = {n: np.ascontiguousarray(v) for n, v in inputs.items()}
    arr = {"x": a["x"].reshape(B * 128, H * W)}
    wo = np.zeros((128, 3, 3, 32), np.float32)
    wo[:, :, :, 0:18] = a["L0_conv_w_off"].transpose(1, 3, 2, 0)
    wo = wo.reshape(128, 3, 96)
    arr["wof"] = wo
    arr["wcv"] = np.ascontiguousarray(a["L0_conv_w_conv"].reshape(128, 128, 9).transpose(1, 2, 0))
    arr["rw"] = a["L0_ffn_router_w"]
    arr["rb"] = np.ascontiguousarray(np.broadcast_to(a["L0_ffn_router_b"][None, :], (128, 8)))
    arr["ew"] = np.ascontiguousarray(a["L0_ffn_expert_w"].transpose(1, 0, 2))
    arr["eb"] = a["L0_ffn_expert_b"]
    arr["al"] = np.ascontiguousarray(a["L1_conv_alphas"].T)
    arr["gw"] = np.ascontiguousarray(a["L1_ffn_gate_w"].T)
    arr["gb"] = a["L1_ffn_gate_b"].reshape(64, 1)
    arr["w1"] = a["L1_ffn_weight1"]
    arr["w2"] = a["L1_ffn_weight2"]
    arr |= constants()
    nc = _bacc.Bacc("TRN2", target_bir_lowering=False, num_devices=1)
    ins, arrays = {}, {}
    for n, v in arr.items():
        arrays["in_" + n] = v
        ins[n] = nc.dram_tensor("in_" + n, v.shape, mybir.dt.from_np(v.dtype), kind="ExternalInput").ap()
    out = nc.dram_tensor("out", (B * 128, H * W), F32, kind="ExternalOutput").ap()

    def dbg(name, shape):
        return nc.dram_tensor(name, shape, F32, kind="Internal").ap()

    program(nc, ins, out, dbg)
    r = _run(nc, [arrays], core_ids=[0])
    return r.results[0]["out"].reshape(B, 128, H, W)
```

```python
from contextlib import ExitStack

import numpy as np
import concourse.bass as bass
from concourse import mybir

F32 = mybir.dt.float32
BF16 = mybir.dt.bfloat16
I32 = mybir.dt.int32
U32 = mybir.dt.uint32
ALU = mybir.AluOpType
ACT = mybir.ActivationFunctionType
AX = mybir.AxisListType

B, C, H, W = 4, 128, 128, 128
NG = B * H // 4
GI = H // 4
PR, PC = 134, 136
PIX = PR * PC
NPART = 120
E0, E1, HID = 8, 64, 512


class Engine:

    def __init__(self, name, sem):
        self.name, self.sem, self.n, self.todo, self.seen = name, sem, 0, [], {}

    def wait(self, *tokens):
        for t in tokens:
            if t is None:
                continue
            s, v = t
            if self.seen.get(s.num, 0) < v:
                self.seen[s.num] = v
                self.todo.append(lambda e, s=s, v=v: e.wait_ge(s, v))

    def op(self, f, *waits, sig=True):
        self.wait(*waits)
        if not sig:
            self.todo.append(f)
            return None
        self.n += 1
        self.todo.append(lambda e, s=self.sem: f(e).then_inc(s, 1))
        return (self.sem, self.n)

    def run(self, e):
        for f in self.todo:
            f(e)
        self.todo = []


class Queue:

    def __init__(self, engine, sems):
        self.engine, self.sems, self.k = engine, sems, 0

    def dma(self, f, *waits):
        i, r = self.k % len(self.sems), self.k // len(self.sems)
        s = self.sems[i]
        self.engine.wait(*waits)
        if r:
            self.engine.wait((s, 16 * r))
        self.engine.todo.append(lambda e: f(e).then_inc(s, 16))
        self.k += 1
        return (s, 16 * (r + 1))

    def all(self):
        n = len(self.sems)
        return [(self.sems[i], 16 * ((self.k - i + n - 1) // n)) for i in range(min(n, self.k))]


class Phase:
    def __init__(self, nc, ctx, tag, queues):
        sem = lambda n: ctx.enter_context(nc.semaphore(f"{tag}_{n}"))
        self.pe, self.act, self.dve, self.pool, self.sp = (
            Engine(n, sem(n)) for n in ("pe", "act", "dve", "pool", "sp"))
        self.q = {}
        for name, (eng, n) in queues.items():
            self.q[name] = Queue({"sp": self.sp, "act": self.act, "pool": self.pool}[eng],
                                 [sem(f"{name}{i}") for i in range(n)])

    def emit(self, nc):
        for q in self.q.values():
            self.sp.wait(*q.all())
        with nc.Block() as block:
            @block.tensor
            def _(e):
                self.pe.run(e)

            @block.scalar
            def _(e):
                self.act.run(e)

            @block.vector
            def _(e):
                self.dve.run(e)

            @block.gpsimd
            def _(e):
                self.pool.run(e)

            @block.sync
            def _(e):
                self.sp.run(e)


def token_stats(p, src, stats, mv, rstd, eps, src_tok, mhalf, after=(), n_act=0):
    t = []
    for i in range(4):
        t.append(p.dve.op(lambda e, i=i: e.bn_stats(stats[:, i, :], src[:, i, :]), src_tok, *(after or ())))
    a = None
    for i in range(4):
        a = p.dve.op(lambda e, i=i: e.bn_aggr(mv[:, i, :], stats[:, i, :]), t[i])
    b = p.pool.op(lambda e: e.tensor_scalar(rstd[:, 0:4], mv[:, :, 1], float(eps), None, ALU.add), a)
    c = p.pool.op(lambda e: e.tensor_tensor(rstd[:, 4:8], rstd[:, 0:4], mhalf[:, 0:4], ALU.pow), b)
    g = None
    if n_act:
        g = p.pool.op(lambda e: e.tensor_tensor(rstd[:, 0:4], rstd[:, 4:8], mv[:, :, 0], ALU.mult), c)
        g = p.pool.op(lambda e: e.tensor_scalar(rstd[:, 0:4], rstd[:, 0:4], -1.0, 0.0, ALU.mult, ALU.add), g)
    return c, g


def token_norm(p, src, mv, rstd, out, ready, after=(), n_act=0):
    c, g = ready
    d, f = None, None
    for i in range(4 - n_act, 4):
        f = p.act.op(lambda e, i=i: e.activation(out[:, i, :], src[:, i, :], ACT.Identity,
                                                 bias=rstd[:, i:i + 1], scale=rstd[:, 4 + i:5 + i]),
                     g, *after)
    for i in range(4 - n_act):
        d = p.dve.op(lambda e, i=i: e.tensor_scalar(out[:, i, :], src[:, i, :], mv[:, i, 0:1],
                                                    rstd[:, 4 + i:5 + i], ALU.subtract, ALU.mult),
                     c, *after)
    return [x for x in (d, f) if x]


def layernorm_tokens(p, src, stats, mv, rstd, out, eps, src_tok, mhalf, after, wait_mv=None, n_act=0):
    ready = token_stats(p, src, stats, mv, rstd, eps, src_tok, mhalf, wait_mv, n_act)
    return token_norm(p, src, mv, rstd, out, ready, after, n_act)


def setup_phase(nc, ctx, p, ins, k, xtp):
    q = p.q["c"]
    z = p.dve.op(lambda e: e.memset(k["zero"][:, :], 0.0))
    p.dve.op(lambda e: e.memset(k["mhalf"][:, :], -0.5))
    m = p.dve.op(lambda e: e.memset(k["ones"][:, :], 1.0))
    q.dma(lambda e: e.dma_start(k["ident"][:, :], ins["ident"][:, :]))
    q.dma(lambda e: e.dma_start(k["wof"][:, :, :], ins["wof"][:, :, :]))
    q.dma(lambda e: e.dma_start(k["selz"][:, :], ins["selz"][:, :]))
    q.dma(lambda e: e.dma_start(k["wcv"][:, :, :], ins["wcv"][:, :, :]))
    s = q.dma(lambda e: e.dma_start(k["self"][:, :, :], ins["sel"][:, :, :]))
    c = q.dma(lambda e: e.dma_start(k["cst"][96:98, :], ins["cst"][:, :]))
    a = p.dve.op(lambda e: e.tensor_copy(k["sel"][:, :, :], k["self"][:, :, :]), s)
    for i in range(NPR):
        p.dve.op(lambda e, i=i: e.tensor_copy(k["P"][96:98, i * 512:(i + 1) * 512], k["cst"][96:98, :]), c)
    for b in range(B):
        v = xtp[b * PIX:(b + 1) * PIX, :]
        for r0 in (0, 131):
            f = v[r0 * PC:(r0 + 3) * PC, :].rearrange("(p r) c -> p (r c)", p=102)
            q.dma(lambda e, f=f: e.dma_start(f, k["zero"][0:102, 0:512]), z)
        g = v[3 * PC:131 * PC, :].rearrange("(r w) c -> r (w c)", w=PC)
        q.dma(lambda e, g=g: e.dma_start(g[:, 0:384], k["zero"][:, 0:384]), z)
        q.dma(lambda e, g=g: e.dma_start(g[:, 131 * 128:136 * 128], k["zero"][:, 0:640]), z)


NPR = 4
NX = 9
NXN = 3
NZ = 16
NSR = 12
NPT = 5
NA_B = 3
POOL_E = (2, 5, 7)
ORDER = ("lp", "o", "b", "n")
SHARES = (1.2, 0, 1.1, 0, 1.1, 0)
SHARE_MAX = 2.0
NA_A = 2
EV_ACT = [(1, 1, 1), (1, 0, 1), (1, 1, 1), (1, 0, 1)]
REACH = 2.0


def pieces(r0, n, ring):
    out = []
    while n:
        s = r0 % ring
        m = min(n, ring - s)
        out.append((r0, s, m))
        r0, n = r0 + m, n - m
    return out


def phase_a(nc, ctx, p, ins, k, xtp, offd, x1d):
    S = lambda shape, dt=F32, name=None: ctx.enter_context(nc.sbuf_tensor(name, shape, dt))
    xin = S([128, NX, 512], name="a_xin")
    tok = S([128, 2, 4, 128], name="a_tok")
    tn = S([128, 3, 4, 128], name="a_tn")
    st = S([128, 2, 4, 6], name="a_st")
    mv = S([128, 2, 4, 2], name="a_mv")
    rs = S([128, 2, 8], name="a_rs")
    xn = S([128, NXN, 4, 130], name="a_xn")
    zs = S([96, NZ, 128], name="a_zs")
    off = S([96, 2, 512], name="a_off")
    r1 = S([96, 2, 512], name="a_r1")
    r2 = S([96, 2, 512], name="a_r2")
    t1 = S([96, 2, 512], BF16, name="a_t1")
    win = S([NPART, NPT, 8, 128], name="a_win")
    ab = S([NPART, 3, 2, 384], name="a_ab")
    sw = S([NPART, 2, 9, 128], name="a_sw")
    sr = S([128, NSR, 9, 128], name="a_sr")
    xo = S([128, 2, 512], name="a_xo")
    PB = [ctx.enter_context(nc.psum_tensor(f"a_p{i}", [128, 512], F32)) for i in range(2)]
    PW = ctx.enter_context(nc.psum_tensor("a_pw", [128, 2, 512], F32))
    PB += [None, None] + [ctx.enter_context(nc.psum_tensor(f"a_p{i}", [128, 512], F32)) for i in range(4, 8)]
    Pt = k["P"]
    pe, act, dve, pool = p.pe, p.act, p.dve, p.pool
    ident = k["ident"]

    dve.op(lambda e: e.memset(xn[:, :, :, 0:1], 0.0))
    zb = dve.op(lambda e: e.memset(xn[:, :, :, 129:130], 0.0))
    tl, tt, tst, tcv = {}, {}, {}, {}
    bank = {"k": 0, "free": [None, None]}
    tns = {}
    toks, ready = {}, {}
    xnw = {}
    xnr = {}
    offw, pw, pr = {}, {}, {}
    offst, offr = {}, {}
    cz, zw, szr = {}, {}, {}
    splits = []
    stores = []

    def take():
        i = bank["k"] % 2
        bank["k"] += 1
        return i, PB[i], bank["free"][i]

    def ln(G):
        b, q = divmod(G, GI)
        i, T, fr = take()
        v = T[:, :].rearrange("p (r c) -> p r c", r=4)
        for r in range(4):
            t = pe.op(lambda e, r=r: e.transpose(v[:, r, :], xin[:, G % NX, r * 128:(r + 1) * 128],
                                                 ident[:, :]), tl[G], fr, sig=(r == 3))
        u = act.op(lambda e: e.copy(tok[:, G % 2, :, :], v), t, *toks.get(G - 2, ()))
        bank["free"][i] = u
        ready[G] = token_stats(p, tok[:, G % 2], st[:, G % 2], mv[:, G % 2], rs[:, G % 2], 1e-6, u,
                               k["mhalf"], toks.get(G - 2), NA_A)

    def norm(G):
        b, q = divmod(G, GI)
        toks[G] = token_norm(p, tok[:, G % 2], mv[:, G % 2], rs[:, G % 2], tn[:, G % 3], ready[G],
                             (tns.get(G - 3), tt.get(G - 3)), NA_A)
        dst = xtp[b * PIX + (4 * q + 3) * PC:b * PIX + (4 * q + 7) * PC, :].rearrange(
            "(r w) c -> w r c", w=PC)[3:131]

        def store():
            tns[G] = tst[G] = p.q["st"].dma(lambda e: e.dma_start(dst, tn[:, G % 3, :, :]), *toks[G])
        stores.append([2, store])

    def back(G):
        b, q = divmod(G, GI)
        i, T, fr = take()
        for r in range(4):
            t = pe.op(lambda e, r=r: e.transpose(T[:, r * 128:(r + 1) * 128], tn[:, G % 3, r, :],
                                                 ident[:, :]), *toks[G], fr, sig=(r == 3))
        tt[G] = t
        u = act.op(lambda e: e.copy(xn[:, G % NXN, :, 1:129], T[:, :].rearrange("p (r c) -> p r c", r=4)),
                   t, tcv.get(G - NXN), zb)
        bank["free"][i] = u
        xnw[G] = u

    def parts(G):
        b, q = divmod(G, GI)
        i, T, fr = take()
        for kx in range(3):
            t = pe.op(lambda e, kx=kx: e.matmul(
                T[0:96, :].rearrange("p (r c) -> p r c", r=4), k["wof"][:, kx, :],
                xn[:, G % NXN, :, kx:kx + 128], start=(kx == 0), stop=(kx == 2)), fr, xnw[G], sig=(kx == 2))
            if kx < 2:
                yield 0.86
        tcv[G] = t
        v = T[0:96, :].rearrange("p (r c) -> p r c", r=4)
        R = b * 132
        for ky in range(3):
            y0, y1 = max(4 * q + 1 - ky, 0), min(4 * q + 5 - ky, H)
            P3 = slice(32 * ky, 32 * ky + 32)
            for r0, s, m in pieces(R + y0, y1 - y0, NZ):
                o = r0 - R + ky - 1 - 4 * q
                u = act.op(lambda e, P3=P3, s=s, m=m, o=o: e.copy(zs[P3, s:s + m, :], v[P3, o:o + m, :]),
                           t, szr.get(G - 2))
        zw[G] = [u]
        bank["free"][i] = u
        if q == 0:
            zw[G].append(dve.op(lambda e: e.memset(zs[0:32, R % NZ, :], 0.0), szr.get(G - 2)))
        if q == GI - 1:
            zw[G].append(dve.op(lambda e: e.memset(zs[64:96, (R + H - 1) % NZ, :], 0.0), szr.get(G - 2)))
        yield 0.86

    def offsets(G):
        b, q = divmod(G, GI)
        i, T, fr = take()
        s = (b * 132 + 4 * q) % NZ
        need = zw[G] + (zw[G + 1] if q < GI - 1 else []) + (zw[G - 1] if q else [])
        t = pe.op(lambda e: e.matmul(T[0:96, :], k["selz"][:, :], zs[:, s:s + 4, :].rearrange(
            "p r c -> p (r c)"), start=True, stop=True), fr, *need)
        szr[G] = t
        w = G % 2
        pp = Pt[0:96, (G % NPR) * 512:(G % NPR + 1) * 512]
        o = act.op(lambda e: e.copy(off[:, w, :], T[0:96, :]), t, offst.get(G - 2), cz.get(G - 2), offr.get(G - 2))
        bank["free"][i] = o
        rows = b * H * W + 4 * q * W

        def store():
            offst[G] = p.q["st"].dma(lambda e: e.dma_start(offd[:, rows:rows + 512], off[0:18, w, :]), o)
        stores.append([2, store])
        h = dve.op(lambda e: e.tensor_copy(pp, off[:, w, :]), o, pr.get(G - NPR))
        a = pool.op(lambda e: e.tensor_tensor(r1[:, w, :], off[:, w, :], pp, ALU.subtract), h, cz.get(G - 2), pw.get(G - 2))
        m1 = pool.op(lambda e: e.tensor_copy(t1[:, w, :], r1[:, w, :]), a)
        c = pool.op(lambda e: e.tensor_tensor(r2[:, w, :], r1[:, w, :], t1[:, w, :], ALU.subtract), m1)
        cz[G] = c

        def rest():
            dve.op(lambda e: e.tensor_copy(Pt[32:64, (G % NPR) * 512:(G % NPR + 1) * 512], r1[32:64, w, :]), a)
            pw[G] = dve.op(lambda e: e.tensor_copy(Pt[64:96, (G % NPR) * 512:(G % NPR + 1) * 512],
                                                   r2[64:96, w, :]), c)
        splits.append([1, rest])

        def reach(dst, alu):
            offr[G] = dve.op(lambda e: e.tensor_reduce(dst, off[:, w, :], AX.X, alu), o)
        splits.append([2, lambda: reach(k["fm"][:, G:G + 1], ALU.max)])
        splits.append([2, lambda: reach(k["fm"][:, NG + G:NG + G + 1], ALU.min)])
        yield 0.86

    winw, winr = {}, {}
    nwin = [0]
    ay_free, ax_free = [None], [None]
    nch = [0]
    chunk_s = {}
    srw, srr = {}, {}
    swr = {}
    smp_free = [None, None, None]
    TB = {0: (0, 3), 1: (3, 6), 2: (6, 8)}

    def kys(c):
        return [ky for ky in range(3) if 0 <= c + 1 - ky < H]

    def load_window(b, c):
        n = nwin[0]
        nwin[0] += 1
        dep = [tst[g] for g in range(b * GI + max(0, (c - 2) // 4), b * GI + min(GI - 1, (c + 2) // 4) + 1)]
        last = []
        for j in range(5):
            r = c + j - 2 + 3
            a = b * PIX + r * PC
            src = bass.AP(xtp.tensor, a * 128, [[128, 24], [16 * 128, 8], [1, 128]])
            last.append(p.q["w"].dma(lambda e, j=j, src=src: e.dma_start(
                win[24 * j:24 * j + 24, n % NPT, :, :], src), *dep, winr.get(n - NPT)))
        winw[(b, c)] = (n, last)

    ax_bufs = {}

    def expand(b, c, ky):
        y = c + 1 - ky
        G = b * GI + y // 4
        col = (G % NPR) * 512 + (y % 4) * 128
        m = nch[0]
        nch[0] += 1
        for half in range(2):
            for kx in range(3):
                tx = pe.op(lambda e, kx=kx, half=half: e.matmul(
                    PW[0:NPART, half, kx * 128:(kx + 1) * 128], k["sel"][0:98, 9 * half + 3 * ky + kx, :],
                    Pt[0:98, col:col + 128], start=True, stop=True), pw[G], ay_free[0],
                    sig=(half == 1 and kx == 2))
        pr[G] = tx
        i = m % 3
        a = act.op(lambda e: e.activation(ab[:, i, :, :], PW[0:NPART, :, 0:384], ACT.Abs), tx,
                   chunk_s.get(m - 3))
        ay_free[0] = a
        return m, ky, a

    def clip(m, a):
        i = m % 3
        return dve.op(lambda e: e.tensor_scalar(ab[:, i, :, :], ab[:, i, :, :], 1.0, 1.0, ALU.min,
                                                ALU.subtract), a)

    def weigh(n, m, ky, v):
        i = m % 3
        chunk_s[m] = dve.op(lambda e: e.tensor_tensor(
            sw[:, n % 2, 3 * ky:3 * ky + 3, :].rearrange("p a b -> p (a b)"), ab[:, i, 0, :],
            ab[:, i, 1, :], ALU.mult), v, swr.get(n - 2))
        return chunk_s[m]

    def sample(b, c, stok, bk):
        n, wt = winw[(b, c)]
        ks = kys(c)
        t0, t1_ = 3 * ks[0], 3 * ks[-1] + 3
        slot = (b * 132 + c) % NSR
        g0, g1 = TB[bk]
        v = PB[4 + bk][:, 0:9 * (g1 - g0) * 16].rearrange("p (t x) -> p t x", t=9)
        for g in range(g0, g1):
            t = pe.op(lambda e, g=g: e.matmul(
                v[:, t0:t1_, (g - g0) * 16:(g - g0 + 1) * 16], win[:, n % NPT, g, :],
                sw[:, n % 2, t0:t1_, 16 * g:16 * g + 16], start=True, stop=True),
                *wt, *stok, smp_free[bk], sig=(g == g1 - 1))
        o = sr[:, slot, t0:t1_, g0 * 16:g1 * 16]
        if EV_ACT[c % 4][bk]:
            x = act.op(lambda e: e.activation(o, v[:, t0:t1_, :], ACT.Copy), t, srr.get(slot))
        else:
            x = dve.op(lambda e: e.tensor_copy(o, v[:, t0:t1_, :]), t, srr.get(slot))
        smp_free[bk] = x
        srw.setdefault((b, c), []).append(x)
        if bk == 2:
            winr[n] = t
            swr[n] = t

    xow, oc_free = {}, [None]
    xl = {}

    def outconv(G):
        b, q = divmod(G, GI)
        todo = []
        for ky in (1, 0, 2):
            for r0, s, m in pieces(b * 132 + 4 * q + ky - 1, 4, NSR):
                o0 = r0 - (b * 132 + 4 * q + ky - 1)
                for kx in range(3):
                    todo.append((3 * ky + kx, s, m, o0))
        need = [t for c in range(4 * q - 1, 4 * q + 5) for t in srw[(b, c)]]
        for n, (tap, s, m, o0) in enumerate(todo):
            if n:
                yield 0.22 * todo[n - 1][2]
            t = pe.op(lambda e, tap=tap, s=s, m=m, o0=o0, n=n: e.matmul(
                PB[7][:, o0 * 128:(o0 + m) * 128].rearrange("p (r c) -> p r c", r=m),
                k["wcv"][:, tap, :], sr[:, s:s + m, tap, :],
                start=(n == 0), stop=(n == len(todo) - 1), skip_group_check=True),
                oc_free[0], *need, sig=(n == len(todo) - 1))
        for c in range(4 * q - 1, 4 * q + 5):
            srr[(b * 132 + c) % NSR] = t
        u = dve.op(lambda e: e.tensor_tensor(xo[:, G % 2, :], PB[7][:, :], xin[:, G % NX, :], ALU.add),
                   t, xow.get(G - 2))
        oc_free[0] = u
        xl[G] = u

        def store():
            xow[G] = p.q["st"].dma(lambda e: e.dma_start(
                x1d[b * 128:(b + 1) * 128, 4 * q * W:4 * q * W + 512], xo[:, G % 2, :]), u)
        stores.append([2, store])
        while late and (late[0] - NX) in xl:
            load(late.pop(0))
        yield 0.22 * todo[-1][2]

    def load(G):
        b, q = divmod(G, GI)
        tl[G] = p.q["ld"].dma(lambda e: e.dma_start(
            xin[:, G % NX, :], ins["x"][b * 128:(b + 1) * 128, 4 * q * W:4 * q * W + 512]), xl.get(G - NX))

    centres = [(b, c) for b in range(B) for c in range(-1, H + 1)]
    rank = {bc: i for i, bc in enumerate(centres)}
    late = []
    jobs = []
    stok = {}
    state = {"done": 0, "loaded": 0, "credit": 0.0}

    def flush():
        for x in stores:
            x[0] -= 1
        while stores and stores[0][0] < 0:
            stores.pop(0)[1]()
        for x in splits:
            x[0] -= 1
        while splits and splits[0][0] < 0:
            splits.pop(0)[1]()

    def piece():
        weight = next(jobs[0], None)
        if weight is None:
            jobs.pop(0)
        return weight or 0.0

    def weave(credit):
        state["credit"] = min(state["credit"] + credit, SHARE_MAX)
        while jobs and state["credit"] > 0:
            state["credit"] -= piece()

    def until(ready):
        while not ready():
            if jobs:
                piece()
            else:
                splits.pop(0)[1]()

    def centre_step(idx):
        bc = centres[idx] if idx < len(centres) else None
        before = centres[idx - 1] if idx else None
        ks = kys(bc[1]) if bc else []
        n = winw[bc][0] if bc else None
        clipped, stk = [], []
        for ky in ks:
            g = bc[0] * GI + (bc[1] + 1 - ky) // 4
            until(lambda: g in pw)
        if before:
            old = before[0] * 132 + before[1] - NSR
            ob, oc = divmod(old + 1, 132)
            og = ob * GI + min((oc - 1 + 1) // 4, GI - 1)
            if ob >= 0 and oc - 1 <= H:
                until(lambda: og in xl)
        flush()
        for j in range(3):
            if j < len(ks):
                m, ky, a = expand(*bc, ks[j])
                clipped.append((m, ky, clip(m, a)))
            weave(SHARES[2 * j])
            if before:
                sample(*before, stok[before], j)
            if j and j - 1 < len(ks):
                m, ky, v = clipped[j - 1]
                stk.append(weigh(n, m, ky, v))
            weave(SHARES[2 * j + 1])
        if len(ks) == 3:
            m, ky, v = clipped[2]
            stk.append(weigh(n, m, ky, v))
        if bc:
            stok[bc] = stk
        if before and before[1] >= 4 and before[1] % 4 == 0:
            jobs.append(outconv(before[0] * GI + before[1] // 4 - 1))

    def advance(upto, between):
        while state["done"] < upto:
            i = state["done"]
            if between:
                between.pop(0)()
            while state["loaded"] < min(i + 4, len(centres)):
                load_window(*centres[state["loaded"]])
                state["loaded"] += 1
            centre_step(i)
            state["done"] += 1

    def finish(job):
        for _ in job:
            pass

    for G in range(NX - 1):
        load(G)
    for G in range(NG + 4):
        steps = {"p": lambda G=G: jobs.append(parts(G - 2)), "o": lambda G=G: jobs.append(offsets(G - 3)),
                 "l": lambda G=G: ln(G), "b": lambda G=G: back(G - 1), "n": lambda G=G: norm(G)}
        live = {"p": 0 <= G - 2 < NG, "o": 0 <= G - 3 < NG, "l": G < NG, "b": 0 <= G - 1 < NG, "n": G < NG}
        between = [lambda w=w: [steps[x]() for x in w if live[x]] for w in ORDER]
        between = [(lambda w=w, steps=steps, live=live: [steps[x]() for x in w if live[x]]) for w in ORDER]
        if G >= 4:
            b, q = divmod(G - 4, GI)
            advance(rank[(b, H) if q == GI - 1 else (b, 4 * q + 1)] + 1, between)
        for f in between:
            f()
        if G < 4:
            while jobs:
                finish(jobs.pop(0))
            for _ in range(3):
                flush()
        n = G + NX - 1
        if NX - 1 <= n < NG:
            late.append(n)
        while late and (late[0] - NX < 0 or (late[0] - NX) in xl):
            load(late.pop(0))
    centre_step(len(centres))
    while jobs:
        finish(jobs.pop(0))
    for _ in range(4):
        flush()


def far_flag(nc, ctx, p, k):
    S = lambda name, shape, dt=F32: ctx.enter_context(nc.sbuf_tensor(name, shape, dt))
    r = S("g_r", [96, 3])
    T = ctx.enter_context(nc.psum_tensor("g_t", [1, 512], F32))
    d = p.dve
    a = d.op(lambda e: e.tensor_reduce(r[:, 0:1], k["fm"][:, 0:NG], AX.X, ALU.max))
    b = d.op(lambda e: e.tensor_reduce(r[:, 1:2], k["fm"][:, NG:2 * NG], AX.X, ALU.min))
    b = d.op(lambda e: e.tensor_scalar(r[:, 1:2], r[:, 1:2], -1.0, None, ALU.mult), b)
    c = d.op(lambda e: e.tensor_tensor(r[:, 2:3], r[:, 0:1], r[:, 1:2], ALU.max), a, b)
    t = p.pe.op(lambda e: e.transpose(T[0:1, 0:96], r[:, 2:3], k["ident"][0:96, 0:96]), c)
    g = d.op(lambda e: e.tensor_reduce(k["gm"][:, 0:1], T[0:1, 0:96], AX.X, ALU.max), t)
    g = d.op(lambda e: e.tensor_scalar(k["gm"][:, 0:1], k["gm"][:, 0:1], REACH, None, ALU.is_gt), g)
    t = d.op(lambda e: e.tensor_copy(k["flag"][:, :], k["gm"][:, 0:1]), g)
    for eng in (p.pe, p.act, p.dve, p.pool, p.sp):
        eng.wait(t)


def far_rows(nc, ins, k, xtp, offd, x1d):
    with ExitStack() as ctx:
        S = lambda name, shape, dt=F32: ctx.enter_context(nc.sbuf_tensor(name, shape, dt))
        orow = S("f_or", [18, 128]); of = S("f_of", [128, 9, 2]); ri = S("f_ri", [128, 9, 2], I32)
        rf = S("f_rf", [128, 9, 2]); gt = S("f_gt", [128, 9, 2]); fl = S("f_fl", [128, 9, 2])
        fr = S("f_fr", [128, 2, 9, 2]); ps = S("f_ps", [128, 9, 2]); xf = S("f_xf", [128, 4, 9])
        ii = S("f_ii", [128, 4, 9], I32); wt = S("f_wt", [128, 4, 9]); ct = S("f_ct", [128, 9, 2])
        ctx0 = S("f_c0", [128, 9, 2]); bb = S("f_bb", [128, 1]); xr = S("f_xr", [128, 128])
        g = S("f_g", [128, 9, 4, 128]); sT = S("f_sT", [128, 9, 128]); xo = S("f_xo", [128, 128])
        P0 = ctx.enter_context(nc.psum_tensor("f_p0", [128, 512], F32))
        PT = [ctx.enter_context(nc.psum_tensor(f"f_pt{i}", [128, 512], F32)) for i in range(3)]
        PO = ctx.enter_context(nc.psum_tensor("f_po", [128, 512], F32))
        s0 = ctx.enter_context(nc.semaphore("f_init"))
        with nc.Block() as block:
            @block.sync
            def _(e):
                e.dma_start(ctx0[:, :, :], ins["far"][:, :, :]).then_inc(s0, 16)
                e.wait_ge(s0, 16)

            @block.vector
            def _(e):
                e.memset(bb[:, :], float(3 * PC + 3))
                e.wait_ge(s0, 16)

            @block.tensor
            def _(e):
                e.wait_ge(s0, 16)

            @block.scalar
            def _(e):
                e.wait_ge(s0, 16)

            @block.gpsimd
            def _(e):
                e.wait_ge(s0, 16)
        names = ("pe", "act", "dve", "pool", "sp", "in0", "in1", "st0", "g0", "g1", "g2", "g3")
        sems = [ctx.enter_context(nc.semaphore("f_" + n)) for n in names]

        def row(b, y):
            sm = dict(zip(names, sems))
            p = Phase.__new__(Phase)
            p.pe, p.act, p.dve, p.pool, p.sp = (Engine(n, sm[n]) for n in names[:5])
            p.q = {"i": Queue(p.sp, [sm["in0"], sm["in1"]]), "g": Queue(p.pool, [sm[f"g{i}"] for i in range(4)]),
                   "o": Queue(p.sp, [sm["st0"]])}
            pe, act, dve, pool = p.pe, p.act, p.dve, p.pool
            t0 = p.q["i"].dma(lambda e: e.dma_start(
                orow[:, :], offd[:, bass.ds(b * (H * W) + y * W, W)]))
            t1 = p.q["i"].dma(lambda e: e.dma_start(
                xr[:, :], ins["x"][bass.ds(b * 128, 128), bass.ds(y * W, W)]))
            t = pe.op(lambda e: e.transpose(P0[:, 0:18], orow[:, :], k["ident"][0:18, 0:18]), t0)
            v = dve.op(lambda e: e.tensor_scalar(of[:, :, :].rearrange("p a b -> p (a b)"), P0[:, 0:18],
                                                 -400.0, 400.0, ALU.max, ALU.min), t)
            v = dve.op(lambda e: e.tensor_copy(ri[:, :, :], of[:, :, :]), v)
            v = dve.op(lambda e: e.tensor_copy(rf[:, :, :], ri[:, :, :]), v)
            v = dve.op(lambda e: e.tensor_tensor(gt[:, :, :], rf[:, :, :], of[:, :, :], ALU.is_gt), v)
            v = dve.op(lambda e: e.tensor_tensor(fl[:, :, :], rf[:, :, :], gt[:, :, :], ALU.subtract), v)
            f1 = dve.op(lambda e: e.tensor_tensor(fr[:, 1], of[:, :, :], fl[:, :, :], ALU.subtract), v)
            f0 = dve.op(lambda e: e.tensor_scalar(fr[:, 0], fr[:, 1], -1.0, 1.0, ALU.mult, ALU.add), f1)
            v = dve.op(lambda e: e.tensor_tensor(ps[:, :, :], fl[:, :, :], ct[:, :, :], ALU.add), v)
            c0 = dve.op(lambda e: e.tensor_scalar(ps[:, :, 0:1], ps[:, :, 0:1], -2.0, 129.0, ALU.max,
                                                  ALU.min), v)
            c1 = dve.op(lambda e: e.tensor_scalar(ps[:, :, 1:2], ps[:, :, 1:2], -2.0, 130.0, ALU.max,
                                                  ALU.min), v)
            v = dve.op(lambda e: e.scalar_tensor_tensor(out=xf[:, 0, :], in0=ps[:, :, 0], scalar=float(PC),
                                                        in1=ps[:, :, 1], op0=ALU.mult, op1=ALU.add), c0, c1)
            v = dve.op(lambda e: e.tensor_scalar(xf[:, 0, :], xf[:, 0, :], bb[:, 0:1], None, ALU.add), v)
            for j, o in ((1, 1), (2, PC), (3, PC + 1)):
                z = dve.op(lambda e, j=j, o=o: e.tensor_scalar(xf[:, j, :], xf[:, 0, :], float(o), None,
                                                               ALU.add), v)
            z = dve.op(lambda e: e.tensor_copy(ii[:, :, :], xf[:, :, :]), z)
            for j in range(4):
                wv = dve.op(lambda e, j=j: e.tensor_tensor(wt[:, j, :], fr[:, j // 2, :, 0],
                                                           fr[:, j % 2, :, 1], ALU.mult), f0)
            nx = dve.op(lambda e: e.tensor_scalar(ct[:, :, 0:1], ct[:, :, 0:1], 1.0, None, ALU.add), v)
            for t_ in range(9):
                for j in range(4):
                    p.q["g"].dma(lambda e, t_=t_, j=j: e.indirect_dma_start(
                        out=g[:, t_, j, :], out_offset=None, in_=xtp[:, :],
                        in_offset=bass.IndirectOffsetOnAxis(ap=ii[:, j, t_:t_ + 1], axis=0)), z)
            dve.wait(*p.q["g"].all())
            pool.wait(*p.q["g"].all())
            for t_ in range(9):
                a = dve.op(lambda e, t_=t_: e.tensor_scalar(g[:, t_, 0, :], g[:, t_, 0, :], wt[:, 0, t_:t_ + 1],
                                                            None, ALU.mult), wv)
                for j in range(1, 4):
                    a = dve.op(lambda e, t_=t_, j=j: e.scalar_tensor_tensor(
                        out=g[:, t_, 0, :], in0=g[:, t_, j, :], scalar=wt[:, j, t_:t_ + 1],
                        in1=g[:, t_, 0, :], op0=ALU.mult, op1=ALU.add), a)
            for t_ in range(9):
                t = pe.op(lambda e, t_=t_: e.transpose(PT[t_ // 3][:, (t_ % 3) * 128:(t_ % 3 + 1) * 128],
                                                       g[:, t_, 0, :], k["ident"][:, :]), a)
            for i in range(3):
                u = act.op(lambda e, i=i: e.copy(sT[:, 3 * i:3 * i + 3, :].rearrange("p a b -> p (a b)"),
                                                 PT[i][:, 0:384]), t)
            for t_ in range(9):
                t = pe.op(lambda e, t_=t_: e.matmul(PO[:, 0:128], k["wcv"][:, t_, :], sT[:, t_, :],
                                                    start=(t_ == 0), stop=(t_ == 8)), u)
            o = dve.op(lambda e: e.tensor_tensor(xo[:, :], PO[:, 0:128], xr[:, :], ALU.add), t, t1)
            s = p.q["o"].dma(lambda e: e.dma_start(
                x1d[bass.ds(b * 128, 128), bass.ds(y * W, W)], xo[:, :]), o)
            p.emit(nc)
            with nc.Block() as block:
                @block.gpsimd
                def _(e):
                    e.dma_reset(range(min(s.num for s in sems[-4:]), max(s.num for s in sems[-4:]) + 1))
                    for s in sems:
                        e.sem_clear(s)

        with nc.Fori(0, B) as b:
            with nc.Block() as block:
                @block.vector
                def _(e):
                    e.tensor_copy(ct[:, :, :], ctx0[:, :, :])
            with nc.Fori(0, H) as y:
                row(b, y)
            with nc.Block() as block:
                @block.vector
                def _(e):
                    e.tensor_scalar(bb[:, :], bb[:, :], float(PIX), None, ALU.add)


def phase_bc(nc, ctx, p, ins, k, x1d, x2d, x3d):
    S = lambda name, shape, dt=F32: ctx.enter_context(nc.sbuf_tensor(name, shape, dt))
    ew = S("b_ew", [128, 8, 128]); rw = S("b_rw", [128, 8]); ebf = S("b_ebf", [96, 3, 128])
    ebb = S("b_ebb", [96, 128], BF16); ebt = S("b_ebt", [96, 3, 128], BF16)
    rb = S("b_rb", [128, 8]); al = S("b_al", [128, 128]); gw = S("b_gw", [128, 2, 128]); gb = S("b_gb", [128, 1])
    sef = S("b_sef", [24, 8, 128]); se = S("b_se", [24, 8, 128], BF16); idb = S("b_idb", [128, 128], BF16)
    x1 = S("b_x1", [128, 3, 512])
    tk = S("b_tk", [128, 5, 4, 128]); tn = S("b_tn", [128, 2, 4, 128]); tnT = S("b_tnT", [128, 2, 512])
    st = S("b_st", [128, 2, 4, 6]); mv = S("b_mv", [128, 2, 4, 2]); rs = S("b_rs", [128, 2, 8])
    lg = S("b_lg", [128, 2, 4, 8]); mx = S("b_mx", [128, 2, 4, 8]); m2 = S("b_m2", [128, 2, 4, 8])
    l2 = S("b_l2", [128, 2, 4, 8]); lm = S("b_lm", [128, 2, 4, 8]); ex = S("b_ex", [128, 2, 4, 8])
    mk = S("b_mk", [128, 2, 4, 8]); pm = S("b_pm", [128, 2, 4, 8]); sm = S("b_sm", [128, 2, 8])
    pw = S("b_pw", [128, 2, 4, 8]); q1 = S("b_q1", [128, 2, 4, 8]); q2 = S("b_q2", [128, 2, 4, 8])
    pp = S("b_pp", [128, 2, 4, 3, 32], BF16); pT = S("b_pT", [96, 3, 512], BF16)
    z = S("b_z", [128, 2, 8, 512]); zp = S("b_zp", [128, 2, 512])
    xa = S("b_xa", [128, 3, 4, 128])
    st2 = S("b_st2", [128, 2, 4, 6]); mv2 = S("b_mv2", [128, 2, 4, 2]); rs2 = S("b_rs2", [128, 2, 8])
    tn2 = S("b_tn2", [128, 2, 4, 128])
    xf = S("b_xf", [128, 128, 128])
    x2r = S("c_x2", [128, 3, 4, 128]); x3t = S("c_x3", [128, 3, 4, 128])
    st3 = S("c_st", [128, 2, 4, 6]); mv3 = S("c_mv", [128, 2, 4, 2]); rs3 = S("c_rs", [128, 2, 8])
    tn3 = S("c_tn", [128, 2, 4, 128]); tnT3 = S("c_tnT", [128, 2, 512]); lo = S("c_lo", [128, 3, 512]); nm = S("c_nm", [128, 3, 1])
    PS = lambda name, shape: ctx.enter_context(nc.psum_tensor(name, shape, F32))
    TB = [PS("b_t0", [128, 512]), PS("b_t1", [128, 512])]
    PB = [PS("b_p0", [128, 512]), PS("b_p1", [128, 512])]
    RB, PT = PS("b_r", [128, 512]), PS("b_pt", [96, 512])
    ZE, ZC = PS("b_ze", [128, 4, 128]), PS("b_zc", [128, 4, 128])
    pe, act, dve, pool = p.pe, p.act, p.dve, p.pool
    ident = k["ident"]

    q = p.q["c"]
    for t, n in ((rw, "rw"), (rb, "rb"), (al, "al"), (gw, "gw"), (gb, "gb"), (sef, "sele")):
        q.dma(lambda e, t=t, n=n: e.dma_start(t[:, :] if len(t.shape) == 2 else t[:, :, :],
                                              ins[n][:, :] if len(t.shape) == 2 else ins[n][:, :, :]))
    q.dma(lambda e: e.dma_start(ebf[:, 0, :], ins["eb"][:, :]))
    q.dma(lambda e: e.dma_start(ew[:, :, :], ins["ew"][:, :, :]))
    consts = q.all()
    pe.wait(*consts)
    dve.wait(*consts)
    act.wait(*consts)
    big = dve.op(lambda e: e.memset(m2[:, :, :, :], 3.0e38))
    dve.op(lambda e: e.tensor_copy(se[:, :, :], sef[:, :, :]))
    cc = dve.op(lambda e: e.tensor_copy(idb[:, :], ident[:, :]))
    for j in range(3):
        cc = dve.op(lambda e, j=j: e.tensor_copy(ebt[:, j, :], ebf[:, j, :]), cc)
        if j < 2:
            cc = dve.op(lambda e, j=j: e.tensor_tensor(ebf[:, j + 1, :], ebf[:, j, :], ebt[:, j, :],
                                                       ALU.subtract), cc)
    for j in range(3):
        cc = dve.op(lambda e, j=j: e.tensor_copy(ebb[32 * j:32 * j + 32, :], ebt[32 * j:32 * j + 32, j, :]), cc)
    ppz = dve.op(lambda e: e.memset(pp[:, :, :, :, :], 0.0))
    pe.wait(cc)

    pool_k = [0]
    free = [None, None]
    pfree = [None, None]
    rfree, ptfree, zefree, zcfree = [None], [None], [None], [None]
    zpr = [None, None]
    npb, nzp = [0], [0]
    T = {}
    g_ = lambda *key: T.get(key)

    def transposes(src, *waits):
        i = pool_k[0] % 2
        pool_k[0] += 1
        D = TB[i]
        for r in range(4):
            t = pe.op(lambda e, r=r: e.transpose(D[:, r * 128:(r + 1) * 128], src(r), ident[:, :]),
                      free[i], *waits, sig=(r == 3))
        return i, D, t

    def rows_of(G):
        b, h = divmod(G, GI)
        n = b * H * W + h * 512
        return lambda d: d[n:n + 512, :].rearrange("(r w) c -> w r c", w=128)

    def load(G):
        b, h = divmod(G, GI)
        T["x1", G] = p.q["ld"].dma(lambda e: e.dma_start(
            x1[:, G % 3, :], x1d[b * 128:(b + 1) * 128, h * 512:h * 512 + 512]), g_("t1", G - 3))

    def tokens(G):
        i, D, t = transposes(lambda r: x1[:, G % 3, r * 128:(r + 1) * 128], T["x1", G])
        T["t1", G] = t
        T["tk", G] = free[i] = act.op(
            lambda e: e.copy(tk[:, G % 5], D[:, :].rearrange("p (r c) -> p r c", r=4)), t,
            g_("x2", G - 5), *(g_("tn", G - 5) or ()))

    def stats1(G):
        T["s1", G] = token_stats(p, tk[:, G % 5], st[:, G % 2], mv[:, G % 2], rs[:, G % 2], 1e-5, T["tk", G],
                                 k["mhalf"], g_("tn", G - 2), NA_B)

    def norm1(G):
        T["tn", G] = token_norm(p, tk[:, G % 5], mv[:, G % 2], rs[:, G % 2], tn[:, G % 2], T["s1", G],
                                (g_("t2", G - 2),), NA_B)

    def channels(G):
        i, D, t = transposes(lambda r: tn[:, G % 2, r, :], *T["tn", G])
        T["t2", G] = t
        T["tT", G] = free[i] = act.op(lambda e: e.copy(tnT[:, G % 2, :], D[:, :]), t, *(g_("z", G - 2) or ()))

    def router(G):
        w = G % 2
        for r in range(4):
            t = pe.op(lambda e, r=r: e.matmul(RB[:, r * 8:r * 8 + 8], tnT[:, w, r * 128:(r + 1) * 128],
                                              rw[:, :], start=True, stop=True), T["tT", G], rfree[0],
                      sig=(r == 3))
        L = dve.op(lambda e: e.tensor_tensor(lg[:, w], RB[:, 0:32].rearrange("p (r e) -> p r e", r=4),
                                             rb[:, None, :].to_broadcast([128, 4, 8]), ALU.add), t,
                   g_("p", G - 2))
        rfree[0] = L
        T["rt", G] = t
        for r in range(4):
            m = dve.op(lambda e, r=r: e.max(mx[:, w, r, :], lg[:, w, r, :]), L)
        lmt = dve.op(lambda e: e.tensor_tensor(lm[:, w], lg[:, w],
                                               mx[:, w, :, 0:1].to_broadcast([128, 4, 8]), ALU.subtract),
                     m, g_("ex", G - 2))
        c = dve.op(lambda e: e.tensor_copy(m2[:, w, :, 0:2], mx[:, w, :, 0:2]), m, big)
        for r in range(4):
            zt = dve.op(lambda e, r=r: e.match_replace(l2[:, w, r, :], m2[:, w, r, :], lg[:, w, r, :],
                                                       -3.0e38), c)
        T["ex", G] = act.op(lambda e: e.activation(ex[:, w], lm[:, w], ACT.Exp), lmt, g_("p", G - 2))
        T["mk", G] = dve.op(lambda e: e.tensor_tensor(mk[:, w], l2[:, w], lg[:, w], ALU.is_lt), zt)

    def weights(G):
        w = G % 2
        t = dve.op(lambda e: e.tensor_tensor(pm[:, w], ex[:, w], mk[:, w], ALU.mult), T["ex", G], T["mk", G])
        s = dve.op(lambda e: e.tensor_reduce(sm[:, w, 0:4], pm[:, w], AX.X, ALU.add), t)
        s = dve.op(lambda e: e.reciprocal(sm[:, w, 4:8], sm[:, w, 0:4]), s)
        s = dve.op(lambda e: e.tensor_tensor(pw[:, w], pm[:, w],
                                             sm[:, w, 4:8, None].to_broadcast([128, 4, 8]), ALU.mult), s)
        s = dve.op(lambda e: e.tensor_copy(pp[:, w, :, 0, 0:8], pw[:, w]), s, ppz, g_("ptm", G - 2))
        s = dve.op(lambda e: e.tensor_tensor(q1[:, w], pw[:, w], pp[:, w, :, 0, 0:8], ALU.subtract), s)
        s = dve.op(lambda e: e.tensor_copy(pp[:, w, :, 0, 8:16], q1[:, w]), s)
        s = dve.op(lambda e: e.tensor_tensor(q2[:, w], q1[:, w], pp[:, w, :, 0, 8:16], ALU.subtract), s)
        s = dve.op(lambda e: e.tensor_copy(pp[:, w, :, 0, 16:24], q2[:, w]), s)
        T["p", G] = dve.op(lambda e: e.tensor_copy(
            pp[:, w, :, 1:3, 0:24], pp[:, w, :, 0:1, 0:24].to_broadcast([128, 4, 2, 24])), s)

    def weights_t(G):
        for r in range(4):
            t = pe.op(lambda e, r=r: e.matmul(PT[:, r * 128:(r + 1) * 128], pp[:, G % 2, r].rearrange("p a b -> p (a b)"), idb[:, :],
                                              start=True, stop=True), T["p", G], ptfree[0], sig=(r == 3))
        T["ptm", G] = t
        T["pT", G] = ptfree[0] = act.op(lambda e: e.copy(pT[:, G % 3, :], PT[:, :]), t, g_("ye", G - 3))

    def scale(G, e0):
        w = G % 2
        i = npb[0] % 2
        npb[0] += 1
        t = pe.op(lambda e: e.matmul(PB[i][:, :], se[:, e0, :], pT[0:24, G % 3, :], start=True, stop=True),
                  T["pT", G], pfree[i])
        if e0 in POOL_E:
            j = nzp[0] % 2
            nzp[0] += 1
            pfree[i] = act.op(lambda e: e.copy(zp[:, j, :], PB[i][:, :]), t, zpr[j])
            zpr[j] = u = pool.op(lambda e: e.tensor_tensor(z[:, w, e0, :], tnT[:, w, :], zp[:, j, :],
                                                           ALU.mult), pfree[i], T["tT", G], g_("ye", G - 2))
        else:
            pfree[i] = u = dve.op(lambda e: e.tensor_tensor(z[:, w, e0, :], tnT[:, w, :], PB[i][:, :],
                                                            ALU.mult), t, T["tT", G], g_("ye", G - 2))
        T.setdefault(("z", G), []).append(u)

    def experts(G, r):
        w = G % 2
        pe.op(lambda e: e.matmul(ZE[:, r, :], pT[:, G % 3, r * 128:(r + 1) * 128], ebb[:, :], start=True,
                                 stop=False), zefree[0], *T["z", G], sig=False)
        for x in range(8):
            t = pe.op(lambda e, x=x: e.matmul(ZE[:, r, :], z[:, w, x, r * 128:(r + 1) * 128], ew[:, x, :],
                                              start=False, stop=(x == 7)), sig=(x == 7))
        if r == 3:
            T["ye", G] = t

    def stats2(G):
        a3 = xa[:, G % 3]
        T["x2", G] = zefree[0] = dve.op(lambda e: e.tensor_tensor(a3, ZE[:, :, :], tk[:, G % 5], ALU.add),
                                        T["ye", G], g_("x2s", G - 3), *(g_("tn2", G - 3) or ()))
        T["s2", G] = token_stats(p, a3, st2[:, G % 2], mv2[:, G % 2], rs2[:, G % 2], 1e-6, T["x2", G],
                                 k["mhalf"], g_("tn2", G - 2), NA_B)
        T["x2s", G] = p.q["st"].dma(lambda e: e.dma_start(rows_of(G)(x2d), a3), T["x2", G])

    def norm2(G):
        w = G % 2
        T["tn2", G] = token_norm(p, xa[:, G % 3], mv2[:, w], rs2[:, w], tn2[:, w], T["s2", G],
                                 (g_("t4", G - 2),), NA_B)

    def place(G):
        b, h = divmod(G, GI)
        i, D, t = transposes(lambda r: tn2[:, G % 2, r, :], *T["tn2", G])
        T["t4", G] = t
        v = D[:, :].rearrange("p (r c) -> p r c", r=4)
        if b % 2:
            runs = [(0, 4, slice(4 * h, 4 * h + 4))]
        elif h == 0:
            runs = [(0, 1, slice(0, 1)), (1, 4, slice(127, 124, -1))]
        else:
            runs = [(0, 4, slice(128 - 4 * h, 124 - 4 * h, -1))]
        for r0, r1, rows in runs:
            act.op(lambda e, r0=r0, r1=r1, rows=rows: e.copy(xf[:, rows, 0:1], v[:, r0:r1, 0:1]), t,
                   g_("c", G - GI))
            u = act.op(lambda e, r0=r0, r1=r1, rows=rows: e.copy(xf[:, rows, 127:0:-1], v[:, r0:r1, 1:128]))
        free[i] = u
        T["xf", G] = u

    def loadc(G):
        T["x2r", G] = p.q["lc"].dma(lambda e: e.dma_start(x2r[:, G % 3], rows_of(G)(x2d)), T["x2s", G],
                                    g_("x3", G - 3))

    def fourier(G):
        b, h = divmod(G, GI)
        need = T["xf", b * GI + GI - 1]
        for r in range(4):
            y = 4 * h + r
            row = (128 - y) % 128 if b % 2 else y
            t = pe.op(lambda e, r=r, row=row: e.matmul(ZC[:, r, :], xf[:, row, :], al[:, :],
                                                       start=True, stop=True), need, zcfree[0], sig=(r == 3))
        T["c", G] = t

    def stats3(G):
        w = G % 2
        a3 = x3t[:, G % 3]
        T["x3", G] = zcfree[0] = dve.op(lambda e: e.tensor_tensor(a3, ZC[:, :, :], x2r[:, G % 3], ALU.add),
                                        T["c", G], T["x2r", G], g_("x3s", G - 3), *(g_("tn3", G - 3) or ()))
        T["s3", G] = token_stats(p, a3, st3[:, w], mv3[:, w], rs3[:, w], 1e-5, T["x3", G], k["mhalf"],
                                 g_("tn3", G - 2), NA_B)
        T["x3s", G] = p.q["st"].dma(lambda e: e.dma_start(rows_of(G)(x3d), a3), T["x3", G])

    def norm3(G):
        w = G % 2
        T["tn3", G] = token_norm(p, x3t[:, G % 3], mv3[:, w], rs3[:, w], tn3[:, w], T["s3", G],
                                 (g_("t5", G - 2),), NA_B)

    def channels3(G):
        i, D, t = transposes(lambda r: tn3[:, G % 2, r, :], *T["tn3", G])
        T["t5", G] = t
        T["tT3", G] = free[i] = act.op(lambda e: e.copy(tnT3[:, G % 2, :], D[:, :]), t, g_("lgm", G - 2))

    def gate(G):
        b, h = divmod(G, GI)
        w = G % 2
        i = pool_k[0] % 2
        pool_k[0] += 1
        D = TB[i]
        o = b % 2
        P = slice(64 * o, 64 * o + 64)
        t = pe.op(lambda e: e.matmul(D[:, :], gw[:, o, :], tnT3[:, w, :], start=True, stop=True),
                  free[i], T["tT3", G])
        T["lgm", G] = t
        u = act.op(lambda e: e.activation(lo[P, G % 3, :], D[P, :], ACT.Identity, bias=gb[P, 0:1]), t,
                   g_("cs", G - 3))
        free[i] = u
        T["lo", G] = u

    def best(G):
        b, h = divmod(G, GI)
        a = b // 2
        P = slice(64 * (b % 2), 64 * (b % 2) + 64)
        cv, ci = k["cv"][P, a, 8 * h:8 * h + 8], k["ci"][P, a, 8 * h:8 * h + 8]
        m = dve.op(lambda e: e.max(cv, lo[P, G % 3, :]), T["lo", G])
        n = dve.op(lambda e: e.tensor_scalar(nm[P, G % 3, :], cv[:, 0:1], -1.0, None, ALU.mult), m,
                   g_("cs", G - 3))
        T["best", G] = n, dve.op(lambda e: e.max_index(ci, cv, lo[P, G % 3, :]), m)

    def sums(G):
        b, h = divmod(G, GI)
        a = b // 2
        P = slice(64 * (b % 2), 64 * (b % 2) + 64)
        T["cs", G] = act.op(lambda e: e.activation(lo[P, G % 3, :], lo[P, G % 3, :], ACT.Exp, bias=nm[P, G % 3, :],
                                                   accum_out=k["cs"][P, a, h:h + 1]), *T["best", G])

    LAG = GI + 6
    for G in range(3):
        load(G)
    for s in range(NG + LAG + 6):
        def at(lag, f, *a):
            if 0 <= s - lag < NG:
                f(s - lag, *a)
        at(LAG, fourier)
        at(LAG + 5, sums)
        at(0, tokens)
        at(3, weights_t)
        at(4, experts, 0)
        at(3, scale, 0)
        at(3, scale, 1)
        at(LAG, stats3)
        at(2, channels)
        at(1, norm1)
        at(LAG + 1, norm3)
        at(4, experts, 1)
        at(3, scale, 2)
        at(3, scale, 3)
        at(5, norm2)
        at(LAG + 4, best)
        at(4, experts, 2)
        at(2, router)
        at(3, scale, 4)
        at(3, scale, 5)
        at(LAG + 2, channels3)
        at(4, experts, 3)
        at(6, place)
        at(2, weights)
        at(3, scale, 6)
        at(3, scale, 7)
        at(4, stats2)
        at(0, stats1)
        at(LAG + 3, gate)
        at(-3, load)
        if s + 2 >= LAG and s + 2 - LAG < NG:
            loadc(s + 2 - LAG)


def phase_d(nc, ctx, p, ins, k, x3d):
    S = lambda name, shape, dt=F32: ctx.enter_context(nc.sbuf_tensor(name, shape, dt))
    N1, N2, BS = 4, 2, 2
    NP_, NCH, EC = B // 2, 8, 8
    w1 = S("d_w1", [128, N1, EC, 512]); w2 = S("d_w2", [128, N2, EC, 4, 128])
    b1r = S("d_b1r", [64, 512]); b2r = S("d_b2r", [128, 128]); base = S("d_base", [128, 2])
    b1t = S("d_b1t", [128, 4, 64])
    v8 = S("d_v8", [128, NP_, 8]); ix = S("d_ix", [128, NP_, 8], U32); nm = S("d_nm", [128, NP_, 1])
    sm = S("d_sm", [128, NP_, 2]); ev = S("d_ev", [128, NP_, 8]); tv = S("d_tv", [128, NP_, 8])
    pf = S("d_pf", [128, NP_, 8]); io = S("d_io", [128, 2, 8 * GI]); cf = S("d_cf", [128, NP_, 8 * GI])
    eqi = S("d_eqi", [128, 8, 8 * GI]); gx = S("d_gx", [128, NP_, GI])
    ixf = S("d_ixf", [128, NP_, 8]); gi = S("d_gi", [128, NP_, 8], I32)
    xg = S("d_xg", [128, NP_, 8, 128]); ln = S("d_ln", [128, 2, 4, 128])
    st = S("d_st", [128, 2, 4, 6]); mv = S("d_mv", [128, 2, 4, 2]); rs = S("d_rs", [128, 2, 8])
    pl = S("d_pl", [128, NP_, 128]); plT = S("d_plT", [128, B, 64])
    hb = S("d_hb", [128, 64, 4, B]); hs = S("d_hs", [128, 64, 4, B])
    oo = S("d_oo", [B, 64, 128]); ov = S("d_ov", [128, NP_, 128])
    bi = S("d_bi", [128, NP_, 8, 128]); ib = S("d_ib", [128, 8, 128])
    A = S("d_A", [128, NP_, 8, 128]); eq = S("d_eq", [128, 8, 128])
    PS = lambda name, shape: ctx.enter_context(nc.psum_tensor(name, shape, F32))
    P0 = PS("d_p0", [128, 512])
    obf = [None, None]
    HB = PS("d_h", [128, 64, 4, B])
    OB = PS("d_o", [128, 2, 512])
    IB = PS("d_i", [128, 2, 512])
    pe, act, dve, pool = p.pe, p.act, p.dve, p.pool
    ident = k["ident"]

    q = p.q["c"]
    tb1 = q.dma(lambda e: e.dma_start(b1r[:, :], ins["w1"][:, 128, :]))
    q.dma(lambda e: e.dma_start(b2r[0:64, :], ins["w2"][:, 512, :]))
    q.dma(lambda e: e.dma_start(b2r[64:128, :], ins["w2"][:, 512, :]))
    q.dma(lambda e: e.dma_start(base[:, :], ins["base"][:, :]))
    q.dma(lambda e: e.dma_start(io[:, :, :], ins["io"][:, :, :]))
    consts = q.all()
    w1t, w2t, w1r, w2r = {}, {}, {}, {}

    def ldw1(c):
        w1t[c] = p.q["w1"].dma(lambda e: e.dma_start(
            w1[:, c % N1], ins["w1"][c * EC:(c + 1) * EC, 0:128, :].rearrange("e d h -> d e h")), w1r.get(c - N1))

    def ldw2(c):
        w2t[c] = p.q["w2"].dma(lambda e: e.dma_start(
            w2[:, c % N2].rearrange("p e c o -> p e (c o)"),
            ins["w2"][c * EC:(c + 1) * EC, 0:512, :].rearrange("e (p c) o -> p e (c o)", c=4)),
            w2r.get(c - N2))

    for c in range(N1):
        ldw1(c)
        if 0 <= c - 1 < N2:
            ldw2(c - 1)
    for c in range(4):
        t = pe.op(lambda e, c=c: e.transpose(P0[:, c * 64:(c + 1) * 64], b1r[:, c:512:4], ident[0:64, 0:64]),
                  tb1, sig=(c == 3))
    tb = act.op(lambda e: e.copy(b1t[:, :, :], P0[:, 0:256].rearrange("p (c e) -> p c e", c=4)), t)
    p0free = tb
    dve.wait(*consts)
    one = None
    tg, tA = {}, {}
    f_, tv_ = {}, {}
    for a in range(NP_):
        m = dve.op(lambda e, a=a: e.max(v8[:, a, :], k["cv"][:, a, :]))
        n = dve.op(lambda e, a=a: e.tensor_scalar(nm[:, a, :], v8[:, a, 0:1], -1.0, None, ALU.mult), m)
        xm = dve.op(lambda e, a=a: e.max_index(ix[:, a, :], v8[:, a, :], k["cv"][:, a, :]), m)
        act.op(lambda e, a=a: e.activation(ev[:, a, :], v8[:, a, :], ACT.Exp, bias=nm[:, a, :]), n)
        xe = act.op(lambda e, a=a: e.activation(gx[:, a, :], k["cv"][:, a, 0:8 * GI:8], ACT.Exp,
                                                bias=nm[:, a, :]))
        f = dve.op(lambda e, a=a: e.tensor_copy(pf[:, a, :], ix[:, a, :]), xm)
        g = dve.op(lambda e, a=a: e.tensor_copy(cf[:, a, :], k["ci"][:, a, :]))
        g = dve.op(lambda e, a=a: e.tensor_tensor(cf[:, a, :], cf[:, a, :], io[:, 1, :], ALU.add), g)
        for kk in range(8):
            h = dve.op(lambda e, a=a, kk=kk: e.scalar_tensor_tensor(
                out=eqi[:, kk, :], in0=io[:, 0, :], scalar=pf[:, a, kk:kk + 1], in1=cf[:, a, :],
                op0=ALU.is_equal, op1=ALU.mult), f, g)
        f = dve.op(lambda e, a=a: e.tensor_reduce(ixf[:, a, :], eqi[:, :, :], AX.X, ALU.add), h)
        f = dve.op(lambda e, a=a: e.tensor_scalar(ixf[:, a, :], ixf[:, a, :], base[:, a:a + 1], None,
                                                  ALU.add), f)
        g = dve.op(lambda e, a=a: e.tensor_copy(gi[:, a, :], ixf[:, a, :]), f)
        r = dve.op(lambda e, a=a: e.tensor_tensor(gx[:, a, :], gx[:, a, :], k["cs"][:, a, :], ALU.mult), xe)
        r = dve.op(lambda e, a=a: e.tensor_reduce(sm[:, a, 0:1], gx[:, a, :], AX.X, ALU.add), r)
        r = dve.op(lambda e, a=a: e.reciprocal(sm[:, a, 1:2], sm[:, a, 0:1]), r)
        tv_[a] = dve.op(lambda e, a=a: e.tensor_scalar(tv[:, a, :], ev[:, a, :], sm[:, a, 1:2], None,
                                                       ALU.mult), r)
        f_[a] = f
        tx = []
        for kk in range(8):
            tx.append(p.q["g"].dma(lambda e, a=a, kk=kk: e.indirect_dma_start(
                out=xg[:, a, kk, :], out_offset=None, in_=x3d[:, :],
                in_offset=bass.IndirectOffsetOnAxis(ap=gi[:, a, kk:kk + 1], axis=0)), g))
        tg[a] = tx
    prev = None
    for a in range(NP_):
        tx, tvt = tg[a], tv_[a]
        for half in range(2):
            last = layernorm_tokens(p, xg[:, a, 4 * half:4 * half + 4, :], st[:, half], mv[:, half],
                                    rs[:, half], ln[:, half], 1e-5, tx[4 * half + 3], k["mhalf"],
                                    (prev,), (prev,))[0]
            if half == 0:
                dve.wait(*tx)
            for j in range(4):
                kk = 4 * half + j
                if kk == 0:
                    prev = dve.op(lambda e, a=a: e.tensor_scalar(pl[:, a, :], ln[:, 0, 0, :], tv[:, a, 0:1],
                                                                 None, ALU.mult), last, tvt)
                else:
                    prev = dve.op(lambda e, a=a, kk=kk: e.scalar_tensor_tensor(
                        out=pl[:, a, :], in0=ln[:, kk // 4, kk % 4, :], scalar=tv[:, a, kk:kk + 1],
                        in1=pl[:, a, :], op0=ALU.mult, op1=ALU.add), last, prev)
        t = pe.op(lambda e, a=a: e.transpose(P0[:, 0:128], pl[:, a, :], ident[:, :]), prev, p0free)
        plt = act.op(lambda e, a=a: e.copy(plT[:, 2 * a:2 * a + 2, :].rearrange("p b e -> p (b e)"),
                                           P0[:, 0:128]), t)
        p0free = plt
    for a in range(NP_):
        f, tvt = f_[a], tv_[a]
        for kk in range(8):
            bt = pool.op(lambda e, a=a, kk=kk: e.tensor_scalar(bi[:, a, kk, :], k["ones"][:, :],
                                                               ixf[:, a, kk:kk + 1], None, ALU.mult), f)
            t = pe.op(lambda e, a=a, kk=kk: e.matmul(IB[:, kk // 4, (kk % 4) * 128:(kk % 4 + 1) * 128],
                                                     bi[:, a, kk, :], ident[:, :], start=True, stop=True),
                      bt, tA.get("ib"), sig=(kk == 7))
        tA["ib"] = act.op(lambda e: e.copy(ib[:, :, :].rearrange("p (a k) c -> p a (k c)", a=2), IB[:, :, :]),
                          t, tA.get("last"))
        prevA, pe_ = None, None
        for kk in range(8):
            dst = A[:, a] if kk == 0 else eq
            pe_ = dve.op(lambda e, a=a, kk=kk, dst=dst: e.tensor_scalar(
                dst[:, :, :], ib[:, :, :], ixf[:, a, kk:kk + 1], tv[:, a, kk:kk + 1], ALU.is_equal, ALU.mult),
                tA["ib"], tvt, prevA)
            if kk:
                prevA = dve.op(lambda e, a=a: e.tensor_tensor(A[:, a], A[:, a], eq[:, :, :], ALU.add), pe_)
            else:
                prevA = pe_
        tA["last"] = prevA
        tA[a] = prevA
    for c in range(NCH):
        for ee in range(EC):
            x = c * EC + ee
            for ch in range(4):
                t = pe.op(lambda e, x=x, ee=ee, ch=ch, c=c: e.matmul(
                    HB[:, x, ch, :], w1[:, c % N1, ee, ch:512:4], plT[:, :, x], start=True, stop=True),
                    w1t[c], plt, sig=(ee == EC - 1 and ch == 3))
        w1r[c] = t
        if c + N1 < NCH:
            ldw1(c + N1)
        if c % BS == BS - 1:
            e0, e1 = (c + 1 - BS) * EC, (c + 1) * EC
            for b in range(B):
                h = dve.op(lambda e, e0=e0, e1=e1, b=b: e.tensor_tensor(
                    hb[:, e0:e1, :, b], HB[:, e0:e1, :, b],
                    b1t[:, :, e0:e1].rearrange("p c e -> p e c"), ALU.add), t, tb)
            hg = act.op(lambda e, e0=e0, e1=e1: e.activation(hs[:, e0:e1].rearrange("p e c b -> p (e c b)"),
                                                             hb[:, e0:e1].rearrange("p e c b -> p (e c b)"),
                                                             ACT.Gelu), h)
            for cc in range(c + 1 - BS, c + 1):
                for ee in range(EC):
                    x = cc * EC + ee
                    j = x // 4 % 2
                    for ch in range(4):
                        t2 = pe.op(lambda e, x=x, j=j, ee=ee, ch=ch, cc=cc: e.matmul(
                            OB[0:B, j, (x % 4) * 128:(x % 4 + 1) * 128], hs[:, x, ch, :],
                            w2[:, cc % N2, ee, ch, :], start=(ch == 0), stop=(ch == 3)),
                            w2t[cc], hg, obf[j], sig=(x % 4 == 3 and ch == 3))
                    if x % 4 == 3:
                        obf[j] = act.op(lambda e, x=x, j=j: e.copy(
                            oo[:, x - 3:x + 1, :].rearrange("b e o -> b (e o)"), OB[0:B, j, :]), t2)
                w2r[cc] = t2
                if cc + N2 < NCH:
                    ldw2(cc + N2)
    ot = {b: p.q["c"].dma(lambda e, b=b: e.dma_start(ov[64 * (b % 2):64 * (b % 2) + 64, b // 2, :],
                                                     oo[b:b + 1, :, :]), obf[1]) for b in range(B)}
    for a in range(NP_):
        o = dve.op(lambda e, a=a: e.tensor_tensor(ov[:, a, :], ov[:, a, :], b2r[:, :], ALU.add),
                   ot[2 * a], ot[2 * a + 1])
        for kk in range(8):
            D = IB[:, kk // 4, (kk % 4) * 128:(kk % 4 + 1) * 128]
            t = pe.op(lambda e, a=a, kk=kk, D=D: e.matmul(D, A[:, a, kk, :], ov[:, a, :], start=True,
                                                          stop=True), o, tA[a], tA.get("fin"), tA["ib"],
                      sig=(kk == 7))
        u = dve.op(lambda e, a=a: e.tensor_tensor(
            xg[:, a].rearrange("p (h k) c -> p h (k c)", h=2), IB[:, :, :],
            xg[:, a].rearrange("p (h k) c -> p h (k c)", h=2), ALU.add), t, *tg[a])
        tA["fin"] = u
        sc = None
        for kk in range(8):
            sc = p.q["sc"].dma(lambda e, a=a, kk=kk: e.indirect_dma_start(
                out=x3d[:, :], out_offset=bass.IndirectOffsetOnAxis(ap=gi[:, a, kk:kk + 1], axis=0),
                in_=xg[:, a, kk, :], in_offset=None), u, sc)


def phase_e(nc, ctx, p, k, x3d, out):
    S = lambda name, shape, dt=F32: ctx.enter_context(nc.sbuf_tensor(name, shape, dt))
    NB_ = 6
    xt = S("e_x", [128, NB_, 4, 128]); xo = S("e_o", [128, NB_, 512])
    PB = [ctx.enter_context(nc.psum_tensor(f"e_p{i}", [128, 512], F32)) for i in range(4)]
    ld, tr, ev, so = {}, {}, {}, {}

    def load(G):
        src = x3d[G * 512:G * 512 + 512, :].rearrange("(r w) c -> w r c", w=128)
        ld[G] = p.q["ld"].dma(lambda e: e.dma_start(xt[:, G % NB_], src), tr.get(G - NB_))

    for G in range(NB_ - 1):
        load(G)
    for G in range(NG):
        b, h = divmod(G, GI)
        D = PB[G % 4]
        for r in range(4):
            t = p.pe.op(lambda e, r=r, D=D, G=G: e.transpose(D[:, r * 128:(r + 1) * 128], xt[:, G % NB_, r, :],
                                                             k["ident"][:, :]), ld[G], ev.get(G - 4),
                        sig=(r == 3))
        tr[G] = t
        eng = p.act if G % 2 else p.dve
        f = (lambda e, D=D, G=G: e.copy(xo[:, G % NB_, :], D[:, :])) if G % 2 else (
            lambda e, D=D, G=G: e.tensor_copy(xo[:, G % NB_, :], D[:, :]))
        ev[G] = eng.op(f, t, so.get(G - NB_))
        so[G] = p.q["st"].dma(lambda e, b=b, h=h, G=G: e.dma_start(
            out[b * 128:(b + 1) * 128, h * 512:h * 512 + 512], xo[:, G % NB_, :]), ev[G])
        if G + NB_ - 1 < NG:
            load(G + NB_ - 1)


def program(nc, ins, out, dbg):
    with ExitStack() as ctx:
        S = lambda name, shape, dt=F32: ctx.enter_context(nc.sbuf_tensor(name, shape, dt))
        D = lambda name, shape: dbg(name, shape)
        k = {
            "zero": S("zero", [128, 640]), "mhalf": S("mhalf", [128, 8]), "ones": S("ones", [128, 128]),
            "ident": S("ident", [128, 128]), "fm": S("fm", [96, 2 * NG]),
            "cv": S("cv", [128, (B + 1) // 2, 8 * GI]), "ci": S("ci", [128, (B + 1) // 2, 8 * GI], U32),
            "cs": S("cs", [128, (B + 1) // 2, GI]),
            "gm": S("gm", [1, 1]), "flag": S("flag", [1, 1], I32),
        }
        xtp = D("xtp", [B * PIX, 128])
        offd = D("offd", [18, B * H * W])
        x1d = D("x1d", [B * 128, H * W])
        x2d = D("x2d", [B * H * W, 128])
        x3d = D("x3d", [B * H * W, 128])
        with ExitStack() as ca:
            SA = lambda name, shape, dt=F32: ca.enter_context(nc.sbuf_tensor(name, shape, dt))
            k |= {"wof": SA("wof", [128, 3, 96]), "selz": SA("selz", [96, 96]), "wcv": SA("wcv", [128, 9, 128]),
                  "sel": SA("sel", [128, 18, 120], BF16), "P": SA("P", [128, NPR * 512], BF16)}
            with ExitStack() as c0:
                k["self"] = c0.enter_context(nc.sbuf_tensor("self", [128, 18, 120], F32))
                k["cst"] = c0.enter_context(nc.sbuf_tensor("cst", [128, 512], F32))
                p0 = Phase(nc, c0, "s", {"c": ("sp", 12)})
                setup_phase(nc, c0, p0, ins, k, xtp)
                p0.emit(nc)
            with ExitStack() as c1:
                p1 = Phase(nc, c1, "a", {"ld": ("sp", 4), "w": ("sp", 20), "st": ("sp", 8)})
                phase_a(nc, c1, p1, ins, k, xtp, offd, x1d)
                p1.emit(nc)
            with ExitStack() as c1:
                pf = Phase(nc, c1, "g", {})
                far_flag(nc, c1, pf, k)
                pf.emit(nc)
            far = nc.values_load(k["flag"][0:1, 0:1], min_val=0, max_val=1)
            with nc.If(far > 0):
                far_rows(nc, ins, k, xtp, offd, x1d)
        with ExitStack() as c2:
            p2 = Phase(nc, c2, "b", {"c": ("sp", 10), "ld": ("sp", 3), "lc": ("sp", 3), "st": ("sp", 6)})
            phase_bc(nc, c2, p2, ins, k, x1d, x2d, x3d)
            p2.emit(nc)
        with ExitStack() as c3:
            p3 = Phase(nc, c3, "d", {"c": ("sp", 5), "w1": ("sp", 5), "w2": ("sp", 3),
                                     "g": ("pool", 8), "sc": ("pool", 2)})
            phase_d(nc, c3, p3, ins, k, x3d)
            p3.emit(nc)
        with ExitStack() as c4:
            p4 = Phase(nc, c4, "e", {"ld": ("sp", 6), "st": ("act", 6)})
            phase_e(nc, c4, p4, k, x3d, out)
            p4.emit(nc)


def constants():
    ident = np.eye(128, dtype=np.float32)
    sel = np.zeros((128, 18, 120), np.float32)
    m = np.arange(120)
    j, i = m // 24, m % 24
    for t in range(9):
        for part in (0, 32, 64):
            sel[part + 2 * t, t, :] = 1.0
            sel[part + 2 * t + 1, 9 + t, :] = 1.0
        sel[96, t, :] = 2 - j
        sel[96, 9 + t, :] = t % 3 + 2 - i
        sel[97, 9 + t, :] = 1.0
    cst = np.ones((2, 512), np.float32)
    cst[1] = np.arange(512) % 16
    base = (np.arange(128)[:, None] // 64 + 2 * np.arange(2)[None, :]).astype(np.float32) * (H * W)
    far = np.zeros((128, 9, 2), np.float32)
    io = np.zeros((128, 2, 8 * GI), np.float32)
    io[:, 0, :] = np.arange(8 * GI)
    io[:, 1, :] = 512 * (np.arange(8 * GI) // 8)
    far[:, :, 0] = np.arange(9)[None, :] // 3 - 1
    far[:, :, 1] = np.arange(9)[None, :] % 3 - 1 + np.arange(128)[:, None]
    sele = np.zeros((24, 8, 128), np.float32)
    for i in range(24):
        sele[i, i % 8, :] = 1.0
    selz = np.tile(np.eye(32, dtype=np.float32), (3, 3))
    return {"io": io, "selz": selz, "sele": sele, "ident": ident, "sel": sel, "cst": cst, "base": base, "far": far}


OUTN = ["out"]
DBG = ["xtp", "offd", "x1d", "x2d", "x3d"]


def kernel(**inputs):
    import concourse.bacc as _bacc
    from concourse.bass_utils import run_bass_kernel_spmd as _run

    a = {n: np.ascontiguousarray(v) for n, v in inputs.items()}
    arr = {"x": a["x"].reshape(B * 128, H * W)}
    wo = np.zeros((128, 3, 3, 32), np.float32)
    wo[:, :, :, 0:18] = a["L0_conv_w_off"].transpose(1, 3, 2, 0)
    wo = wo.reshape(128, 3, 96)
    arr["wof"] = wo
    arr["wcv"] = np.ascontiguousarray(a["L0_conv_w_conv"].reshape(128, 128, 9).transpose(1, 2, 0))
    arr["rw"] = a["L0_ffn_router_w"]
    arr["rb"] = np.ascontiguousarray(np.broadcast_to(a["L0_ffn_router_b"][None, :], (128, 8)))
    arr["ew"] = np.ascontiguousarray(a["L0_ffn_expert_w"].transpose(1, 0, 2))
    arr["eb"] = np.zeros((3, 32, 128), np.float32)
    arr["eb"][:, 0:24] = np.tile(a["L0_ffn_expert_b"], (3, 1))
    arr["eb"] = arr["eb"].reshape(96, 128)
    arr["al"] = np.ascontiguousarray(a["L1_conv_alphas"].T)
    arr["gw"] = np.zeros((128, 2, 128), np.float32)
    for i in range(2):
        arr["gw"][:, i, 64 * i:64 * i + 64] = a["L1_ffn_gate_w"].T
    arr["gb"] = np.tile(a["L1_ffn_gate_b"], 2).reshape(128, 1)
    arr["w1"] = a["L1_ffn_weight1"]
    arr["w2"] = a["L1_ffn_weight2"]
    arr |= constants()
    nc = _bacc.Bacc("TRN2", target_bir_lowering=False, num_devices=1)
    ins, arrays = {}, {}
    for n, v in arr.items():
        arrays["in_" + n] = v
        ins[n] = nc.dram_tensor("in_" + n, v.shape, mybir.dt.from_np(v.dtype), kind="ExternalInput").ap()
    out = nc.dram_tensor("out", (B * 128, H * W), F32, kind="ExternalOutput").ap()

    def dbg(name, shape):
        return nc.dram_tensor(name, shape, F32, kind="Internal").ap()

    program(nc, ins, out, dbg)
    r = _run(nc, [arrays], core_ids=[0])
    return r.results[0]["out"].reshape(B, 128, H, W)
```
